# Optimizing a Trainium2 kernel written in Bass

```python
import numpy as np
import jax
import jax.numpy as jnp

def _softmax(x, axis=-1):
    return jax.nn.softmax(x, axis=axis)

def _gelu(x):
    return jax.nn.gelu(x, approximate=True)

def _silu(x):
    return jax.nn.silu(x)

def _sigmoid(x):
    return jax.nn.sigmoid(x)

def _layernorm(x, axis=-1, eps=1e-05):
    m = jnp.mean(x, axis=axis, keepdims=True)
    v = jnp.var(x, axis=axis, keepdims=True)
    return (x - m) / jnp.sqrt(v + eps)

def _scatter_add(tgt, idx, src, axis=0):
    return tgt.at[idx].add(src)

def _segment_sum(src, seg, n):
    return jax.ops.segment_sum(src, seg, n)
kernel_name = 'mk_gnn_resnorm_d4_gnn_r64_697858'

def setup_inputs(seed: int=0):
    np.random.seed(seed)
    _w = jnp.asarray

    def _rec_inputs():
        import jax
        import jax.numpy as jnp
        _gk = jax.random.key(seed)
        x = -0.0003713 + 1 * jax.random.normal(jax.random.fold_in(_gk, 1), (50000, 128), jnp.float32)
        src = jax.random.randint(jax.random.fold_in(_gk, 2), (25000,), 0, 50000, jnp.int32)
        dst = jax.random.randint(jax.random.fold_in(_gk, 3), (25000,), 0, 50000, jnp.int32)
        _o = jnp.argsort(dst, stable=True)
        src = src[_o]
        dst = dst[_o]
        edge_attr_16 = -0.00010739 + 0.99994 * jax.random.normal(jax.random.fold_in(_gk, 12), (25000, 16), jnp.float32)
        edge_type_3 = jax.random.randint(jax.random.fold_in(_gk, 14), (25000,), 0, 3, jnp.int32)
        return (x, src, dst, edge_attr_16, edge_type_3)
    x, src, dst, edge_attr_16, edge_type_3 = _rec_inputs()

    def _L0_gnn_setup():
        import jax, jax.numpy as jnp
        import numpy as np
        N_NODES = 100000
        N_EDGES = 25000
        IN_DIM = 128
        HID = 128

        def _sage_conv(h, src, dst, Wl, bl, Wr, n_nodes):
            msg = h[src]
            agg = jax.ops.segment_sum(msg, dst, num_segments=n_nodes)
            deg = jax.ops.segment_sum(jnp.ones((src.shape[0],), h.dtype), dst, num_segments=n_nodes)
            agg = agg / jnp.maximum(deg, 1.0)[:, None]
            return agg @ Wl + bl + h @ Wr
        key = jax.random.key(seed)
        ks = jax.random.split(key, 8)
        x = jax.random.normal(ks[0], (N_NODES, IN_DIM), dtype=jnp.float32)
        edge_index = jax.random.randint(ks[1], (2, N_EDGES), 0, N_NODES, dtype=jnp.int32)
        s = 1.0 / np.sqrt(IN_DIM)
        Wl1 = jax.random.uniform(ks[2], (IN_DIM, HID), jnp.float32, -s, s)
        bl1 = jnp.zeros((HID,), jnp.float32)
        Wr1 = jax.random.uniform(ks[3], (IN_DIM, HID), jnp.float32, -s, s)
        s2 = 1.0 / np.sqrt(HID)
        Wl2 = jax.random.uniform(ks[4], (HID, HID), jnp.float32, -s2, s2)
        bl2 = jnp.zeros((HID,), jnp.float32)
        Wr2 = jax.random.uniform(ks[5], (HID, HID), jnp.float32, -s2, s2)
        return {'x': x, 'edge_index': edge_index, 'Wl1': Wl1, 'bl1': bl1, 'Wr1': Wr1, 'Wl2': Wl2, 'bl2': bl2, 'Wr2': Wr2}
    _L0_gnn_all = _L0_gnn_setup()
    _L0_gnn_in = {k: v for k, v in _L0_gnn_all.items() if k in ('Wl1', 'bl1', 'Wr1', 'Wl2', 'bl2', 'Wr2')}
    del _L0_gnn_all

    def _L1_gnn_setup():
        import jax, jax.numpy as jnp
        import numpy as np
        N_NODES = 50000
        N_EDGES = 25000
        IN_DIM = 128
        HEADS = 4
        HEAD_DIM = 32
        N_REL = 3
        NEG_SLOPE = 0.2
        key = jax.random.key(seed)
        ks = jax.random.split(key, 8)
        x = jax.random.normal(ks[0], (N_NODES, IN_DIM), dtype=jnp.float32)
        edge_index = jax.random.randint(ks[1], (2, N_EDGES), 0, N_NODES, dtype=jnp.int64)
        edge_type = jax.random.randint(ks[2], (N_EDGES,), 0, N_REL, dtype=jnp.int64)
        s = 1.0 / np.sqrt(IN_DIM)
        W = jax.random.normal(ks[3], (N_REL, IN_DIM, HEADS * HEAD_DIM), dtype=jnp.float32) * s
        att_src = jax.random.normal(ks[4], (N_REL, HEADS, HEAD_DIM), dtype=jnp.float32) * s
        att_dst = jax.random.normal(ks[5], (N_REL, HEADS, HEAD_DIM), dtype=jnp.float32) * s
        bias = jnp.zeros((N_REL, HEADS * HEAD_DIM), dtype=jnp.float32)
        rel_w = jnp.ones((N_REL,), dtype=jnp.float32)
        return {'x': x, 'W': W, 'att_src': att_src, 'att_dst': att_dst, 'bias': bias, 'rel_w': rel_w, 'edge_index': edge_index, 'edge_type': edge_type}
    _L1_gnn_all = _L1_gnn_setup()
    _L1_gnn_in = {k: v for k, v in _L1_gnn_all.items() if k in ('W', 'att_src', 'att_dst', 'bias', 'rel_w')}
    del _L1_gnn_all

    def _L2_gnn_setup():
        import jax, jax.numpy as jnp
        import numpy as np
        N_NODES = 100000
        N_EDGES = 9375
        D_IN = 128
        D_OUT = 128
        key = jax.random.key(seed)
        k1, k2, k3, k4, k5 = jax.random.split(key, 5)
        feat = jax.random.normal(k1, (N_NODES, D_IN), dtype=jnp.float32)
        weight = jax.random.normal(k2, (D_IN, D_OUT), dtype=jnp.float32) * (1.0 / np.sqrt(D_IN))
        bias = jax.random.normal(k3, (D_OUT,), dtype=jnp.float32) * 0.01
        src = jax.random.randint(k4, (N_EDGES,), 0, N_NODES, dtype=jnp.int32)
        dst = jax.random.randint(k5, (N_EDGES,), 0, N_NODES, dtype=jnp.int32)
        return {'feat': feat, 'weight': weight, 'bias': bias, 'src': src, 'dst': dst}
    _L2_gnn_all = _L2_gnn_setup()
    _L2_gnn_in = {k: v for k, v in _L2_gnn_all.items() if k in ('weight', 'bias')}
    del _L2_gnn_all

    def _L3_gnn_setup():
        import jax, jax.numpy as jnp
        import numpy as np
        BN_EPS = 0.001
        D = 128
        EDGE_DIM = 16
        N_NODES = 50000
        N_EDGES = 12500

        def _bn(x, gamma, beta, mean, var):
            return (x - mean) * jax.lax.rsqrt(var + BN_EPS) * gamma + beta
        key = jax.random.key(seed)
        ks = jax.random.split(key, 12)
        inp = {'node_feat': jax.random.normal(ks[0], (N_NODES, D), jnp.float32), 'edge_feat': jax.random.normal(ks[1], (N_EDGES, EDGE_DIM), jnp.float32), 'src': jax.random.randint(ks[2], (N_EDGES,), 0, N_NODES, jnp.int32), 'dst': jax.random.randint(ks[3], (N_EDGES,), 0, N_NODES, jnp.int32), 'We1': jax.random.normal(ks[4], (EDGE_DIM, 2 * D), jnp.float32) * 0.05, 'be1': jnp.zeros((2 * D,), jnp.float32), 'We2': jax.random.normal(ks[5], (2 * D, D), jnp.float32) * 0.05, 'be2': jnp.zeros((D,), jnp.float32), 'eps': jax.random.normal(ks[6], (1,), jnp.float32) * 0.05, 'Wm1': jax.random.normal(ks[7], (D, 2 * D), jnp.float32) * 0.05, 'bm1': jnp.zeros((2 * D,), jnp.float32), 'g1': jnp.ones((2 * D,), jnp.float32), 'b1': jnp.zeros((2 * D,), jnp.float32), 'm1': jnp.zeros((2 * D,), jnp.float32), 'v1': jnp.ones((2 * D,), jnp.float32), 'Wm2': jax.random.normal(ks[8], (2 * D, D), jnp.float32) * 0.05, 'bm2': jnp.zeros((D,), jnp.float32), 'g2': jnp.ones((D,), jnp.float32), 'b2': jnp.zeros((D,), jnp.float32), 'm2': jnp.zeros((D,), jnp.float32), 'v2': jnp.ones((D,), jnp.float32)}
        return inp
    _L3_gnn_all = _L3_gnn_setup()
    _L3_gnn_in = {k: v for k, v in _L3_gnn_all.items() if k in ('We1', 'be1', 'We2', 'be2', 'eps', 'Wm1', 'bm1', 'g1', 'b1', 'm1', 'v1', 'Wm2', 'bm2', 'g2', 'b2', 'm2', 'v2')}
    del _L3_gnn_all
    return {'x': x, 'src': src, 'dst': dst, 'edge_attr_16': edge_attr_16, 'edge_type_3': edge_type_3, 'L0_gnn_Wl1': _L0_gnn_in['Wl1'], 'L0_gnn_bl1': _L0_gnn_in['bl1'], 'L0_gnn_Wr1': _L0_gnn_in['Wr1'], 'L0_gnn_Wl2': _L0_gnn_in['Wl2'], 'L0_gnn_bl2': _L0_gnn_in['bl2'], 'L0_gnn_Wr2': _L0_gnn_in['Wr2'], 'L1_gnn_W': _L1_gnn_in['W'], 'L1_gnn_att_src': _L1_gnn_in['att_src'], 'L1_gnn_att_dst': _L1_gnn_in['att_dst'], 'L1_gnn_bias': _L1_gnn_in['bias'], 'L1_gnn_rel_w': _L1_gnn_in['rel_w'], 'L2_gnn_weight': _L2_gnn_in['weight'], 'L2_gnn_bias': _L2_gnn_in['bias'], 'L3_gnn_We1': _L3_gnn_in['We1'], 'L3_gnn_be1': _L3_gnn_in['be1'], 'L3_gnn_We2': _L3_gnn_in['We2'], 'L3_gnn_be2': _L3_gnn_in['be2'], 'L3_gnn_eps': _L3_gnn_in['eps'], 'L3_gnn_Wm1': _L3_gnn_in['Wm1'], 'L3_gnn_bm1': _L3_gnn_in['bm1'], 'L3_gnn_g1': _L3_gnn_in['g1'], 'L3_gnn_b1': _L3_gnn_in['b1'], 'L3_gnn_m1': _L3_gnn_in['m1'], 'L3_gnn_v1': _L3_gnn_in['v1'], 'L3_gnn_Wm2': _L3_gnn_in['Wm2'], 'L3_gnn_bm2': _L3_gnn_in['bm2'], 'L3_gnn_g2': _L3_gnn_in['g2'], 'L3_gnn_b2': _L3_gnn_in['b2'], 'L3_gnn_m2': _L3_gnn_in['m2'], 'L3_gnn_v2': _L3_gnn_in['v2']}

def reference(x, src, dst, edge_attr_16, edge_type_3, L0_gnn_Wl1, L0_gnn_bl1, L0_gnn_Wr1, L0_gnn_Wl2, L0_gnn_bl2, L0_gnn_Wr2, L1_gnn_W, L1_gnn_att_src, L1_gnn_att_dst, L1_gnn_bias, L1_gnn_rel_w, L2_gnn_weight, L2_gnn_bias, L3_gnn_We1, L3_gnn_be1, L3_gnn_We2, L3_gnn_be2, L3_gnn_eps, L3_gnn_Wm1, L3_gnn_bm1, L3_gnn_g1, L3_gnn_b1, L3_gnn_m1, L3_gnn_v1, L3_gnn_Wm2, L3_gnn_bm2, L3_gnn_g2, L3_gnn_b2, L3_gnn_m2, L3_gnn_v2):
    import jax
    import jax.numpy as jnp

    def _L0_gnn_ref(x, edge_index, Wl1, bl1, Wr1, Wl2, bl2, Wr2):
        import jax, jax.numpy as jnp
        import numpy as np
        N_NODES = 100000
        N_EDGES = 25000
        IN_DIM = 128
        HID = 128

        def _sage_conv(h, src, dst, Wl, bl, Wr, n_nodes):
            msg = h[src]
            agg = jax.ops.segment_sum(msg, dst, num_segments=n_nodes)
            deg = jax.ops.segment_sum(jnp.ones((src.shape[0],), h.dtype), dst, num_segments=n_nodes)
            agg = agg / jnp.maximum(deg, 1.0)[:, None]
            return agg @ Wl + bl + h @ Wr
        src, dst = (edge_index[0], edge_index[1])
        n = x.shape[0]
        h = jax.nn.relu(_sage_conv(x, src, dst, Wl1, bl1, Wr1, n))
        h = jax.nn.relu(_sage_conv(h, src, dst, Wl2, bl2, Wr2, n))
        return h

    def _L1_gnn_ref(x, W, att_src, att_dst, bias, rel_w, edge_index, edge_type):
        import jax, jax.numpy as jnp
        import numpy as np
        N_NODES = 50000
        N_EDGES = 25000
        IN_DIM = 128
        HEADS = 4
        HEAD_DIM = 32
        N_REL = 3
        NEG_SLOPE = 0.2
        N = x.shape[0]
        NEG = jnp.float32(-1000000000.0)
        self_idx = jnp.arange(N, dtype=edge_index.dtype)
        src = jnp.concatenate([edge_index[0], self_idx])
        dst = jnp.concatenate([edge_index[1], self_idx])
        weights = jax.nn.softmax(rel_w)
        out = jnp.zeros((N, HEADS * HEAD_DIM), dtype=x.dtype)
        for r in range(N_REL):
            h = (x @ W[r]).reshape(N, HEADS, HEAD_DIM)
            a_s = jnp.einsum('nhc,hc->nh', h, att_src[r])
            a_d = jnp.einsum('nhc,hc->nh', h, att_dst[r])
            score = jax.nn.leaky_relu(a_s[src] + a_d[dst], NEG_SLOPE)
            mask = jnp.concatenate([edge_type == r, jnp.ones((N,), dtype=bool)])
            score = jnp.where(mask[:, None], score, NEG)
            smax = jax.ops.segment_max(score, dst, num_segments=N)
            ex = jnp.exp(score - smax[dst])
            denom = jax.ops.segment_sum(ex, dst, num_segments=N)
            alpha = ex / denom[dst]
            msg = alpha[:, :, None] * h[src]
            rel_out = jax.ops.segment_sum(msg, dst, num_segments=N).reshape(N, HEADS * HEAD_DIM)
            out = out + weights[r] * (rel_out + bias[r])
        return out

    def _L2_gnn_ref(feat, weight, bias, src, dst):
        import jax, jax.numpy as jnp
        import numpy as np
        N_NODES = 100000
        N_EDGES = 9375
        D_IN = 128
        D_OUT = 128
        n = feat.shape[0]
        deg = jax.ops.segment_sum(jnp.ones_like(dst, dtype=feat.dtype), dst, num_segments=n)
        norm = jnp.clip(deg, 1.0) ** (-0.5)
        x = feat * norm[:, None]
        agg = jax.ops.segment_sum(x[src], dst, num_segments=n)
        h = agg * norm[:, None]
        return h @ weight + bias

    def _L3_gnn_ref(node_feat, edge_feat, src, dst, We1, be1, We2, be2, eps, Wm1, bm1, g1, b1, m1, v1, Wm2, bm2, g2, b2, m2, v2):
        import jax, jax.numpy as jnp
        import numpy as np
        BN_EPS = 0.001
        D = 128
        EDGE_DIM = 16
        N_NODES = 50000
        N_EDGES = 12500

        def _bn(x, gamma, beta, mean, var):
            return (x - mean) * jax.lax.rsqrt(var + BN_EPS) * gamma + beta
        e = (edge_feat @ We1 + be1) @ We2 + be2
        msg = jax.nn.relu(e + node_feat[src])
        pooled = jax.ops.segment_sum(msg, dst, num_segments=node_feat.shape[0])
        h = (1.0 + eps) * node_feat + pooled
        h = jax.nn.relu(_bn(h @ Wm1 + bm1, g1, b1, m1, v1)) @ Wm2 + bm2
        return _bn(h, g2, b2, m2, v2)
    edge_index = jnp.stack([src, dst])
    x = _layernorm(x + _L0_gnn_ref(x, edge_index, L0_gnn_Wl1, L0_gnn_bl1, L0_gnn_Wr1, L0_gnn_Wl2, L0_gnn_bl2, L0_gnn_Wr2), axis=-1)
    x = _layernorm(x + _L1_gnn_ref(x, L1_gnn_W, L1_gnn_att_src, L1_gnn_att_dst, L1_gnn_bias, L1_gnn_rel_w, edge_index, edge_type_3), axis=-1)
    x = _layernorm(x + _L2_gnn_ref(x, L2_gnn_weight, L2_gnn_bias, src, dst), axis=-1)
    x = _layernorm(x + _L3_gnn_ref(x, edge_attr_16, src, dst, L3_gnn_We1, L3_gnn_be1, L3_gnn_We2, L3_gnn_be2, L3_gnn_eps, L3_gnn_Wm1, L3_gnn_bm1, L3_gnn_g1, L3_gnn_b1, L3_gnn_m1, L3_gnn_v1, L3_gnn_Wm2, L3_gnn_bm2, L3_gnn_g2, L3_gnn_b2, L3_gnn_m2, L3_gnn_v2), axis=-1)
    return x

_drawn_inputs = setup_inputs


def setup_inputs(seed=0):
    import zlib

    import numpy as np

    out = dict(_drawn_inputs(seed))
    spreads = {'L0_gnn_bl1': (0.0, 0.276),
     'L0_gnn_bl2': (0.0, 0.1),
     'L1_gnn_bias': (0.0, 0.1),
     'L1_gnn_rel_w': (1.0, 0.2),
     'L3_gnn_be1': (0.0, 0.56),
     'L3_gnn_be2': (0.0, 0.502),
     'L3_gnn_bm1': (0.0, 0.1),
     'L3_gnn_g1': (1.0, 0.2),
     'L3_gnn_b1': (0.0, 0.1),
     'L3_gnn_m1': (0.0, 0.1),
     'L3_gnn_v1': (1.0, 0.2),
     'L3_gnn_bm2': (0.0, 0.1),
     'L3_gnn_g2': (1.0, 0.2),
     'L3_gnn_b2': (0.0, 0.1),
     'L3_gnn_m2': (0.0, 0.1),
     'L3_gnn_v2': (1.0, 0.2)}
    factors = {'L1_gnn_att_dst': 5.985, 'L2_gnn_bias': 6.433}
    for name, (base, spread) in spreads.items():
        noise = np.random.default_rng([zlib.crc32(name.encode()), seed]).standard_normal(out[name].shape)
        drawn = base * np.exp(spread * noise) if base else spread * noise
        out[name] = jnp.asarray(drawn.astype(out[name].dtype))
    for name, factor in factors.items():
        out[name] = (out[name] * factor).astype(out[name].dtype)
    return out
```

```python
from contextlib import ExitStack

import concourse.bass as bass
from concourse import mybir

F32 = mybir.dt.float32
I32 = mybir.dt.int32
BF16 = mybir.dt.bfloat16
ALU = mybir.AluOpType
ACT = mybir.ActivationFunctionType
AX_X = mybir.AxisListType.X

D = 128
T = 128
G = 4
W = G * T
CHUNKS = 7
R, H = 3, 4
RH = R * H
HD = D // H
Q = CHUNKS * RH
FAR = float(1 << 20)
MASKED = 1.0e9
LN_EPS = 1e-5
BN_EPS = 1e-3


def steps(eng, groups, lag, body):
    def fixed(s):
        def at(k):
            g = s - k
            return (g, g // 2, g % 2) if 0 <= g < groups else None
        return at

    first = lag + 2 + (lag % 2)
    pairs = (groups - 1 - first) // 2
    if pairs < 2:
        for s in range(groups + lag):
            body(fixed(s))
        return
    for s in range(first):
        body(fixed(s))
    with eng.Fori(0, pairs) as i:
        for u in range(2):
            def at(k, u=u):
                c = first + u - k
                return i * 2 + c, i + c // 2, c % 2
            body(at)
    for s in range(first + 2 * pairs, groups + lag):
        body(fixed(s))


def rounds(at, *table):
    for line in table:
        for lag, stage in line:
            g = at(lag)
            if g is not None:
                stage(*g)


class Kit:

    def __init__(self, nc, ctx):
        self.nc, self.ctx = nc, ctx
        self.passing = []
        self.held = {n: ctx.enter_context(nc.semaphore(f"held_{n}")) for n in ("pe", "act", "dve", "pool", "sp")}

    def sb(self, name, shape, dt=F32, ctx=None):
        return (ctx or self.ctx).enter_context(self.nc.sbuf_tensor(name, shape, dt))

    def sem(self, name, lasting=False):
        if lasting:
            return self.ctx.enter_context(self.nc.semaphore(name))
        self.passing.append(self.nc.alloc_semaphore(name=name))
        return self.passing[-1]

    def end_phase(self):
        sems, self.passing = self.passing, []
        with self.nc.Block() as block:
            @block.gpsimd
            def _(pool):
                self.nc.clear_and_free_semaphores(sems)

    def hold(self, name, eng, *waits):
        for sem, value in waits:
            if isinstance(value, int) and value <= 0:
                continue
            eng.wait_ge(sem, value)
            if not isinstance(value, int):
                eng.sem_inc(self.held[name], 1)


def need(eng, sem, value):
    if not (isinstance(value, int) and value <= 0):
        eng.wait_ge(sem, value)


class Norm:

    def __init__(self, kit, ctx, name):
        nc = kit.nc
        self.kit, self.name = kit, name
        self.stats = kit.sb(f"{name}_stats", [T, G, 6], ctx=ctx)
        self.mv = [kit.sb(f"{name}_mv{b}", [T, G, 2], ctx=ctx) for b in range(2)]
        self.std = [kit.sb(f"{name}_std{b}", [T, G], ctx=ctx) for b in range(2)]
        self.rstd = [kit.sb(f"{name}_rstd{b}", [T, G], ctx=ctx) for b in range(2)]
        self.counted = kit.sem(f"{name}_counted")
        self.moments = kit.sem(f"{name}_moments")
        self.rooted = kit.sem(f"{name}_rooted")
        self.inverted = kit.sem(f"{name}_inverted")
        self.done = kit.sem(f"{name}_done")

    def bn_moments(self, dve, x, g, b):
        nc = self.kit.nc
        need(dve, self.moments, g)
        for j in range(G):
            last = nc.vector.bn_stats(self.stats[:, j, :], x[:, j, :])
        last.then_inc(self.counted, 1)
        self.kit.hold("dve", dve, (self.counted, g + 1))
        for j in range(G):
            last = nc.vector.bn_aggr(self.mv[b][:, j, :], self.stats[:, j, :])
        last.then_inc(self.moments, 1)

    def root(self, act, eps, g, b):
        act.wait_ge(self.moments, g + 1)
        self.kit.nc.scalar.activation(self.std[b][:, :], self.mv[b][:, :, 1], ACT.Sqrt,
                                      bias=eps).then_inc(self.rooted, 1)

    def scale(self, dve, out, x, g, b):
        nc = self.kit.nc
        dve.wait_ge(self.rooted, g + 1)
        nc.vector.reciprocal(self.rstd[b][:, :], self.std[b][:, :]).then_inc(self.inverted, 1)
        dve.wait_ge(self.inverted, g + 1)
        for j in range(G):
            last = nc.vector.tensor_scalar(out[:, j, :], x[:, j, :], self.mv[b][:, j, 0:1], self.rstd[b][:, j:j + 1],
                                           ALU.subtract, ALU.mult)
        last.then_inc(self.done, 1)


def tiles(buf):
    return buf[:, :].rearrange("p (j d) -> p j d", j=G)


def prepare(kit, k, ins):
    nc = kit.nc
    with ExitStack() as ctx:
        def sb(name, shape, dt=F32):
            return kit.sb(name, shape, dt, ctx)

        W = sb("w_cat_loose", [D, R, D])
        att = sb("att", [T, 2, R * D])
        prod = sb("att_prod", [T, R, D])
        a_dst = sb("a_dst", [D, RH])
        bias_r = sb("bias_r", [R, D])
        we1 = sb("we1", [16, 2 * D])
        we1t = sb("we1t", [D, 2, 16])
        we2 = sb("we2", [D, 2, D])
        be1 = sb("be1", [D, 2])
        be2 = sb("be2", [D, 1])
        relw = sb("relw", [T, R])
        relw3 = sb("relw3", [R, 1])
        tmp = sb("tmp", [T, 16])
        colm = sb("colm", [D, 6, 2])
        col2 = sb("col2", [D, 6])
        P0 = ctx.enter_context(nc.psum_tensor("prep0", [T, 512], F32))
        P1 = ctx.enter_context(nc.psum_tensor("prep1", [T, 512], F32))
        P2 = ctx.enter_context(nc.psum_tensor("prep2", [T, 512], F32))
        loaded, made, chain, turned, folded, rooted, masks = (kit.sem(f"prep_{n}") for n in (
            "loaded", "made", "chain", "turned", "folded", "rooted", "masks"))
        loads = []

        def col(ap):
            return ap.rearrange("(p a) -> p a", a=1)

        def bcast(ap, n):
            return ap.rearrange("(a n) -> a n", a=1).to_broadcast([T, n])

        loads += [(k.wl1, ins["L0_gnn_Wl1"]), (k.wr1, ins["L0_gnn_Wr1"]), (k.wl2, ins["L0_gnn_Wl2"]),
                  (k.wr2, ins["L0_gnn_Wr2"]), (k.w2, ins["L2_gnn_weight"]), (k.wm1, ins["L3_gnn_Wm1"]),
                  (we1, ins["L3_gnn_We1"])]
        loads = [(a[:, :], b) for a, b in loads]
        loads += [(W[:, :, :], ins["L1_gnn_W"].rearrange("r k n -> k r n")),
                  (k.wm2[:, :, :], ins["L3_gnn_Wm2"].rearrange("(a k) n -> k a n", a=2)),
                  (we2[:, :, :], ins["L3_gnn_We2"].rearrange("(a k) n -> k a n", a=2)),
                  (bias_r[:, :], ins["L1_gnn_bias"]),
                  (relw[:, :], bcast(ins["L1_gnn_rel_w"], R)),
                  (k.eps1[:, :], bcast(ins["L3_gnn_eps"], 1)),
                  (k.bl1_col[:, :], col(ins["L0_gnn_bl1"])), (k.bl2_col[:, :], col(ins["L0_gnn_bl2"])),
                  (be2[:, :], col(ins["L3_gnn_be2"])),
                  (be1[:, :], ins["L3_gnn_be1"].rearrange("(a p) -> p a", a=2)),
                  (k.bl1_row[:, :], bcast(ins["L0_gnn_bl1"], D)), (k.bl2_row[:, :], bcast(ins["L0_gnn_bl2"], D)),
                  (k.b2_row[:, :], bcast(ins["L2_gnn_bias"], D)),
                  (att[:, 0, :], bcast(ins["L1_gnn_att_src"].rearrange("r h c -> (r h c)"), R * D)),
                  (att[:, 1, :], bcast(ins["L1_gnn_att_dst"].rearrange("r h c -> (r h c)"), R * D))]
        for n, name in enumerate(("bm1", "g1", "b1", "m1", "v1")):
            loads.append((colm[:, n, :], ins[f"L3_gnn_{name}"].rearrange("(a p) -> p a", a=2)))
        for n, name in enumerate(("bm2", "g2", "b2", "m2", "v2")):
            loads.append((col2[:, n:n + 1], col(ins[f"L3_gnn_{name}"])))

        with nc.Block() as block:
            @block.sync
            def _(sp):
                with nc.allow_non_contiguous_dma(reason="per-feature vectors, one value to a partition"):
                    for dst, src in loads:
                        sp.dma_start(dst, src).then_inc(loaded, 16)
                sp.wait_ge(loaded, 16 * len(loads))

            @block.gpsimd
            def _(pool):
                nc.gpsimd.memset(k.ident[:, :], 0.0).then_inc(masks, 1)
                nc.gpsimd.memset(k.chunk_of[:, :], 1.0).then_inc(masks, 1)
                nc.gpsimd.memset(k.one_chunk[:, :, :], 0.0).then_inc(masks, 1)
                nc.gpsimd.memset(k.head_sel[:, :, :, :], 0.0).then_inc(masks, 1)
                pool.wait_ge(masks, 4)
                nc.gpsimd.affine_select(out=k.ident[:, :], in_=k.ident[:, :], compare_op=ALU.not_equal, fill=1.0,
                                        base=0, pattern=[[-1, T]], channel_multiplier=1).then_inc(made, 1)
                nc.gpsimd.affine_select(out=k.chunk_of[:, :], in_=k.chunk_of[:, :], compare_op=ALU.is_ge, fill=0.0,
                                        base=0, pattern=[[1, Q]], channel_multiplier=-RH).then_inc(masks, 1)
                pool.wait_ge(masks, 5)
                nc.gpsimd.affine_select(out=k.chunk_of[:, :], in_=k.chunk_of[:, :], compare_op=ALU.is_ge, fill=0.0,
                                        base=RH - 1, pattern=[[-1, Q]], channel_multiplier=RH).then_inc(made, 1)
                nc.gpsimd.affine_select(out=k.one_chunk[:, :, :], in_=k.one_chunk[:, :, :],
                                        compare_op=ALU.not_equal, fill=1.0, base=0,
                                        pattern=[[-1, CHUNKS], [0, T]], channel_multiplier=1).then_inc(made, 1)
                for r in range(R):
                    nc.gpsimd.affine_select(out=k.head_sel[:, r, :, :], in_=k.head_sel[:, r, :, :],
                                            compare_op=ALU.not_equal, fill=1.0, base=-H * r,
                                            pattern=[[-RH, CHUNKS], [-1, H]], channel_multiplier=1).then_inc(made, 1)

            @block.scalar
            def _(act):
                act.wait_ge(folded, 1)
                nc.scalar.activation(tmp[:, 0:R], tmp[:, 4:4 + R], ACT.Exp).then_inc(rooted, 1)
                act.wait_ge(folded, 2)
                nc.scalar.activation(colm[:, 5, :], colm[:, 4, :], ACT.Sqrt).then_inc(rooted, 1)
                nc.scalar.activation(col2[:, 5:6], col2[:, 4:5], ACT.Sqrt).then_inc(rooted, 1)

            @block.tensor
            def _(pe):
                pe.wait_ge(loaded, 16 * len(loads))
                pe.wait_ge(made, 3 + R)
                for a in range(2):
                    last = nc.tensor.transpose(P0[:, 16 * a:16 * a + 16], we1[:, a * D:(a + 1) * D],
                                               k.ident[0:16, 0:16])
                last.then_inc(turned, 1)
                pe.wait_ge(folded, 3)
                for a in range(2):
                    nc.tensor.matmul(P1[0:16, 0:D], we1t[:, a, :], we2[:, a, :], start=a == 0, stop=a == 1)
                for a in range(2):
                    last = nc.tensor.matmul(P2[:, 0:1], we2[:, a, :], be1[:, a:a + 1], start=a == 0, stop=a == 1)
                last.then_inc(turned, 1)
                pe.wait_ge(folded, 4)
                nc.tensor.matmul(P0[:, 64:65], bias_r[:, :], relw3[:, :], start=True, stop=True).then_inc(turned, 1)

            @block.vector
            def _(dve):
                count = [0]

                def link(ins):
                    count[0] += 1
                    ins.then_inc(chain, 1)
                    dve.wait_ge(chain, count[0])

                link(nc.vector.memset(k.eps[:, :], LN_EPS))
                link(nc.vector.memset(k.one[:, :], 1.0))
                dve.wait_ge(loaded, 16 * len(loads))
                link(nc.vector.reduce_max(tmp[:, 3:4], relw[:, :], AX_X))
                nc.vector.tensor_scalar(tmp[:, 4:4 + R], relw[:, :], tmp[:, 3:4], None,
                                        ALU.subtract).then_inc(folded, 1)
                dve.wait_ge(rooted, 1)
                link(nc.vector.reduce_sum(tmp[:, 8:9], tmp[:, 0:R], AX_X))
                link(nc.vector.reciprocal(tmp[:, 9:10], tmp[:, 8:9]))
                link(nc.vector.tensor_scalar(k.rel[:, :], tmp[:, 0:R], tmp[:, 9:10], None, ALU.mult))
                link(nc.vector.tensor_scalar(colm[:, 4, :], colm[:, 4, :], BN_EPS, None, ALU.add))
                nc.vector.tensor_scalar(col2[:, 4:5], col2[:, 4:5], BN_EPS, None, ALU.add).then_inc(folded, 1)
                link(nc.vector.tensor_copy(k.w_cat[:, :, :], W[:, :, :]))
                link(nc.vector.tensor_scalar(k.w_bar[:, :], W[:, 0, :], k.rel[:, 0:1], None, ALU.mult))
                for r in range(1, R):
                    link(nc.vector.scalar_tensor_tensor(k.w_bar[:, :], W[:, r, :], k.rel[:, r:r + 1],
                                                        k.w_bar[:, :], ALU.mult, ALU.add))
                for s, out in ((0, k.score_w[:, 1, 0:RH]), (1, a_dst[:, :])):
                    link(nc.vector.tensor_tensor(prod[:, :, :], W[:, :, :],
                                                 att[:, s, :].rearrange("p (r d) -> p r d", r=R), ALU.mult))
                    link(nc.vector.reduce_sum(out, prod[:, :, :].rearrange("p r (h c) -> p (r h) c", h=H), AX_X))
                link(nc.vector.memset(k.score_w[:, 1, RH:2 * RH], 0.0))
                for s in range(2):
                    link(nc.vector.tensor_tensor(k.score_w[:, 0, s * RH:(s + 1) * RH], k.score_w[:, 1, 0:RH],
                                                 a_dst[:, :], ALU.add))
                dve.wait_ge(turned, 1)
                nc.vector.tensor_copy(we1t[:, :, :], P0[:, 0:32].rearrange("p (a n) -> p a n", a=2)).then_inc(folded, 1)
                dve.wait_ge(turned, 2)
                link(nc.vector.tensor_copy(k.we[:, :], P1[0:16, 0:D]))
                link(nc.vector.tensor_tensor(k.be_col[:, :], P2[:, 0:1], be2[:, :], ALU.add))
                dve.wait_ge(made, 3 + R)
                link(nc.vector.tensor_tensor(tmp[0:R, 12:12 + R], k.rel[0:R, :], k.ident[0:R, 0:R], ALU.mult))
                nc.vector.reduce_sum(relw3[:, :], tmp[0:R, 12:12 + R], AX_X).then_inc(folded, 1)
                dve.wait_ge(turned, 3)
                link(nc.vector.tensor_copy(k.bbar_col[:, :], P0[:, 64:65]))
                hw = k.head_w[:, :].rearrange("q (c h) -> q c h", h=H)
                link(nc.vector.tensor_scalar(hw, k.head_sel[:, 0, :, :], k.rel[0:Q, 0:1], None, ALU.mult))
                for r in range(1, R):
                    link(nc.vector.scalar_tensor_tensor(hw, k.head_sel[:, r, :, :], k.rel[0:Q, r:r + 1], hw,
                                                        ALU.mult, ALU.add))
                dve.wait_ge(rooted, 3)
                link(nc.vector.tensor_scalar(k.eps1[:, :], k.eps1[:, :], 1.0, None, ALU.add))
                for cc, scale, bias in ((lambda n: colm[:, n, :], k.bn1_s[:, :], k.bn1_b[:, :]),
                                        (lambda n: col2[:, n:n + 1], k.bn2_s[:, :], k.bn2_b[:, :])):
                    link(nc.vector.reciprocal(cc(5), cc(5)))
                    link(nc.vector.tensor_tensor(scale, cc(5), cc(1), ALU.mult))
                    link(nc.vector.tensor_tensor(cc(0), cc(0), cc(3), ALU.subtract))
                    link(nc.vector.tensor_tensor(cc(0), cc(0), scale, ALU.mult))
                    link(nc.vector.tensor_tensor(bias, cc(0), cc(2), ALU.add))
                link(nc.vector.tensor_scalar(k.bn1_s_own[:, :], k.bn1_s[:, :], k.eps1[:, 0:1], None, ALU.mult))


class Scans:

    def __init__(self, kit, k, ctx, name, psum):
        self.kit, self.k, self.nc = kit, k, kit.nc
        self.row = kit.sb(f"{name}_row", [1, RH, CHUNKS], ctx=ctx)
        self.into = kit.sb(f"{name}_into", [1, CHUNKS, RH], ctx=ctx)
        self.carry = kit.sb(f"{name}_carry", [Q, 1], ctx=ctx)
        self.end = kit.sb(f"{name}_end", [Q, 1], ctx=ctx)
        self.turn, self.back = psum[0:1, 0:Q], psum[0:Q, 128:129]
        self.end_ready, self.turned, self.into_ready, self.returned = (
            kit.sem(f"{name}_{n}") for n in ("end_ready", "turned", "into_ready", "returned"))
        self.dve_n = self.pe_n = 0

    def pe_row(self, pe):
        self.pe_n += 1
        pe.wait_ge(self.end_ready, self.pe_n)
        self.nc.tensor.transpose(self.turn, self.end[:, :], self.k.ident[0:Q, 0:Q]).then_inc(self.turned, 1)

    def pe_scan(self, pe):
        self.pe_row(pe)
        pe.wait_ge(self.into_ready, self.pe_n)
        self.nc.tensor.matmul(self.back, self.into[:, :, :].rearrange("p c r -> p (c r)"), self.k.one[0:1, 0:1],
                              start=True, stop=True).then_inc(self.returned, 1)

    def gather_row(self, dve, link, src, forward):
        self.dve_n += 1
        self.nc.vector.tensor_copy(self.end[:, :], src).then_inc(self.end_ready, 1)
        dve.wait_ge(self.turned, self.dve_n)
        turned = self.turn.rearrange("p (c r) -> p r c", r=RH)
        for c in range(CHUNKS):
            s = c if forward else CHUNKS - 1 - c
            last = self.nc.vector.tensor_copy(self.row[:, :, c:c + 1], turned[:, :, s:s + 1])
        link(last)

    def flags_row(self, dve, link, product, out, forward):
        edge = product[:, -1:] if forward else product[:, 0:1]
        self.gather_row(dve, link, edge, forward)
        link(self.nc.vector.tensor_copy(out[:, :, :], self.row[:, :, :]))
        link(self.nc.vector.memset(out[:, :, 0:1], 0.0))
        self.nc.vector.memset(self.into[:, :, :], 0.0).then_inc(self.into_ready, 1)
        dve.wait_ge(self.returned, self.dve_n)

    def scan(self, dve, link, out, data, flags, product, flags_row, op, forward):
        vec = self.nc.vector
        n = out.shape[1]
        if forward:
            link(vec.tensor_tensor_scan(out[:, :], flags, data, 0.0, ALU.mult, op))
        else:
            link(vec.tensor_tensor_scan(out[:, ::-1], flags[:, ::-1], data[:, ::-1], 0.0, ALU.mult, op))
        self.gather_row(dve, link, out[:, n - 1:n] if forward else out[:, 0:1], forward)
        row = self.row[:, :, :].rearrange("p r c -> p (r c)")
        link(vec.tensor_tensor_scan(row, flags_row[:, :, :].rearrange("p r c -> p (r c)"), row, 0.0, ALU.mult, op))
        link(vec.memset(self.into[:, :, :], 0.0))
        for c in range(1, CHUNKS):
            d = c if forward else CHUNKS - 1 - c
            last = vec.tensor_copy(self.into[:, d:d + 1, :].rearrange("p c r -> p r c"), self.row[:, :, c - 1:c])
        last.then_inc(self.into_ready, 1)
        dve.wait_ge(self.returned, self.dve_n)
        link(vec.tensor_copy(self.carry[:, :], self.back))
        link(vec.scalar_tensor_tensor(out[:, :], product, self.carry[:, 0:1], out[:, :], ALU.mult, op))


class Chain:

    def __init__(self, kit, name):
        self.sem, self.count = kit.sem(name), 0

    def on(self, eng):
        def link(ins):
            self.count += 1
            ins.then_inc(self.sem, 1)
            eng.wait_ge(self.sem, self.count)
        return link


def turn_rows(kit, k, name, psum, src, parts, M, take):
    nc = kit.nc
    turned, took = kit.sem(f"{name}_turned"), kit.sem(f"{name}_took")
    with nc.Block() as block:
        @block.tensor
        def _(pe):
            for n in range(M // 4):
                need(pe, took, n - 1)
                for j in range(4):
                    t = 4 * n + j
                    last = nc.tensor.transpose(psum[n % 2][:, j * T:j * T + parts], src[:, t * T:(t + 1) * T],
                                               k.ident[0:parts, 0:parts])
                last.then_inc(turned, 1)

        @block.vector
        def _(dve):
            for n in range(M // 4):
                dve.wait_ge(turned, n + 1)
                take(n, psum[n % 2][:, :].rearrange("p (j q) -> p j q", j=4)).then_inc(took, 1)


def by_chunk(rows):
    return rows[:, :].rearrange("p (c j) -> p j c", c=CHUNKS)


def index_stage(kit, k, src, dst, etype, N, E, M):
    nc = kit.nc
    CH = M * T
    PIECES = CH // 512
    with ExitStack() as ctx:
        def sb(name, shape, dt=F32):
            return kit.sb(name, shape, dt, ctx)

        raw = sb("raw", [T, CH + 2], I32)
        val = sb("val", [T, CH + 2])
        same7 = sb("same7", [CHUNKS, CH])
        next7 = sb("next7", [CHUNKS, CH])
        far7 = sb("far7", [T, CH])
        wide = sb("wide", [Q, CH])
        wide2 = sb("wide2", [Q, CH])
        number7 = wide2[0:CHUNKS, :].bitcast(I32)
        psum = [ctx.enter_context(nc.psum_tensor(f"ix{i}", [T, 512], F32)) for i in range(8)]
        sc = Scans(kit, k, ctx, "ixs", psum[7])
        cleared, loaded, numbered, spread, copied, turned0, took0, copied_same = (kit.sem(f"ix_{n}") for n in (
            "cleared", "loaded", "numbered", "spread", "copied", "turned0", "took0", "copied_same"))
        chain = Chain(kit, "ix_chain")
        parts = max(p for p in range(1, T + 1) if N % p == 0)
        identity = sb("identity_place", [parts, N // parts], I32)
        loads = []
        for c in range(CHUNKS):
            lo, hi = max(c * CH - 1, 0), min(c * CH + CH + 1, E)
            at = lo - (c * CH - 1)
            for base, a in ((0, dst), (96, dst), (32, src), (64, etype)):
                loads.append((raw[base + c:base + c + 1, at:at + hi - lo], a[lo:hi].rearrange("(a n) -> a n", a=1)))

        with nc.Block() as block:
            @block.sync
            def _(sp):
                sp.wait_ge(cleared, 1)
                for o, i in loads:
                    sp.dma_start(o, i).then_inc(loaded, 16)
                sp.wait_ge(loaded, 16 * len(loads))
                sp.wait_ge(numbered, 3)
                sp.dma_start(k.place[:, :].rearrange("(p n) a -> p (n a)", p=parts), identity[:, :]
                             ).then_inc(kit.place_clear, 16)
                sp.wait_ge(kit.place_clear, 16)

            @block.gpsimd
            def _(pool):
                nc.gpsimd.iota(k.edge_row[:, :], pattern=[[T, k.NT]], base=N, channel_multiplier=1).then_inc(numbered, 1)
                nc.gpsimd.iota(number7[:, :], pattern=[[1, CH]], base=N, channel_multiplier=CH).then_inc(numbered, 1)
                nc.gpsimd.iota(identity[:, :], pattern=[[1, N // parts]], base=0,
                               channel_multiplier=N // parts).then_inc(numbered, 1)

            @block.vector
            def _(dve):
                v, link = nc.vector, chain.on(dve)
                link(v.memset(raw[:, :], 0))
                for base in (0, 96):
                    link(v.memset(raw[base:base + CHUNKS, 0:1], -1))
                    link(v.memset(raw[base:base + CHUNKS, 1:CH + 1], N))
                    link(v.memset(raw[base:base + CHUNKS, CH + 1:CH + 2], N + 1))
                v.memset(sc.into[:, :, :], 0.0).then_inc(cleared, 1)
                dve.wait_ge(loaded, 16 * len(loads))
                link(v.tensor_copy(val[:, :], raw[:, :]))
                link(v.tensor_tensor(same7[:, :], val[0:CHUNKS, 1:CH + 1], val[0:CHUNKS, 0:CH], ALU.is_equal))
                link(v.tensor_tensor(next7[:, :], val[0:CHUNKS, 1:CH + 1], val[0:CHUNKS, 2:CH + 2], ALU.is_equal))
                a96, f96 = val[96:96 + CHUNKS, :], far7[96:96 + CHUNKS, :]
                link(v.tensor_tensor(f96, a96[:, 1:CH + 1], a96[:, 2:CH + 2], ALU.is_equal))
                link(v.scalar_tensor_tensor(a96[:, 1:CH + 1], f96, FAR, a96[:, 1:CH + 1], ALU.mult, ALU.add))
                link(v.tensor_scalar(val[0:CHUNKS, 1:CH + 1], val[0:CHUNKS, 1:CH + 1], float(N - 1), None, ALU.min))
                dve.wait_ge(numbered, 2)
                link(v.tensor_copy(far7[0:CHUNKS, :], number7[:, :]))
                link(v.tensor_scalar(raw[0:CHUNKS, 0:CH].bitcast(F32), next7[:, :], -1.0, 1.0, ALU.mult, ALU.add))
                link(v.tensor_tensor(far7[0:CHUNKS, :], far7[0:CHUNKS, :], raw[0:CHUNKS, 0:CH].bitcast(F32), ALU.mult))

        def take(n, bank):
            for f, out in enumerate((k.dst_i, k.src_i, k.type_f, k.last_i)):
                ins = nc.vector.tensor_copy(by_chunk(out)[:, 4 * n:4 * n + 4, :], bank[:, :, 32 * f:32 * f + CHUNKS])
            return ins

        turn_rows(kit, k, "ix_all", psum, val[:, 1:CH + 1], T, M, take)

        jobs = [(same7, k.same84), (next7, k.next84), (far7, wide)]
        with nc.Block() as block:
            @block.tensor
            def _(pe):
                for n in range(3 * PIECES):
                    at = n % PIECES * 512
                    need(pe, copied, n - 1)
                    nc.tensor.matmul(psum[n % 2][0:Q, :], k.chunk_of[:, :], jobs[n // PIECES][0][0:CHUNKS, at:at + 512],
                                     start=True, stop=True).then_inc(spread, 1)
                for n in range(k.NG):
                    at = n % PIECES * 512
                    need(pe, copied_same, n - 1)
                    nc.tensor.matmul(psum[2 + n % 2][:, :], k.one_chunk[:, n // PIECES, :], same7[:, at:at + 512],
                                     start=True, stop=True).then_inc(turned0, 1)

            @block.vector
            def _(dve):
                for n in range(3 * PIECES):
                    at = n % PIECES * 512
                    dve.wait_ge(spread, n + 1)
                    nc.vector.tensor_copy(jobs[n // PIECES][1][:, at:at + 512], psum[n % 2][0:Q, :]).then_inc(copied, 1)

            @block.scalar
            def _(act):
                for n in range(k.NG):
                    act.wait_ge(turned0, n + 1)
                    nc.scalar.activation(k.same[:, n * 512:(n + 1) * 512], psum[2 + n % 2][:, :],
                                         ACT.Copy).then_inc(copied_same, 1)

        with nc.Block() as block:
            @block.vector
            def _(dve):
                v, link = nc.vector, chain.on(dve)
                for r in range(R):
                    link(v.tensor_scalar(k.is_type[:, :, r], k.type_f[:, :], float(r), None, ALU.is_equal))
                link(v.memset(wide2[:, :], 0.0))
                link(v.tensor_tensor_scan(k.prod_f[:, :], k.same84[:, :], wide2[:, :], 1.0, ALU.mult, ALU.add))
                link(v.tensor_tensor_scan(k.prod_b[:, ::-1], k.next84[:, ::-1], wide2[:, ::-1], 1.0, ALU.mult, ALU.add))
                sc.flags_row(dve, link, k.prod_f, k.flow_f, True)
                sc.flags_row(dve, link, k.prod_b, k.flow_b, False)
                sc.scan(dve, link, wide2, wide[:, :], k.next84[:, :], k.prod_b[:, :], k.flow_b, ALU.add, False)

            @block.tensor
            def _(pe):
                for _ in range(3):
                    sc.pe_scan(pe)

        turn_rows(kit, k, "ix_pos", psum, wide2, Q, M, lambda n, bank: nc.vector.tensor_copy(
            by_chunk(k.dstp_i)[:, 4 * n:4 * n + 4, :], bank[:, :, 0:Q:RH]))

        with nc.Block() as block:
            @block.vector
            def _(dve):
                v, link = nc.vector, chain.on(dve)
                link(v.memset(wide[:, :], 1.0))
                sc.scan(dve, link, wide2, wide[:, :], k.same84[:, :], k.prod_f[:, :], k.flow_f, ALU.add, True)

            @block.tensor
            def _(pe):
                sc.pe_scan(pe)

        turn_rows(kit, k, "ix_deg", psum, wide2, Q, M, lambda n, bank: nc.vector.tensor_copy(
            by_chunk(k.deg)[:, 4 * n:4 * n + 4, :], bank[:, :, 0:Q:RH]))
        with nc.Block() as block:
            @block.vector
            def _(dve):
                nc.vector.reciprocal(k.rdeg[:, :], k.deg[:, :]).then_inc(cleared, 1)

            @block.scalar
            def _(act):
                act.wait_ge(cleared, 2)
                nc.scalar.activation(k.norm[:, :], k.rdeg[:, :], ACT.Sqrt)


def place_stage_pool(kit, k, pool, bufs):
    nc = kit.nc
    now, vals, got, staged, put, fetched, kept = bufs
    pool.wait_ge(kit.place_clear, 16)

    def scatter(i, first):
        if not first:
            kit.hold("pool", pool, (put, i * 16 * G))
        nc.gpsimd.tensor_copy(now[:, :], k.last_i[:, bass.ds(i * G, G)]).then_inc(staged, 1)
        nc.gpsimd.tensor_copy(vals[:, :], k.edge_row[:, bass.ds(i * G, G)]).then_inc(staged, 1)
        kit.hold("pool", pool, (staged, i * 2 + 2))
        for j in range(G):
            pool.indirect_dma_start(k.place, bass.IndirectOffsetOnAxis(ap=now[:, j:j + 1], axis=0),
                                    vals[:, j:j + 1], None, bounds_check=k.N - 1, oob_is_err=False).then_inc(put, 16)

    scatter(0, True)
    with pool.Fori(1, k.NG) as i:
        scatter(i, False)
    pool.wait_ge(put, k.NG * G * 16)

    def fetch(i, first):
        nc.gpsimd.tensor_copy(now[:, :], k.src_i[:, bass.ds(i * G, G)]).then_inc(staged, 1)
        kit.hold("pool", pool, (staged, 2 * k.NG + 1 + i))
        for j in range(G):
            pool.indirect_dma_start(got[:, j:j + 1], None, k.place,
                                    bass.IndirectOffsetOnAxis(ap=now[:, j:j + 1], axis=0)).then_inc(fetched, 16)
        kit.hold("pool", pool, (fetched, (i + 1) * 16 * G))
        nc.gpsimd.tensor_copy(k.srcp_i[:, bass.ds(i * G, G)], got[:, :]).then_inc(kept, 1)
        kit.hold("pool", pool, (kept, i + 1))

    fetch(0, True)
    with pool.Fori(1, k.NG) as i:
        fetch(i, False)


def dense_pass(kit, k, x, out):
    nc = kit.nc
    N = k.N
    groups = -(-N // W)
    LAG = 9
    with ExitStack() as ctx:
        def pair(name, shape=(T, W), dt=F32):
            return [kit.sb(f"dn_{name}{b}", list(shape), dt, ctx) for b in range(2)]

        X, XT, H1T, H1R, H2T, YT, X1R, X1T, Y2T = (pair(n) for n in "X XT H1T H1R H2T YT X1R X1T Y2T".split())
        X2R, Y3, X3R, X3T, MA, MB, T7, Y4T, X4R = (pair(n) for n in "X2R Y3 X3R X3T MA MB T7 Y4T X4R".split())
        B = [ctx.enter_context(nc.psum_tensor(f"dn_bank{i}", [T, 512], F32)) for i in range(8)]
        ln = [Norm(kit, ctx, f"dn_ln{i}") for i in range(4)]
        now = kit.sb("pl_now", [T, G], I32, ctx)
        vals = kit.sb("pl_vals", [T, G], I32, ctx)
        got = kit.sb("pl_got", [T, G], I32, ctx)
        pool_bufs = (now, vals, got) + tuple(kit.sem(f"pl_{n}", n in ("put", "fetched"))
                                             for n in ("staged", "put", "fetched", "kept"))
        sem = {n: kit.sem(f"dn_{n}") for n in (
            "xt_turned xt h1_mul h1t h1_turned h1r h2_mul h2t yt yt_turned x1_turned x1t bar_mul y2t y2_turned "
            "y3 x3_turned x3t ma_mul mb_mul ma mb out_mul t7 y4t y4_turned").split()}
        x_in = [kit.sem(f"dn_x_in{b}") for b in range(2)]
        h1_out, x1_out, x2_out, x3_out, out_out = ([kit.sem(f"dn_{n}{b}") for b in range(2)] for n in (
            "h1_out", "x1_out", "x2_out", "x3_out", "out_out"))
        S = sem

        def rows(dram, g):
            base = g * W if not isinstance(g, int) else min(g * W, N - W)
            return dram[bass.ds(base, W), :].rearrange("(p j) d -> p (j d)", j=G)

        with nc.Block() as block:
            @block.gpsimd
            def _(pool):
                place_stage_pool(kit, k, pool, pool_bufs)

            @block.sync
            def _(sp):
                def load(g, h, b):
                    need(sp, S["xt_turned"], g - 1)
                    sp.dma_start(X[b][:, :], rows(x, g)).then_inc(x_in[b], 16)

                def store(dram, buf, written, stored):
                    def stage(g, h, b):
                        sp.wait_ge(written, g + 1)
                        if isinstance(g, int) and g == groups - 1:
                            sp.wait_ge(stored[1 - b], 16 * ((g - 1) // 2 + 1))
                        sp.dma_start(rows(dram, g), buf[b][:, :]).then_inc(stored[b], 16)
                    return stage

                def body(at):
                    rounds(at, [(0, load),
                                (2, store(k.tab[0], H1R, S["h1r"], h1_out)),
                                (3, store(k.tab[1], X1R, ln[0].done, x1_out)),
                                (5, store(k.tab[2], X2R, ln[1].done, x2_out)),
                                (6, store(k.tab[3], X3R, ln[2].done, x3_out)),
                                (9, store(out, X4R, ln[3].done, out_out))])

                steps(sp, groups, LAG, body)
                for s in (h1_out, x1_out, x2_out, x3_out, out_out):
                    for b in range(2):
                        sp.wait_ge(s[b], 16 * ((groups - b + 1) // 2))

            @block.tensor
            def _(pe):
                def turn(bank, buf, done):
                    for j in range(G):
                        last = nc.tensor.transpose(bank[:, j * T:(j + 1) * T], buf[:, j * T:(j + 1) * T], k.ident[:, :])
                    last.then_inc(done, 1)

                def turn_x(g, h, b):
                    pe.wait_ge(x_in[b], (h + 1) * 16)
                    need(pe, S["xt"], g)
                    need(pe, S["h1r"], g - 1)
                    turn(B[0], X[b], S["xt_turned"])

                def mul_h1(g, h, b):
                    pe.wait_ge(S["xt"], g + 1)
                    need(pe, S["h2t"], g)
                    nc.tensor.matmul(B[1][:, :], k.wr1[:, :], XT[b][:, :], start=True, stop=True).then_inc(S["h1_mul"], 1)

                def turn_h1(g, h, b):
                    pe.wait_ge(S["h1t"], g + 1)
                    pe.wait_ge(S["xt"], (min(g + 2, groups) if isinstance(g, int) else g + 2))
                    turn(B[0], H1T[b], S["h1_turned"])

                def mul_h2(g, h, b):
                    pe.wait_ge(S["h1t"], g + 1)
                    nc.tensor.matmul(B[1][:, :], k.wr2[:, :], H1T[b][:, :], start=True, stop=True).then_inc(S["h2_mul"], 1)

                def turn_y(g, h, b):
                    pe.wait_ge(S["yt"], g + 1)
                    need(pe, ln[0].done, g)
                    turn(B[2], YT[b], S["yt_turned"])

                def turn_x1(g, h, b):
                    pe.wait_ge(ln[0].done, g + 1)
                    need(pe, S["y2t"], g)
                    turn(B[3], X1R[b], S["x1_turned"])

                def mul_bar(g, h, b):
                    pe.wait_ge(S["x1t"], g + 1)
                    nc.tensor.matmul(B[3][:, :], k.w_bar[:, :], X1T[b][:, :], start=True, stop=True).then_inc(S["bar_mul"], 1)

                def turn_y2(g, h, b):
                    pe.wait_ge(S["y2t"], g + 1)
                    need(pe, ln[1].done, g)
                    turn(B[4], Y2T[b], S["y2_turned"])

                def turn_x3(g, h, b):
                    pe.wait_ge(ln[2].done, g + 1)
                    need(pe, S["ma"], g)
                    turn(B[5], X3R[b], S["x3_turned"])

                def mul_ma(g, h, b):
                    pe.wait_ge(S["x3t"], g + 1)
                    nc.tensor.matmul(B[5][:, :], k.wm1[:, 0:D], X3T[b][:, :], start=True, stop=True).then_inc(S["ma_mul"], 1)

                def mul_mb(g, h, b):
                    need(pe, S["t7"], g)
                    nc.tensor.matmul(B[6][:, :], k.wm1[:, D:2 * D], X3T[b][:, :], start=True, stop=True).then_inc(S["mb_mul"], 1)

                def mul_out(g, h, b):
                    pe.wait_ge(S["mb"], (min(g + 1, groups) if isinstance(g, int) else g + 1))
                    nc.tensor.matmul(B[6][:, :], k.wm2[:, 0, :], MA[b][:, :], start=True, stop=False)
                    nc.tensor.matmul(B[6][:, :], k.wm2[:, 1, :], MB[b][:, :], start=False, stop=True).then_inc(S["out_mul"], 1)

                def turn_y4(g, h, b):
                    pe.wait_ge(S["y4t"], g + 1)
                    need(pe, ln[3].done, g)
                    turn(B[7], Y4T[b], S["y4_turned"])

                def body(at):
                    rounds(at,
                           [(1, turn_x), (2, mul_h1), (3, turn_y), (4, turn_x1), (5, turn_y2), (7, turn_x3),
                            (8, mul_out), (9, turn_y4)],
                           [(2, turn_h1), (4, mul_bar), (7, mul_ma)],
                           [(2, mul_h2), (7, mul_mb)])

                steps(pe, groups, LAG, body)

            @block.scalar
            def _(act):
                def copy(dst, bank, ready, done, free=None):
                    def stage(g, h, b):
                        if free is not None:
                            need(act, free, g - 1)
                        act.wait_ge(ready, g + 1)
                        nc.scalar.activation(dst[b][:, :], bank[:, :], ACT.Copy).then_inc(done, 1)
                    return stage

                def affine(dst, bank, ready, done, func, bias, scale=1.0, free=None, out=None):
                    def stage(g, h, b):
                        if out is not None and not (isinstance(h, int) and h <= 0):
                            act.wait_ge(out[b], h * 16)
                        if free is not None:
                            need(act, free, g - 1)
                        act.wait_ge(ready, g + 1)
                        nc.scalar.activation(dst[b][:, :], bank[:, :], func, bias=bias, scale=scale).then_inc(done, 1)
                    return stage

                def copy_h1(g, h, b):
                    if not (isinstance(h, int) and h <= 0):
                        act.wait_ge(h1_out[b], h * 16)
                    act.wait_ge(S["h1_turned"], g + 1)
                    nc.scalar.activation(H1R[b][:, :], B[0][:, :], ACT.Copy).then_inc(S["h1r"], 1)

                def root(n):
                    return lambda g, h, b: ln[n].root(act, k.eps[:, 0:1], g, b)

                def body(at):
                    rounds(at,
                           [(1, copy(XT, B[0], S["xt_turned"], S["xt"], S["yt"])),
                            (2, affine(H1T, B[1], S["h1_mul"], S["h1t"], ACT.Relu, k.bl1_col[:, 0:1], free=S["h2_mul"])),
                            (3, root(0)),
                            (4, copy(X1T, B[3], S["x1_turned"], S["x1t"], S["y2t"])),
                            (5, root(1)),
                            (7, copy(X3T, B[5], S["x3_turned"], S["x3t"], S["y4t"])),
                            (8, affine(T7, B[6], S["out_mul"], S["t7"], ACT.Identity, k.bn2_b[:, 0:1],
                                       k.bn2_s[:, 0:1], free=S["y4t"])),
                            (9, root(3))],
                           [(2, copy_h1), (6, root(2)),
                            (7, affine(MA, B[5], S["ma_mul"], S["ma"], ACT.Relu, k.bn1_b[:, 0:1],
                                       k.bn1_s_own[:, 0:1], free=S["out_mul"]))],
                           [(2, affine(H2T, B[1], S["h2_mul"], S["h2t"], ACT.Relu, k.bl2_col[:, 0:1], free=S["yt"])),
                            (7, affine(MB, B[6], S["mb_mul"], S["mb"], ACT.Relu, k.bn1_b[:, 1:2],
                                       k.bn1_s_own[:, 1:2], free=S["out_mul"]))])

                steps(act, groups, LAG, body)

            @block.vector
            def _(dve):
                v = nc.vector

                def free_out(stored, h, b):
                    if not (isinstance(h, int) and h <= 0):
                        dve.wait_ge(stored[b], h * 16)

                def add_y(g, h, b):
                    need(dve, S["yt_turned"], g - 1)
                    dve.wait_ge(S["h2t"], g + 1)
                    v.tensor_tensor(YT[b][:, :], H2T[b][:, :], XT[b][:, :], ALU.add).then_inc(S["yt"], 1)

                def measure(n, bank, ready):
                    def stage(g, h, b):
                        dve.wait_ge(ready, g + 1)
                        ln[n].bn_moments(dve, tiles(bank), g, b)
                    return stage

                def scale(n, dst, bank, stored, turned=None):
                    def stage(g, h, b):
                        free_out(stored, h, b)
                        if turned is not None:
                            need(dve, turned, g - 1)
                        ln[n].scale(dve, tiles(dst[b]), tiles(bank), g, b)
                    return stage

                def add_y2(g, h, b):
                    need(dve, S["y2_turned"], g - 1)
                    dve.wait_ge(S["bar_mul"], g + 1)
                    v.scalar_tensor_tensor(Y2T[b][:, :], B[3][:, :], k.bbar_col[:, 0:1], X1T[b][:, :],
                                           ALU.add, ALU.add).then_inc(S["y2t"], 1)

                def add_y3(g, h, b):
                    dve.wait_ge(ln[1].done, g + 1)
                    v.tensor_tensor(tiles(Y3[b]), tiles(X2R[b]), over(k.b2_row), ALU.add).then_inc(S["y3"], 1)
                    dve.wait_ge(S["y3"], g + 1)
                    ln[2].bn_moments(dve, tiles(Y3[b]), g, b)

                def scale_y3(g, h, b):
                    free_out(x3_out, h, b)
                    need(dve, S["x3_turned"], g - 1)
                    ln[2].scale(dve, tiles(X3R[b]), tiles(Y3[b]), g, b)

                def add_y4(g, h, b):
                    need(dve, S["y4_turned"], g - 1)
                    dve.wait_ge(S["t7"], g + 1)
                    v.tensor_tensor(Y4T[b][:, :], T7[b][:, :], X3T[b][:, :], ALU.add).then_inc(S["y4t"], 1)

                def body(at):
                    rounds(at,
                           [(3, measure(0, B[2], S["yt_turned"])), (5, measure(1, B[4], S["y2_turned"])),
                            (6, add_y3), (9, measure(3, B[7], S["y4_turned"])), (8, add_y4)],
                           [(3, scale(0, X1R, B[2], x1_out, S["x1_turned"])), (5, scale(1, X2R, B[4], x2_out)),
                            (6, scale_y3), (9, scale(3, X4R, B[7], out_out))],
                           [(2, add_y), (4, add_y2)])

                steps(dve, groups, LAG, body)


def over(row):
    return row[:, :].rearrange("p (a d) -> p a d", a=1).to_broadcast([T, G, D])


def turn(nc, k, bank, buf, done):
    for j in range(G):
        last = nc.tensor.transpose(bank[:, j * T:(j + 1) * T], buf[:, j * T:(j + 1) * T], k.ident[:, :])
    last.then_inc(done, 1)


def multiply_rows(nc, bank, turned, weights, done):
    for j in range(G):
        last = nc.tensor.matmul(bank[:, j * T:(j + 1) * T], turned[:, j * T:(j + 1) * T], weights, start=True, stop=True)
    last.then_inc(done, 1)


def edge_rows(dram, g, base):
    return dram[bass.ds(g * W + base, W), :].rearrange("(j p) d -> p j d", p=T)


class Gather:

    def __init__(self, kit, ctx, name, index, table, bufs):
        self.kit, self.index, self.table, self.bufs = kit, index, table, bufs
        self.now = [kit.sb(f"{name}_now{b}", [T, G], I32, ctx) for b in range(2)]
        self.staged = kit.sem(f"{name}_staged")
        self.arrived = [kit.sem(f"{name}_arrived{b}", True) for b in range(2)]

    def stage(self, pool, free):
        def run(g, h, b):
            nc = self.kit.nc
            waits = list(free(g, h, b))
            if not (isinstance(h, int) and h <= 0):
                waits.append((self.arrived[b], h * 16 * G))
            self.kit.hold("pool", pool, *waits)
            nc.gpsimd.tensor_copy(self.now[b][:, :], self.index[:, bass.ds(g * G, G)]).then_inc(self.staged, 1)
            self.kit.hold("pool", pool, (self.staged, g + 1))
            for j in range(G):
                pool.indirect_dma_start(self.bufs[b][:, j * T:(j + 1) * T], None, self.table,
                                        bass.IndirectOffsetOnAxis(ap=self.now[b][:, j:j + 1], axis=0)
                                        ).then_inc(self.arrived[b], 16)
        return run

    def wait(self, eng, h, b):
        eng.wait_ge(self.arrived[b], (h + 1) * 16 * G)


def segment_sum(kit, k, dve, out, messages, ready, summed, free):
    def stage(g, h, b):
        for sem, value in free(g):
            need(dve, sem, value)
        need(dve, summed, g)
        kit.hold("dve", dve, (ready, g + 1))
        first = isinstance(g, int) and g == 0
        kit.nc.vector.tensor_tensor_scan(out[b][:, :], k.same[:, bass.ds(g * W, W)], messages[b][:, :],
                                         0.0 if first else out[1 - b][:, W - 1:W], ALU.mult, ALU.add).then_inc(summed, 1)
    return stage


def sage(kit, k, name, table, index, own_index, own_table, x_rows, weights, out_table, norm):
    nc = kit.nc
    wl, wr, bias = weights
    LAG = 4
    with ExitStack() as ctx:
        def pair(n):
            return [kit.sb(f"{name}_{n}{b}", [T, W], F32, ctx) for b in range(2)]

        XS, XD, XDT, AG, BASE, MIX, HR = (pair(n) for n in "XS XD XDT AG BASE MIX HR".split())
        if norm:
            XR, Y, OUT = (pair(n) for n in "XR Y OUT".split())
            ln = Norm(kit, ctx, f"{name}_ln")
        else:
            OUT = HR
        B = [ctx.enter_context(nc.psum_tensor(f"{name}_bank{i}", [T, 512], F32)) for i in range(4)]
        src_g = Gather(kit, ctx, f"{name}_src", index, table, XS)
        own_g = Gather(kit, ctx, f"{name}_own", own_index, table, XD) if own_index is not None else None
        s_turned, d_turned, summed, xdt, a_mul, b_mul, base, mixed, hr, added = (kit.sem(f"{name}_{n}") for n in (
            "s_turned", "d_turned", "summed", "xdt", "a_mul", "b_mul", "base", "mixed", "hr", "added"))
        own_in, kept, x_in, stored = ([kit.sem(f"{name}_{n}{b}") for b in range(2)] for n in (
            "own_in", "kept", "x_in", "stored"))
        done = ln.done if norm else hr

        with nc.Block() as block:
            @block.gpsimd
            def _(pool):
                lines = [(0, src_g.stage(pool, lambda g, h, b: [(s_turned, g - 1)]))]
                if own_g:
                    lines.append((0, own_g.stage(pool, lambda g, h, b: [(d_turned, g - 1), (kept[b], h * 16)])))
                steps(pool, k.NG, LAG, lambda at: rounds(at, lines))

            @block.sync
            def _(sp):
                def load(g, h, b):
                    need(sp, d_turned, g - 1)
                    sp.dma_start(tiles(XD[b]), edge_rows(own_table, g, k.N)).then_inc(own_in[b], 16)

                def load_x(g, h, b):
                    need(sp, added, g - 1)
                    sp.dma_start(tiles(XR[b]), edge_rows(x_rows, g, 0)).then_inc(x_in[b], 16)

                def keep(g, h, b):
                    own_g.wait(sp, h, b)
                    sp.dma_start(edge_rows(x_rows, g, 0), tiles(XD[b])).then_inc(kept[b], 16)

                def store(g, h, b):
                    sp.wait_ge(done, g + 1)
                    sp.dma_start(edge_rows(out_table, g, k.N), tiles(OUT[b])).then_inc(stored[b], 16)

                lines = [(1, keep)] if own_g else [(0, load), (1, load_x)]
                steps(sp, k.NG, LAG, lambda at: rounds(at, lines + [(LAG, store)]))
                for b in range(2):
                    sp.wait_ge(stored[b], 16 * ((k.NG - b + 1) // 2))
                    if own_g:
                        sp.wait_ge(kept[b], 16 * ((k.NG - b + 1) // 2))

            @block.tensor
            def _(pe):
                def turns(g, h, b):
                    src_g.wait(pe, h, b)
                    need(pe, summed, g)
                    turn(nc, k, B[0], XS[b], s_turned)
                    if own_g:
                        own_g.wait(pe, h, b)
                    else:
                        pe.wait_ge(own_in[b], (h + 1) * 16)
                    need(pe, xdt, g)
                    turn(nc, k, B[1], XD[b], d_turned)

                def products(g, h, b):
                    need(pe, base, g)
                    pe.wait_ge(xdt, g + 1)
                    multiply_rows(nc, B[3], XDT[b], wr[:, :], b_mul)
                    need(pe, mixed, g)
                    pe.wait_ge(summed, g + 1)
                    multiply_rows(nc, B[2], AG[b], wl[:, :], a_mul)

                steps(pe, k.NG, LAG, lambda at: rounds(at, [(1, turns), (2, products)]))

            @block.scalar
            def _(act):
                def copy_own(g, h, b):
                    need(act, b_mul, g - 1)
                    act.wait_ge(d_turned, g + 1)
                    nc.scalar.activation(XDT[b][:, :], B[1][:, :], ACT.Copy).then_inc(xdt, 1)

                def relu(g, h, b):
                    if norm:
                        need(act, added, g - 1)
                    elif not (isinstance(h, int) and h <= 0):
                        act.wait_ge(stored[b], h * 16)
                    act.wait_ge(mixed, g + 1)
                    nc.scalar.activation(HR[b][:, :], MIX[b][:, :], ACT.Relu).then_inc(hr, 1)

                lines = [(1, copy_own), (2, relu)]
                if norm:
                    lines.append((3, lambda g, h, b: ln.root(act, k.eps[:, 0:1], g, b)))
                steps(act, k.NG, LAG, lambda at: rounds(at, lines))

            @block.vector
            def _(dve):
                v = nc.vector
                total = segment_sum(kit, k, dve, AG, [B[0]] * 2, s_turned, summed, lambda g: [(a_mul, g - 1)])

                def add_bias(g, h, b):
                    dve.wait_ge(b_mul, g + 1)
                    v.tensor_tensor(tiles(BASE[b]), tiles(B[3]), over(bias), ALU.add).then_inc(base, 1)

                def mix(g, h, b):
                    need(dve, hr, g - 1)
                    kit.hold("dve", dve, (base, g + 1), (a_mul, g + 1))
                    for j in range(G):
                        last = v.scalar_tensor_tensor(MIX[b][:, j * T:(j + 1) * T], B[2][:, j * T:(j + 1) * T],
                                                      k.rdeg[:, bass.ds(g * G + j, 1)], BASE[b][:, j * T:(j + 1) * T],
                                                      ALU.mult, ALU.add)
                    last.then_inc(mixed, 1)

                def add_x(g, h, b):
                    dve.wait_ge(x_in[b], (h + 1) * 16)
                    dve.wait_ge(hr, g + 1)
                    v.tensor_tensor(Y[b][:, :], HR[b][:, :], XR[b][:, :], ALU.add).then_inc(added, 1)
                    dve.wait_ge(added, g + 1)
                    ln.bn_moments(dve, tiles(Y[b]), g, b)

                def scale(g, h, b):
                    if not (isinstance(h, int) and h <= 0):
                        dve.wait_ge(stored[b], h * 16)
                    ln.scale(dve, tiles(OUT[b]), tiles(Y[b]), g, b)

                table = [[(1, total), (2, add_bias)], [(2, mix)]]
                if norm:
                    table = [[(1, total), (2, add_bias), (3, add_x)], [(2, mix), (3, scale)]]
                steps(dve, k.NG, LAG, lambda at: rounds(at, *table))


def gat_messages(kit, k):
    nc = kit.nc
    LAG = 3
    name = "ga"
    with ExitStack() as ctx:
        def pair(n):
            return [kit.sb(f"{name}_{n}{b}", [T, W], F32, ctx) for b in range(2)]

        XS, XD, DF, DFT, XDT, Z = (pair(n) for n in "XS XD DF DFT XDT Z".split())
        PART = [kit.sb(f"{name}_part{i}", [T, D], F32, ctx) for i in range(4)]
        B = [ctx.enter_context(nc.psum_tensor(f"{name}_bank{i}", [T, 512], F32)) for i in range(8)]
        src_g = Gather(kit, ctx, f"{name}_src", k.srcp_i, k.tab[1], XS)
        dst_g = Gather(kit, ctx, f"{name}_dst", k.dstp_i, k.tab[1], XD)
        diff, f_turned, d_turned, dft, xdt, s_mul, taken, z_mul, z0, z1, zed = (kit.sem(f"{name}_{n}") for n in (
            "diff", "f_turned", "d_turned", "dft", "xdt", "s_mul", "taken", "z_mul", "z0", "z1", "zed"))
        stored = [kit.sem(f"{name}_stored{b}") for b in range(2)]

        with nc.Block() as block:
            @block.gpsimd
            def _(pool):
                lines = [(0, src_g.stage(pool, lambda g, h, b: [(diff, g - 1)])),
                         (0, dst_g.stage(pool, lambda g, h, b: [(diff, g - 1), (d_turned, g - 1)]))]
                steps(pool, k.NG, LAG, lambda at: rounds(at, lines))

            @block.sync
            def _(sp):
                def store(g, h, b):
                    sp.wait_ge(zed, g * G + G)
                    sp.dma_start(edge_rows(k.messages, g, 0), tiles(Z[b])).then_inc(stored[b], 16)

                steps(sp, k.NG, LAG, lambda at: rounds(at, [(LAG, store)]))
                for b in range(2):
                    sp.wait_ge(stored[b], 16 * ((k.NG - b + 1) // 2))

            @block.tensor
            def _(pe):
                def turns(g, h, b):
                    dst_g.wait(pe, h, b)
                    need(pe, xdt, g)
                    turn(nc, k, B[1], XD[b], d_turned)
                    pe.wait_ge(diff, g + 1)
                    need(pe, dft, g)
                    turn(nc, k, B[0], DF[b], f_turned)

                def scores(g, h, b):
                    pe.wait_ge(dft, g + 1)
                    pe.wait_ge(xdt, g + 1)
                    need(pe, taken, g)
                    for j in range(G):
                        out, at = B[2][:, j * 2 * RH:(j + 1) * 2 * RH], slice(j * T, (j + 1) * T)
                        nc.tensor.matmul(out, XDT[b][:, at], k.score_w[:, 0, :], start=True, stop=False)
                        last = nc.tensor.matmul(out, DFT[b][:, at], k.score_w[:, 1, :], start=False, stop=True)
                    last.then_inc(s_mul, 1)

                def messages(g, h, b):
                    for j in range(G):
                        need(pe, zed, g * G + j - 3)
                        nc.tensor.matmul(B[3 + j][:, 0:R * D], DFT[b][:, j * T:(j + 1) * T],
                                         k.w_cat[:, :, :].rearrange("k r n -> k (r n)"),
                                         start=True, stop=True).then_inc(z_mul, 1)

                steps(pe, k.NG, LAG, lambda at: rounds(at, [(1, turns), (2, scores), (2, messages)]))

            @block.scalar
            def _(act):
                def copies(g, h, b):
                    need(act, s_mul, g - 1)
                    act.wait_ge(d_turned, g + 1)
                    nc.scalar.activation(XDT[b][:, :], B[1][:, :], ACT.Copy).then_inc(xdt, 1)
                    need(act, z_mul, (g - 1) * G)
                    act.wait_ge(f_turned, g + 1)
                    nc.scalar.activation(DFT[b][:, :], B[0][:, :], ACT.Copy).then_inc(dft, 1)

                def first(g, h, b):
                    for j in range(G):
                        n = g * G + j
                        kit.hold("act", act, (zed, n - 3), (z_mul, n + 1))
                        nc.scalar.activation(PART[j][:, :], B[3 + j][:, 0:D], ACT.Copy,
                                             scale=k.is_type[:, bass.ds(n, 1), 0]).then_inc(z0, 1)

                steps(act, k.NG, LAG, lambda at: rounds(at, [(1, copies), (2, first)]))

            @block.vector
            def _(dve):
                v = nc.vector

                def subtract(g, h, b):
                    need(dve, f_turned, g - 1)
                    src_g.wait(dve, h, b)
                    dst_g.wait(dve, h, b)
                    v.tensor_tensor(DF[b][:, :], XS[b][:, :], XD[b][:, :], ALU.subtract).then_inc(diff, 1)

                def take(g, h, b):
                    kit.hold("dve", dve, (s_mul, g + 1))
                    v.tensor_copy(k.scores[:, bass.ds(g * G, G), :],
                                  B[2][:, 0:G * 2 * RH].rearrange("p (j n) -> p j n", j=G)).then_inc(taken, 1)

                def select(g, h, b):
                    if not (isinstance(h, int) and h <= 0):
                        dve.wait_ge(stored[b], h * 16)
                    for j in range(G):
                        n = g * G + j
                        kit.hold("dve", dve, (z0, n + 1))
                        v.scalar_tensor_tensor(PART[j][:, :], B[3 + j][:, D:2 * D], k.is_type[:, bass.ds(n, 1), 1],
                                               PART[j][:, :], ALU.mult, ALU.add).then_inc(z1, 1)
                        kit.hold("dve", dve, (z1, n + 1))
                        v.scalar_tensor_tensor(Z[b][:, j * T:(j + 1) * T], B[3 + j][:, 2 * D:3 * D],
                                               k.is_type[:, bass.ds(n, 1), 2], PART[j][:, :],
                                               ALU.mult, ALU.add).then_inc(zed, 1)

                steps(dve, k.NG, LAG, lambda at: rounds(at, [(1, subtract), (2, take), (2, select)]))


def attention(kit, k, M):
    nc = kit.nc
    CH = M * T
    with ExitStack() as ctx:
        def sb(name, shape, dt=F32):
            return kit.sb(name, shape, dt, ctx)

        rel = sb("at_rel", [T, k.NT, RH])
        off = sb("at_off", [T, k.NT])
        by_tile = sb("at_by_tile", [T, M, CHUNKS, RH])
        score = sb("at_score", [Q, CH])
        work = sb("at_work", [Q, CH])
        peak = sb("at_peak", [Q, CH])
        last = sb("at_last", [Q, CH], BF16)
        psum = [ctx.enter_context(nc.psum_tensor(f"at{i}", [T, 512], F32)) for i in range(8)]
        sc = Scans(kit, k, ctx, "ats", psum[7])
        chain, turned, took, act_in, act_out, out_mul, out_took = Chain(kit, "at_chain"), *(
            kit.sem(f"at_{n}") for n in ("turned", "took", "act_in", "act_out", "out_mul", "out_took"))

        with nc.Block() as block:
            @block.vector
            def _(dve):
                v, link = nc.vector, chain.on(dve)
                s = k.scores[:, :, :].rearrange("p t n -> p (t n)")
                link(v.scalar_tensor_tensor(s, s, 0.2, s, ALU.mult, ALU.max))
                link(v.tensor_tensor(rel[:, :, :], k.scores[:, :, 0:RH], k.scores[:, :, RH:2 * RH], ALU.subtract))
                for r in range(R):
                    mask = k.is_type[:, :, r]
                    link(v.tensor_scalar(off[:, :], mask, MASKED, -MASKED, ALU.mult, ALU.add))
                    part = rel[:, :, r * H:(r + 1) * H]
                    link(v.tensor_tensor(part, part, across(mask), ALU.mult))
                    link(v.tensor_tensor(by_tile[:, :, :, r * H:(r + 1) * H].rearrange("p j c n -> p c j n"),
                                         part.rearrange("p (c j) n -> p c j n", c=CHUNKS),
                                         across(off[:, :]).rearrange("p (c j) n -> p c j n", c=CHUNKS), ALU.add))

        with nc.Block() as block:
            @block.tensor
            def _(pe):
                for n in range(M // 4):
                    need(pe, took, n - 1)
                    for j in range(4):
                        ins = nc.tensor.transpose(psum[n % 2][0:Q, j * T:(j + 1) * T], by_tile[:, 4 * n + j, :, :].rearrange("p c n -> p (c n)"),
                                                  k.ident[:, :])
                    ins.then_inc(turned, 1)

            @block.vector
            def _(dve):
                for n in range(M // 4):
                    dve.wait_ge(turned, n + 1)
                    nc.vector.tensor_copy(score[:, n * 512:(n + 1) * 512], psum[n % 2][0:Q, :]).then_inc(took, 1)

        with nc.Block() as block:
            @block.tensor
            def _(pe):
                for _ in range(4):
                    sc.pe_scan(pe)

            @block.scalar
            def _(act):
                act.wait_ge(act_in, 1)
                nc.scalar.activation(score[:, :], score[:, :], ACT.Exp).then_inc(act_out, 1)
                nc.scalar.activation(peak[:, :], peak[:, :], ACT.Exp, scale=-1.0).then_inc(act_out, 1)

            @block.vector
            def _(dve):
                v, link = nc.vector, chain.on(dve)
                link(v.tensor_scalar(last[:, :], k.next84[:, :], -1.0, 1.0, ALU.mult, ALU.add))
                sc.scan(dve, link, work, score[:, :], k.same84[:, :], k.prod_f[:, :], k.flow_f, ALU.max, True)
                link(v.tensor_scalar(work[:, :], work[:, :], 0.0, None, ALU.max))
                link(v.tensor_tensor(work[:, :], work[:, :], last[:, :], ALU.mult))
                sc.scan(dve, link, peak, work[:, :], k.next84[:, :], k.prod_b[:, :], k.flow_b, ALU.add, False)
                v.tensor_tensor(score[:, :], score[:, :], peak[:, :], ALU.subtract).then_inc(act_in, 1)
                dve.wait_ge(act_out, 2)
                sc.scan(dve, link, work, score[:, :], k.same84[:, :], k.prod_f[:, :], k.flow_f, ALU.add, True)
                link(v.tensor_tensor(work[:, :], work[:, :], peak[:, :], ALU.add))
                link(v.tensor_tensor(work[:, :], work[:, :], last[:, :], ALU.mult))
                sc.scan(dve, link, peak, work[:, :], k.next84[:, :], k.prod_b[:, :], k.flow_b, ALU.add, False)
                link(v.reciprocal(peak[:, :], peak[:, :]))
                link(v.tensor_tensor(score[:, :], score[:, :], peak[:, :], ALU.mult))

        with nc.Block() as block:
            @block.tensor
            def _(pe):
                for n in range(M // 4):
                    need(pe, out_took, n - 1)
                    for j in range(4):
                        t = 4 * n + j
                        ins = nc.tensor.matmul(psum[n % 2][:, j * CHUNKS * H:(j + 1) * CHUNKS * H],
                                               score[:, t * T:(t + 1) * T], k.head_w[:, :], start=True, stop=True)
                    ins.then_inc(out_mul, 1)

            @block.vector
            def _(dve):
                beta = k.beta[:, :, :].rearrange("p (c j) h -> p j c h", c=CHUNKS)
                for n in range(M // 4):
                    dve.wait_ge(out_mul, n + 1)
                    p = psum[n % 2][:, 0:4 * CHUNKS * H].rearrange("p (j c h) -> p j c h", j=4, h=H)
                    for j in range(4):
                        ins = nc.vector.tensor_copy(beta[:, 4 * n + j, :, :], p[:, j, :, :])
                    ins.then_inc(out_took, 1)


def across(ap):
    return ap.rearrange("p (t a) -> p t a", a=1).to_broadcast([ap.shape[0], ap.shape[1], H])


def gat_combine(kit, k):
    nc = kit.nc
    LAG = 4
    name = "gb"
    with ExitStack() as ctx:
        def pair(n):
            return [kit.sb(f"{name}_{n}{b}", [T, W], F32, ctx) for b in range(2)]

        Z, V, XD, XDT, AG, Y, YS, OUT, OUTN = (pair(n) for n in "Z V XD XDT AG Y YS OUT OUTN".split())
        B = [ctx.enter_context(nc.psum_tensor(f"{name}_bank{i}", [T, 512], F32)) for i in range(4)]
        ln = Norm(kit, ctx, f"{name}_ln")
        weighted, v_turned, d_turned, summed, xdt, mul, y, ys, y_turned, scaled = (kit.sem(f"{name}_{n}") for n in (
            "weighted", "v_turned", "d_turned", "summed", "xdt", "mul", "y", "ys", "y_turned", "scaled"))
        z_in, x_in, stored, stored_n = ([kit.sem(f"{name}_{n}{b}") for b in range(2)] for n in (
            "z_in", "x_in", "stored", "stored_n"))

        with nc.Block() as block:
            @block.sync
            def _(sp):
                def load(g, h, b):
                    need(sp, weighted, g - 1)
                    sp.dma_start(tiles(Z[b]), edge_rows(k.messages, g, 0)).then_inc(z_in[b], 16)
                    need(sp, d_turned, g - 1)
                    sp.dma_start(tiles(XD[b]), edge_rows(k.tab[1], g, k.N)).then_inc(x_in[b], 16)

                def store(g, h, b):
                    sp.wait_ge(ln.done, g + 1)
                    sp.dma_start(edge_rows(k.x_own, g, 0), tiles(OUT[b])).then_inc(stored[b], 16)
                    sp.wait_ge(scaled, g + 1)
                    sp.dma_start(edge_rows(k.tab[2], g, k.N), tiles(OUTN[b])).then_inc(stored_n[b], 16)

                steps(sp, k.NG, LAG, lambda at: rounds(at, [(0, load), (LAG, store)]))
                for b in range(2):
                    sp.wait_ge(stored[b], 16 * ((k.NG - b + 1) // 2))
                    sp.wait_ge(stored_n[b], 16 * ((k.NG - b + 1) // 2))

            @block.tensor
            def _(pe):
                def turns(g, h, b):
                    pe.wait_ge(x_in[b], (h + 1) * 16)
                    need(pe, xdt, g)
                    turn(nc, k, B[1], XD[b], d_turned)
                    pe.wait_ge(weighted, g + 1)
                    need(pe, summed, g)
                    turn(nc, k, B[0], V[b], v_turned)

                def product(g, h, b):
                    pe.wait_ge(xdt, g + 1)
                    need(pe, y, g)
                    nc.tensor.matmul(B[2][:, :], k.w_bar[:, :], XDT[b][:, :], start=True, stop=True).then_inc(mul, 1)

                def turn_y(g, h, b):
                    pe.wait_ge(ys, g + 1)
                    need(pe, ln.done, g)
                    turn(nc, k, B[3], YS[b], y_turned)

                steps(pe, k.NG, LAG, lambda at: rounds(at, [(1, turns), (2, product), (3, turn_y)]))

            @block.scalar
            def _(act):
                def copy_own(g, h, b):
                    need(act, y, g - 1)
                    act.wait_ge(d_turned, g + 1)
                    nc.scalar.activation(XDT[b][:, :], B[1][:, :], ACT.Copy).then_inc(xdt, 1)

                def scale_out(g, h, b):
                    if not (isinstance(h, int) and h <= 0):
                        act.wait_ge(stored_n[b], h * 16)
                    kit.hold("act", act, (ln.done, g + 1))
                    for j in range(G):
                        last = nc.scalar.activation(OUTN[b][:, j * T:(j + 1) * T], OUT[b][:, j * T:(j + 1) * T], ACT.Copy,
                                                    scale=k.norm[:, bass.ds(g * G + j, 1)])
                    last.then_inc(scaled, 1)

                steps(act, k.NG, LAG, lambda at: rounds(at, [
                    (1, copy_own), (3, lambda g, h, b: ln.root(act, k.eps[:, 0:1], g, b)), (4, scale_out)]))

            @block.vector
            def _(dve):
                v = nc.vector
                total = segment_sum(kit, k, dve, AG, [B[0]] * 2, v_turned, summed, lambda g: [(ys, g - 1)])

                def weigh(g, h, b):
                    need(dve, v_turned, g - 1)
                    kit.hold("dve", dve, (z_in[b], (h + 1) * 16))
                    beta = k.beta[:, bass.ds(g * G, G), :].rearrange("p t h -> p (t h)")
                    v.tensor_tensor(V[b][:, :].rearrange("p (q c) -> p q c", c=HD),
                                    Z[b][:, :].rearrange("p (q c) -> p q c", c=HD),
                                    beta.rearrange("p (q a) -> p q a", a=1).to_broadcast([T, G * H, HD]),
                                    ALU.mult).then_inc(weighted, 1)

                def add_own(g, h, b):
                    need(dve, ys, g - 1)
                    dve.wait_ge(mul, g + 1)
                    v.scalar_tensor_tensor(Y[b][:, :], B[2][:, :], k.bbar_col[:, 0:1], XDT[b][:, :],
                                           ALU.add, ALU.add).then_inc(y, 1)

                def add_sum(g, h, b):
                    need(dve, y_turned, g - 1)
                    dve.wait_ge(y, g + 1)
                    v.tensor_tensor(YS[b][:, :], Y[b][:, :], AG[b][:, :], ALU.add).then_inc(ys, 1)

                def measure(g, h, b):
                    dve.wait_ge(y_turned, g + 1)
                    ln.bn_moments(dve, tiles(B[3]), g, b)

                def scale(g, h, b):
                    if not (isinstance(h, int) and h <= 0):
                        dve.wait_ge(stored[b], h * 16)
                    need(dve, scaled, g - 1)
                    ln.scale(dve, tiles(OUT[b]), tiles(B[3]), g, b)

                steps(dve, k.NG, LAG, lambda at: rounds(
                    at, [(1, weigh), (2, add_own), (3, measure)], [(1, total), (2, add_sum), (3, scale)]))


def gcn(kit, k):
    nc = kit.nc
    LAG = 4
    name = "gc"
    with ExitStack() as ctx:
        def pair(n):
            return [kit.sb(f"{name}_{n}{b}", [T, W], F32, ctx) for b in range(2)]

        XS, AG, XR, BASE, MIX, OUT = (pair(n) for n in "XS AG XR BASE MIX OUT".split())
        B = [ctx.enter_context(nc.psum_tensor(f"{name}_bank{i}", [T, 512], F32)) for i in range(2)]
        ln = Norm(kit, ctx, f"{name}_ln")
        src_g = Gather(kit, ctx, f"{name}_src", k.srcp_i, k.tab[2], XS)
        turned, summed, mul, base, mixed = (kit.sem(f"{name}_{n}") for n in ("turned", "summed", "mul", "base", "mixed"))
        x_in, stored = ([kit.sem(f"{name}_{n}{b}") for b in range(2)] for n in ("x_in", "stored"))

        with nc.Block() as block:
            @block.gpsimd
            def _(pool):
                steps(pool, k.NG, LAG, lambda at: rounds(at, [(0, src_g.stage(pool, lambda g, h, b: [(turned, g - 1)]))]))

            @block.sync
            def _(sp):
                def load(g, h, b):
                    need(sp, base, g - 1)
                    sp.dma_start(tiles(XR[b]), edge_rows(k.x_own, g, 0)).then_inc(x_in[b], 16)

                def store(g, h, b):
                    sp.wait_ge(ln.done, g + 1)
                    sp.dma_start(edge_rows(k.tab[3], g, k.N), tiles(OUT[b])).then_inc(stored[b], 16)

                steps(sp, k.NG, LAG, lambda at: rounds(at, [(1, load), (LAG, store)]))
                for b in range(2):
                    sp.wait_ge(stored[b], 16 * ((k.NG - b + 1) // 2))

            @block.tensor
            def _(pe):
                def turn_s(g, h, b):
                    src_g.wait(pe, h, b)
                    need(pe, summed, g)
                    turn(nc, k, B[0], XS[b], turned)

                def product(g, h, b):
                    pe.wait_ge(summed, g + 1)
                    need(pe, mixed, g)
                    multiply_rows(nc, B[1], AG[b], k.w2[:, :], mul)

                steps(pe, k.NG, LAG, lambda at: rounds(at, [(1, turn_s), (2, product)]))

            @block.scalar
            def _(act):
                steps(act, k.NG, LAG, lambda at: rounds(at, [(3, lambda g, h, b: ln.root(act, k.eps[:, 0:1], g, b))]))

            @block.vector
            def _(dve):
                v = nc.vector
                total = segment_sum(kit, k, dve, AG, [B[0]] * 2, turned, summed, lambda g: [(mul, g - 1)])

                def add_bias(g, h, b):
                    dve.wait_ge(x_in[b], (h + 1) * 16)
                    v.tensor_tensor(tiles(BASE[b]), tiles(XR[b]), over(k.b2_row), ALU.add).then_inc(base, 1)

                def mix(g, h, b):
                    kit.hold("dve", dve, (base, g + 1), (mul, g + 1))
                    for j in range(G):
                        last = v.scalar_tensor_tensor(MIX[b][:, j * T:(j + 1) * T], B[1][:, j * T:(j + 1) * T],
                                                      k.norm[:, bass.ds(g * G + j, 1)], BASE[b][:, j * T:(j + 1) * T],
                                                      ALU.mult, ALU.add)
                    last.then_inc(mixed, 1)

                def measure(g, h, b):
                    dve.wait_ge(mixed, g + 1)
                    ln.bn_moments(dve, tiles(MIX[b]), g, b)

                def scale(g, h, b):
                    if not (isinstance(h, int) and h <= 0):
                        dve.wait_ge(stored[b], h * 16)
                    ln.scale(dve, tiles(OUT[b]), tiles(MIX[b]), g, b)

                steps(dve, k.NG, LAG, lambda at: rounds(
                    at, [(1, total), (2, add_bias), (3, measure)], [(2, mix), (3, scale)]))


def gin(kit, k, edge_attr, out, E):
    nc = kit.nc
    LAG = 6
    name = "gi"
    A = edge_attr.shape[1]
    with ExitStack() as ctx:
        def pair(n, shape=(T, W), dt=F32):
            return [kit.sb(f"{name}_{n}{b}", list(shape), dt, ctx) for b in range(2)]

        XS, MS, AG, XD, XDT, HT, MA, MB, T7, YT, OUT = (pair(n) for n in "XS MS AG XD XDT HT MA MB T7 YT OUT".split())
        ea_last = kit.sb(f"{name}_ea_last", [T, G, A], F32, ctx)
        EA, EAT, now = pair("EA", (T, G, A)), pair("EAT", (A, W)), pair("now", (T, G), I32)
        B = [ctx.enter_context(nc.psum_tensor(f"{name}_bank{i}", [T, 512], F32)) for i in range(8)]
        ln = Norm(kit, ctx, f"{name}_ln")
        src_g = Gather(kit, ctx, f"{name}_src", k.srcp_i, k.tab[3], XS)
        (e_clear, e_turned, eat, m_sum, ms, summed, d_turned, xdt, ht, ma_mul, mb_mul, ma, mb, out_mul, t7, yt, y_turned,
         staged) = (kit.sem(f"{name}_{n}") for n in (
             "e_clear e_turned eat m_sum ms summed d_turned xdt ht ma_mul mb_mul ma mb out_mul t7 yt y_turned staged"
         ).split())
        e_last = kit.sem(f"{name}_e_last")
        put = [kit.sem(f"{name}_put{b}", True) for b in range(2)]
        e_in, x_in = ([kit.sem(f"{name}_{n}{b}") for b in range(2)] for n in ("e_in", "x_in"))
        rest = E - (k.NG - 1) * W

        with nc.Block() as block:
            @block.gpsimd
            def _(pool):
                def put_rows(g, h, b):
                    waits = [(put[b], h * 16 * G)] if not (isinstance(h, int) and h <= 0) else []
                    kit.hold("pool", pool, *waits)
                    nc.gpsimd.tensor_copy(now[b][:, :], k.last_i[:, bass.ds(g * G, G)]).then_inc(staged, 1)
                    kit.hold("pool", pool, (staged, g + 1), (ln.done, g + 1))
                    for j in range(G):
                        pool.indirect_dma_start(out, bass.IndirectOffsetOnAxis(ap=now[b][:, j:j + 1], axis=0),
                                                OUT[b][:, j * T:(j + 1) * T], None, bounds_check=k.N - 1,
                                                oob_is_err=False).then_inc(put[b], 16)

                steps(pool, k.NG, LAG, lambda at: rounds(
                    at, [(0, src_g.stage(pool, lambda g, h, b: [(m_sum, g - 1)])), (LAG, put_rows)]))
                for b in range(2):
                    pool.wait_ge(put[b], 16 * G * ((k.NG - b + 1) // 2))

            @block.sync
            def _(sp):
                def load_e(g, h, b):
                    need(sp, e_turned, g - 1)
                    if isinstance(g, int) and g == k.NG - 1:
                        sp.wait_ge(e_clear, 1)
                        for j in range(-(-rest // T)):
                            n = min(T, rest - j * T)
                            sp.dma_start(ea_last[0:n, j, :], edge_attr[g * W + j * T:g * W + j * T + n, :]
                                         ).then_inc(e_last, 16)
                    else:
                        sp.dma_start(EA[b][:, :, :], edge_attr[bass.ds(g * W, W), :].rearrange(
                            "(j p) a -> p j a", p=T)).then_inc(e_in[b], 16)

                def load_x(g, h, b):
                    need(sp, d_turned, g - 1)
                    sp.dma_start(tiles(XD[b]), edge_rows(k.tab[3], g, k.N)).then_inc(x_in[b], 16)

                steps(sp, k.NG, LAG, lambda at: rounds(at, [(0, load_e), (1, load_x)]))

            @block.tensor
            def _(pe):
                def turn_e(g, h, b):
                    last_one = isinstance(g, int) and g == k.NG - 1
                    if last_one:
                        pe.wait_ge(e_last, 16 * -(-rest // T))
                    else:
                        pe.wait_ge(e_in[b], (h + 1) * 16)
                    rows = ea_last if last_one else EA[b]
                    need(pe, eat, g)
                    for j in range(G):
                        last = nc.tensor.transpose(B[0][0:A, j * T:(j + 1) * T], rows[:, j, :], k.ident[:, :])
                    last.then_inc(e_turned, 1)

                def message(g, h, b):
                    src_g.wait(pe, h, b)
                    pe.wait_ge(eat, g + 1)
                    need(pe, ms, g)
                    for j in range(G):
                        at = slice(j * T, (j + 1) * T)
                        nc.tensor.matmul(B[1][:, at], k.we[:, :], EAT[b][:, at], start=True, stop=False)
                        last = nc.tensor.matmul(B[1][:, at], XS[b][:, at], k.ident[:, :], start=False, stop=True)
                    last.then_inc(m_sum, 1)

                def turn_x(g, h, b):
                    pe.wait_ge(x_in[b], (h + 1) * 16)
                    need(pe, xdt, g)
                    turn(nc, k, B[2], XD[b], d_turned)

                def hidden(g, h, b):
                    pe.wait_ge(ht, g + 1)
                    need(pe, ma, g)
                    nc.tensor.matmul(B[3][:, :], k.wm1[:, 0:D], HT[b][:, :], start=True, stop=True).then_inc(ma_mul, 1)
                    need(pe, mb, g)
                    nc.tensor.matmul(B[4][:, :], k.wm1[:, D:2 * D], HT[b][:, :], start=True, stop=True).then_inc(mb_mul, 1)

                def project(g, h, b):
                    pe.wait_ge(mb, g + 1)
                    need(pe, t7, g)
                    nc.tensor.matmul(B[5][:, :], k.wm2[:, 0, :], MA[b][:, :], start=True, stop=False)
                    nc.tensor.matmul(B[5][:, :], k.wm2[:, 1, :], MB[b][:, :], start=False, stop=True).then_inc(out_mul, 1)

                def turn_y(g, h, b):
                    pe.wait_ge(yt, g + 1)
                    need(pe, ln.done, g)
                    turn(nc, k, B[6], YT[b], y_turned)

                steps(pe, k.NG, LAG, lambda at: rounds(at, [
                    (1, turn_e), (4, project), (2, turn_x), (3, hidden), (5, turn_y)], [(1, message)]))

            @block.scalar
            def _(act):
                def turned_e(g, h, b):
                    need(act, m_sum, g - 1)
                    act.wait_ge(e_turned, g + 1)
                    nc.scalar.activation(EAT[b][:, :], B[0][0:A, :], ACT.Copy).then_inc(eat, 1)

                def relu_message(g, h, b):
                    need(act, summed, g - 1)
                    act.wait_ge(m_sum, g + 1)
                    nc.scalar.activation(MS[b][:, :], B[1][:, :], ACT.Relu, bias=k.be_col[:, 0:1]).then_inc(ms, 1)

                def copy_x(g, h, b):
                    need(act, yt, g - 1)
                    act.wait_ge(d_turned, g + 1)
                    nc.scalar.activation(XDT[b][:, :], B[2][:, :], ACT.Copy).then_inc(xdt, 1)

                def relu_hidden(g, h, b):
                    need(act, out_mul, g - 1)
                    for i, (m, mul, done) in enumerate(((MA, ma_mul, ma), (MB, mb_mul, mb))):
                        act.wait_ge(mul, g + 1)
                        nc.scalar.activation(m[b][:, :], B[3 + i][:, :], ACT.Relu, bias=k.bn1_b[:, i:i + 1],
                                             scale=k.bn1_s[:, i:i + 1]).then_inc(done, 1)

                def affine(g, h, b):
                    need(act, yt, g - 1)
                    act.wait_ge(out_mul, g + 1)
                    nc.scalar.activation(T7[b][:, :], B[5][:, :], ACT.Identity, bias=k.bn2_b[:, 0:1],
                                         scale=k.bn2_s[:, 0:1]).then_inc(t7, 1)

                steps(act, k.NG, LAG, lambda at: rounds(at, [
                    (1, turned_e), (4, affine), (2, copy_x), (3, relu_hidden),
                    (5, lambda g, h, b: ln.root(act, k.eps[:, 0:1], g, b))], [(1, relu_message)]))

            @block.vector
            def _(dve):
                v = nc.vector
                total = segment_sum(kit, k, dve, AG, MS, ms, summed, lambda g: [(ht, g - 1)])
                v.memset(ea_last[:, :, :], 0.0).then_inc(e_clear, 1)

                def own(g, h, b):
                    need(dve, mb_mul, g - 1)
                    dve.wait_ge(xdt, g + 1)
                    dve.wait_ge(summed, g + 1)
                    v.scalar_tensor_tensor(HT[b][:, :], XDT[b][:, :], k.eps1[:, 0:1], AG[b][:, :],
                                           ALU.mult, ALU.add).then_inc(ht, 1)

                def add_x(g, h, b):
                    need(dve, y_turned, g - 1)
                    dve.wait_ge(t7, g + 1)
                    v.tensor_tensor(YT[b][:, :], T7[b][:, :], XDT[b][:, :], ALU.add).then_inc(yt, 1)

                def measure(g, h, b):
                    dve.wait_ge(y_turned, g + 1)
                    ln.bn_moments(dve, tiles(B[6]), g, b)

                def scale(g, h, b):
                    if not (isinstance(h, int) and h <= 0):
                        dve.wait_ge(put[b], h * 16 * G)
                    ln.scale(dve, tiles(OUT[b]), tiles(B[6]), g, b)

                steps(dve, k.NG, LAG, lambda at: rounds(
                    at, [(4, add_x), (5, measure)], [(2, own), (5, scale)], [(1, total)]))


class Tensors:
    pass


def gnn(nc, x, src, dst, edge_attr, edge_type, ins, out, place, tabs, x_own, messages):
    N, E = x.shape[0], src.shape[0]
    M = 4 * -(-E // (CHUNKS * G * T))
    with ExitStack() as ctx:
        kit = Kit(nc, ctx)
        k = Tensors()
        k.N, k.NT = N, CHUNKS * M
        k.NG = k.NT // G
        k.place, k.tab, k.x_own, k.messages = place, tabs, x_own, messages
        CH = M * T
        sb = kit.sb
        k.eps, k.one, k.eps1 = sb("eps", [T, 1]), sb("one", [T, 1]), sb("eps1", [T, 1])
        k.ident = sb("ident", [T, T])
        k.chunk_of = sb("chunk_of", [CHUNKS, Q])
        k.one_chunk = sb("one_chunk", [CHUNKS, CHUNKS, T])
        k.head_sel = sb("head_sel", [Q, R, CHUNKS, H])
        k.head_w = sb("head_w", [Q, CHUNKS * H])
        k.rel = sb("rel", [T, R])
        k.wl1, k.wr1, k.wl2, k.wr2, k.w2, k.w_bar = (sb(n, [D, D]) for n in "wl1 wr1 wl2 wr2 w2 w_bar".split())
        k.w_cat, k.wm1, k.wm2 = sb("w_cat", [D, R, D]), sb("wm1", [D, 2 * D]), sb("wm2", [D, 2, D])
        k.we = sb("we", [16, D])
        k.score_w = sb("score_w", [D, 2, 2 * RH])
        k.bl1_row, k.bl2_row, k.b2_row = (sb(n, [T, D]) for n in "bl1_row bl2_row b2_row".split())
        k.bl1_col, k.bl2_col, k.bbar_col, k.be_col, k.bn2_s, k.bn2_b = (
            sb(n, [D, 1]) for n in "bl1_col bl2_col bbar_col be_col bn2_s bn2_b".split())
        k.bn1_s, k.bn1_b, k.bn1_s_own = (sb(n, [D, 2]) for n in "bn1_s bn1_b bn1_s_own".split())
        k.src_i, k.dst_i, k.last_i, k.srcp_i, k.dstp_i, k.edge_row = (
            sb(n, [T, k.NT], I32) for n in "src_i dst_i last_i srcp_i dstp_i edge_row".split())
        k.type_f, k.deg, k.rdeg, k.norm = (sb(n, [T, k.NT]) for n in "type_f deg rdeg norm".split())
        k.is_type = sb("is_type", [T, k.NT, R])
        k.same = sb("same", [T, k.NT * T], BF16)
        k.same84, k.next84, k.prod_f, k.prod_b = (sb(n, [Q, CH], BF16) for n in "same84 next84 prod_f prod_b".split())
        k.flow_f, k.flow_b = (sb(n, [1, RH, CHUNKS]) for n in "flow_f flow_b".split())
        kit.place_clear = kit.sem("place_clear", True)

        prepare(kit, k, ins)
        kit.end_phase()
        index_stage(kit, k, src, dst, edge_type, N, E, M)
        kit.end_phase()
        dense_pass(kit, k, x, out)
        kit.end_phase()
        sage(kit, k, "s1", x, k.src_i, k.dst_i, None, x_own, (k.wl1, k.wr1, k.bl1_row), tabs[0], False)
        kit.end_phase()
        sage(kit, k, "s2", tabs[0], k.srcp_i, None, tabs[0], x_own, (k.wl2, k.wr2, k.bl2_row), tabs[1], True)
        kit.end_phase()
        with ExitStack() as gat:
            k.scores = sb("scores", [T, k.NT, 2 * RH], F32, gat)
            k.beta = sb("beta", [T, k.NT, H], F32, gat)
            gat_messages(kit, k)
            kit.end_phase()
            attention(kit, k, M)
            kit.end_phase()
            gat_combine(kit, k)
            kit.end_phase()
        gcn(kit, k)
        kit.end_phase()
        gin(kit, k, edge_attr, out, E)


_DATA = ("x", "src", "dst", "edge_attr_16", "edge_type_3")


def kernel(**inputs):
    import numpy as np
    import concourse.bacc as bacc
    from concourse.bass_utils import run_bass_kernel_spmd as run

    nc = bacc.Bacc("TRN2", target_bir_lowering=False, num_devices=1)
    arrays = {name: np.ascontiguousarray(a) for name, a in inputs.items()}
    args = {name: nc.dram_tensor(name, a.shape, mybir.dt.from_np(a.dtype), kind="ExternalInput").ap()
            for name, a in arrays.items()}
    N, E = arrays["x"].shape[0], arrays["src"].shape[0]
    EP = CHUNKS * G * T * -(-E // (CHUNKS * G * T))
    out = nc.dram_tensor("out", (N, D), F32, kind="ExternalOutput").ap()
    place = nc.dram_tensor("place", (N, 1), I32).ap()
    tabs = [nc.dram_tensor(f"tab{i}", (N + EP, D), F32).ap() for i in range(4)]
    x_own = nc.dram_tensor("x_own", (EP, D), F32).ap()
    messages = nc.dram_tensor("messages", (EP, D), F32).ap()
    gnn(nc, *(args[n] for n in _DATA), {n: a for n, a in args.items() if n not in _DATA}, out, place, tabs,
        x_own, messages)
    return run(nc, [arrays], core_ids=[0]).results[0]["out"]
```

```python
from contextlib import ExitStack

import concourse.bass as bass
from concourse import mybir

F32 = mybir.dt.float32
I32 = mybir.dt.int32
BF16 = mybir.dt.bfloat16
ALU = mybir.AluOpType
ACT = mybir.ActivationFunctionType
AX_X = mybir.AxisListType.X

D = 128
T = 128
G = 4
W = G * T
CHUNKS = 7
R, H = 3, 4
RH = R * H
HD = D // H
Q = CHUNKS * RH
FAR = float(1 << 20)
MASKED = 1.0e9
LN_EPS = 1e-5
BN_EPS = 1e-3


def steps(eng, groups, lag, body):
    def fixed(s):
        def at(k):
            g = s - k
            return (g, g // 2, g % 2) if 0 <= g < groups else None
        return at

    first = lag + 2 + (lag % 2)
    pairs = (groups - 1 - first) // 2
    if pairs < 2:
        for s in range(groups + lag):
            body(fixed(s))
        return
    for s in range(first):
        body(fixed(s))
    with eng.Fori(0, pairs) as i:
        for u in range(2):
            def at(k, u=u):
                c = first + u - k
                return i * 2 + c, i + c // 2, c % 2
            body(at)
    for s in range(first + 2 * pairs, groups + lag):
        body(fixed(s))


def rounds(at, *table):
    for line in table:
        for lag, stage in line:
            g = at(lag)
            if g is not None:
                stage(*g)


class Kit:

    def __init__(self, nc, ctx):
        self.nc, self.ctx = nc, ctx
        self.passing = []
        self.held = {n: ctx.enter_context(nc.semaphore(f"held_{n}")) for n in ("pe", "act", "dve", "pool", "sp")}

    def sb(self, name, shape, dt=F32, ctx=None):
        return (ctx or self.ctx).enter_context(self.nc.sbuf_tensor(name, shape, dt))

    def sem(self, name, lasting=False):
        if lasting:
            return self.ctx.enter_context(self.nc.semaphore(name))
        self.passing.append(self.nc.alloc_semaphore(name=name))
        return self.passing[-1]

    def end_phase(self):
        sems, self.passing = self.passing, []
        with self.nc.Block() as block:
            @block.gpsimd
            def _(pool):
                self.nc.clear_and_free_semaphores(sems)

    def hold(self, name, eng, *waits):
        for sem, value in waits:
            if isinstance(value, int) and value <= 0:
                continue
            eng.wait_ge(sem, value)
            if not isinstance(value, int):
                eng.sem_inc(self.held[name], 1)


def need(eng, sem, value):
    if not (isinstance(value, int) and value <= 0):
        eng.wait_ge(sem, value)


class Norm:

    def __init__(self, kit, ctx, name):
        nc = kit.nc
        self.kit, self.name = kit, name
        self.stats = kit.sb(f"{name}_stats", [T, G, 6], ctx=ctx)
        self.mv = [kit.sb(f"{name}_mv{b}", [T, G, 2], ctx=ctx) for b in range(2)]
        self.std = [kit.sb(f"{name}_std{b}", [T, G], ctx=ctx) for b in range(2)]
        self.rstd, self.shift = ([kit.sb(f"{name}_{n}{b}", [T, G], ctx=ctx) for b in range(2)] for n in ("rstd", "shift"))
        self.counted = kit.sem(f"{name}_counted")
        self.moments = kit.sem(f"{name}_moments")
        self.rooted = kit.sem(f"{name}_rooted")
        self.inverted = kit.sem(f"{name}_inverted")
        self.done = kit.sem(f"{name}_done")

    def bn_moments(self, dve, x, g, b):
        nc = self.kit.nc
        need(dve, self.moments, g)
        need(dve, self.inverted, 2 * g - 2)
        for j in range(G):
            last = nc.vector.bn_stats(self.stats[:, j, :], x[:, j, :])
        last.then_inc(self.counted, 1)
        self.kit.hold("dve", dve, (self.counted, g + 1))
        for j in range(G):
            last = nc.vector.bn_aggr(self.mv[b][:, j, :], self.stats[:, j, :])
        last.then_inc(self.moments, 1)

    def root(self, act, eps, g, b):
        act.wait_ge(self.moments, g + 1)
        self.kit.nc.scalar.activation(self.std[b][:, :], self.mv[b][:, :, 1], ACT.Sqrt,
                                      bias=eps).then_inc(self.rooted, 1)

    def invert(self, dve, g, b):
        nc = self.kit.nc
        need(dve, self.done, g - 1)
        dve.wait_ge(self.rooted, g + 1)
        nc.vector.reciprocal(self.rstd[b][:, :], self.std[b][:, :]).then_inc(self.inverted, 1)
        dve.wait_ge(self.inverted, 2 * g + 1)
        nc.vector.scalar_tensor_tensor(self.shift[b][:, :], self.mv[b][:, :, 0], -1.0, self.rstd[b][:, :],
                                       ALU.mult, ALU.mult).then_inc(self.inverted, 1)

    def scale(self, act, out, x, g, b):
        act.wait_ge(self.inverted, 2 * g + 2)
        for j in range(G):
            last = self.kit.nc.scalar.activation(out[:, j, :], x[:, j, :], ACT.Identity, bias=self.shift[b][:, j:j + 1],
                                                 scale=self.rstd[b][:, j:j + 1])
        last.then_inc(self.done, 1)


def tiles(buf):
    return buf[:, :].rearrange("p (j d) -> p j d", j=G)


def prepare(kit, k, ins):
    nc = kit.nc
    with ExitStack() as ctx:
        def sb(name, shape, dt=F32):
            return kit.sb(name, shape, dt, ctx)

        W = sb("w_cat_loose", [D, R, D])
        att = sb("att", [T, 2, R * D])
        prod = sb("att_prod", [T, R, D])
        a_dst = sb("a_dst", [D, RH])
        bias_r = sb("bias_r", [R, D])
        we1 = sb("we1", [16, 2 * D])
        we1t = sb("we1t", [D, 2, 16])
        we2 = sb("we2", [D, 2, D])
        be1 = sb("be1", [D, 2])
        be2 = sb("be2", [D, 1])
        relw = sb("relw", [T, R])
        relw3 = sb("relw3", [R, D])
        mix = sb("mix", [D, 3, D])
        sums = sb("sums", [T, 2])
        tmp = sb("tmp", [T, 16])
        colm = sb("colm", [D, 6, 2])
        row2 = sb("row2", [T, 6, D])
        P0 = ctx.enter_context(nc.psum_tensor("prep0", [T, 512], F32))
        P1 = ctx.enter_context(nc.psum_tensor("prep1", [T, 512], F32))
        P2 = ctx.enter_context(nc.psum_tensor("prep2", [T, 512], F32))
        loaded, made, chain, turned, folded, rooted, masks = (kit.sem(f"prep_{n}") for n in (
            "loaded", "made", "chain", "turned", "folded", "rooted", "masks"))
        loads = []

        def col(ap):
            return ap.rearrange("(p a) -> p a", a=1)

        def bcast(ap, n):
            return ap.rearrange("(a n) -> a n", a=1).to_broadcast([T, n])

        loads += [(k.wl1, ins["L0_gnn_Wl1"]), (k.wr1, ins["L0_gnn_Wr1"]), (k.wl2, ins["L0_gnn_Wl2"]),
                  (k.wr2, ins["L0_gnn_Wr2"]), (k.w2, ins["L2_gnn_weight"]), (k.wm1, ins["L3_gnn_Wm1"]),
                  (we1, ins["L3_gnn_We1"])]
        loads = [(a[:, :], b) for a, b in loads]
        loads += [(W[:, :, :], ins["L1_gnn_W"].rearrange("r k n -> k r n")),
                  (k.wm2[:, :, :], ins["L3_gnn_Wm2"].rearrange("(a k) n -> k a n", a=2)),
                  (we2[:, :, :], ins["L3_gnn_We2"].rearrange("(a k) n -> k a n", a=2)),
                  (bias_r[:, :], ins["L1_gnn_bias"]),
                  (relw[:, :], bcast(ins["L1_gnn_rel_w"], R)),
                  (k.eps1[:, :], bcast(ins["L3_gnn_eps"], 1)),
                  (k.bl1_col[:, :], col(ins["L0_gnn_bl1"])), (k.bl2_col[:, :], col(ins["L0_gnn_bl2"])),
                  (be2[:, :], col(ins["L3_gnn_be2"])),
                  (be1[:, :], ins["L3_gnn_be1"].rearrange("(a p) -> p a", a=2)),
                  (k.bl1_row[:, :], bcast(ins["L0_gnn_bl1"], D)), (k.bl2_row[:, :], bcast(ins["L0_gnn_bl2"], D)),
                  (k.b2_row[:, :], bcast(ins["L2_gnn_bias"], D)),
                  (att[:, 0, :], bcast(ins["L1_gnn_att_src"].rearrange("r h c -> (r h c)"), R * D)),
                  (att[:, 1, :], bcast(ins["L1_gnn_att_dst"].rearrange("r h c -> (r h c)"), R * D))]
        for n, name in enumerate(("bm1", "g1", "b1", "m1", "v1")):
            loads.append((colm[:, n, :], ins[f"L3_gnn_{name}"].rearrange("(a p) -> p a", a=2)))
        for n, name in enumerate(("bm2", "g2", "b2", "m2", "v2")):
            loads.append((row2[:, n, :], bcast(ins[f"L3_gnn_{name}"], D)))

        with nc.Block() as block:
            @block.sync
            def _(sp):
                with nc.allow_non_contiguous_dma(reason="per-feature vectors, one value to a partition"):
                    for dst, src in loads:
                        sp.dma_start(dst, src).then_inc(loaded, 16)
                sp.wait_ge(loaded, 16 * len(loads))

            @block.gpsimd
            def _(pool):
                nc.gpsimd.memset(k.ident[:, :], 0.0).then_inc(masks, 1)
                nc.gpsimd.memset(k.chunk_of[:, :], 1.0).then_inc(masks, 1)
                nc.gpsimd.memset(k.one_chunk[:, :, :], 0.0).then_inc(masks, 1)
                nc.gpsimd.memset(k.head_sel[:, :, :, :], 0.0).then_inc(masks, 1)
                pool.wait_ge(masks, 4)
                nc.gpsimd.affine_select(out=k.ident[:, :], in_=k.ident[:, :], compare_op=ALU.not_equal, fill=1.0,
                                        base=0, pattern=[[-1, T]], channel_multiplier=1).then_inc(made, 1)
                nc.gpsimd.affine_select(out=k.chunk_of[:, :], in_=k.chunk_of[:, :], compare_op=ALU.is_ge, fill=0.0,
                                        base=0, pattern=[[1, Q]], channel_multiplier=-RH).then_inc(masks, 1)
                pool.wait_ge(masks, 5)
                nc.gpsimd.affine_select(out=k.chunk_of[:, :], in_=k.chunk_of[:, :], compare_op=ALU.is_ge, fill=0.0,
                                        base=RH - 1, pattern=[[-1, Q]], channel_multiplier=RH).then_inc(made, 1)
                nc.gpsimd.affine_select(out=k.one_chunk[:, :, :], in_=k.one_chunk[:, :, :],
                                        compare_op=ALU.not_equal, fill=1.0, base=0,
                                        pattern=[[-1, CHUNKS], [0, T]], channel_multiplier=1).then_inc(made, 1)
                for r in range(R):
                    nc.gpsimd.affine_select(out=k.head_sel[:, r, :, :], in_=k.head_sel[:, r, :, :],
                                            compare_op=ALU.not_equal, fill=1.0, base=-H * r,
                                            pattern=[[-RH, CHUNKS], [-1, H]], channel_multiplier=1).then_inc(made, 1)

            @block.scalar
            def _(act):
                act.wait_ge(folded, 1)
                nc.scalar.activation(tmp[:, 0:R], tmp[:, 4:4 + R], ACT.Exp).then_inc(rooted, 1)
                act.wait_ge(folded, 2)
                nc.scalar.activation(colm[:, 5, :], colm[:, 4, :], ACT.Sqrt).then_inc(rooted, 1)
                nc.scalar.activation(row2[:, 5, :], row2[:, 4, :], ACT.Sqrt).then_inc(rooted, 1)

            @block.tensor
            def _(pe):
                pe.wait_ge(loaded, 16 * len(loads))
                pe.wait_ge(made, 3 + R)
                for a in range(2):
                    last = nc.tensor.transpose(P0[:, 16 * a:16 * a + 16], we1[:, a * D:(a + 1) * D],
                                               k.ident[0:16, 0:16])
                last.then_inc(turned, 1)
                pe.wait_ge(folded, 3)
                for a in range(2):
                    nc.tensor.matmul(P1[0:16, 0:D], we1t[:, a, :], we2[:, a, :], start=a == 0, stop=a == 1)
                for a in range(2):
                    last = nc.tensor.matmul(P2[:, 0:1], we2[:, a, :], be1[:, a:a + 1], start=a == 0, stop=a == 1)
                last.then_inc(turned, 1)
                pe.wait_ge(folded, 4)
                nc.tensor.matmul(P0[:, 64:64 + D], relw3[:, :], bias_r[:, :], start=True, stop=True)
                nc.tensor.matmul(P0[:, 256:256 + D], k.centre[:, :], mix[:, 0, :], start=True, stop=True)
                nc.tensor.transpose(P0[:, 384:384 + D], mix[:, 0, :], k.ident[:, :]).then_inc(turned, 1)
                pe.wait_ge(folded, 5)
                nc.tensor.transpose(P1[:, 0:D], mix[:, 1, :], k.ident[:, :])
                nc.tensor.matmul(P1[:, D:2 * D], mix[:, 2, :], k.centre[:, :], start=True, stop=True).then_inc(turned, 1)
                pe.wait_ge(folded, 6)
                nc.tensor.matmul(P1[:, 2 * D:3 * D], mix[:, 0, :], k.centre[:, :], start=True, stop=True).then_inc(turned, 1)

            @block.vector
            def _(dve):
                count = [0]

                def link(ins):
                    count[0] += 1
                    ins.then_inc(chain, 1)
                    dve.wait_ge(chain, count[0])

                link(nc.vector.memset(k.eps[:, :], LN_EPS))
                link(nc.vector.memset(k.one[:, :], 1.0))
                dve.wait_ge(loaded, 16 * len(loads))
                link(nc.vector.reduce_max(tmp[:, 3:4], relw[:, :], AX_X))
                nc.vector.tensor_scalar(tmp[:, 4:4 + R], relw[:, :], tmp[:, 3:4], None,
                                        ALU.subtract).then_inc(folded, 1)
                dve.wait_ge(rooted, 1)
                link(nc.vector.reduce_sum(tmp[:, 8:9], tmp[:, 0:R], AX_X))
                link(nc.vector.reciprocal(tmp[:, 9:10], tmp[:, 8:9]))
                link(nc.vector.tensor_scalar(k.rel[:, :], tmp[:, 0:R], tmp[:, 9:10], None, ALU.mult))
                link(nc.vector.tensor_scalar(colm[:, 4, :], colm[:, 4, :], BN_EPS, None, ALU.add))
                nc.vector.tensor_scalar(row2[:, 4, :], row2[:, 4, :], BN_EPS, None, ALU.add).then_inc(folded, 1)
                link(nc.vector.tensor_copy(k.w_cat[:, 0:R * D].rearrange("k (r n) -> k r n", r=R), W[:, :, :]))
                link(nc.vector.tensor_scalar(k.w_bar[:, :], W[:, 0, :], k.rel[:, 0:1], None, ALU.mult))
                for r in range(1, R):
                    link(nc.vector.scalar_tensor_tensor(k.w_bar[:, :], W[:, r, :], k.rel[:, r:r + 1],
                                                        k.w_bar[:, :], ALU.mult, ALU.add))
                a_src = k.w_cat[:, R * D:R * D + RH]
                for s, out in ((0, a_src), (1, a_dst[:, :])):
                    link(nc.vector.tensor_tensor(prod[:, :, :], W[:, :, :],
                                                 att[:, s, :].rearrange("p (r d) -> p r d", r=R), ALU.mult))
                    link(nc.vector.reduce_sum(out, prod[:, :, :].rearrange("p r (h c) -> p (r h) c", h=H), AX_X))
                link(nc.vector.tensor_tensor(k.self_w[:, :], a_src, a_dst[:, :], ALU.add))
                dve.wait_ge(turned, 1)
                nc.vector.tensor_copy(we1t[:, :, :], P0[:, 0:32].rearrange("p (a n) -> p a n", a=2)).then_inc(folded, 1)
                dve.wait_ge(turned, 2)
                link(nc.vector.tensor_copy(k.we[:, :], P1[0:16, 0:D]))
                link(nc.vector.tensor_tensor(k.be_col[:, :], P2[:, 0:1], be2[:, :], ALU.add))
                dve.wait_ge(made, 3 + R)
                link(nc.vector.tensor_tensor(tmp[0:R, 12:12 + R], k.rel[0:R, :], k.ident[0:R, 0:R], ALU.mult))
                link(nc.vector.reduce_sum(tmp[0:R, 15:16], tmp[0:R, 12:12 + R], AX_X))
                link(nc.vector.memset(relw3[:, :], 1.0))
                link(nc.vector.tensor_scalar(relw3[:, :], relw3[:, :], tmp[0:R, 15:16], None, ALU.mult))
                link(nc.vector.tensor_scalar(k.centre[:, :], k.ident[:, :], -1.0 / D, None, ALU.add))
                link(nc.vector.tensor_tensor(mix[:, 0, :], k.ident[:, :], k.w_bar[:, :], ALU.add))
                for rows, n in ((k.b2_row, T), (bias_r, R)):
                    link(nc.vector.reduce_sum(sums[0:n, 0:1], rows[:, :], AX_X))
                    link(nc.vector.tensor_scalar(sums[0:n, 1:2], sums[0:n, 0:1], -1.0 / D, None, ALU.mult))
                    ins = nc.vector.tensor_scalar(rows[:, :], rows[:, :], sums[0:n, 1:2], None, ALU.add)
                    if rows is k.b2_row:
                        link(ins)
                ins.then_inc(folded, 1)
                dve.wait_ge(turned, 3)
                link(nc.vector.tensor_copy(k.bbar_row[:, :], P0[:, 64:64 + D]))
                link(nc.vector.tensor_copy(mix[:, 1, :], P0[:, 256:256 + D]))
                nc.vector.tensor_copy(mix[:, 2, :], P0[:, 384:384 + D]).then_inc(folded, 1)
                dve.wait_ge(turned, 4)
                link(nc.vector.tensor_copy(k.own_mix[:, :], P1[:, D:2 * D]))
                nc.vector.tensor_copy(mix[:, 0, :], P1[:, 0:D]).then_inc(folded, 1)
                dve.wait_ge(turned, 5)
                link(nc.vector.tensor_copy(k.pair_mix[:, D:2 * D], P1[:, 2 * D:3 * D]))
                link(nc.vector.tensor_copy(k.pair_mix[:, 0:D], k.centre[:, :]))
                hw = k.head_w[:, :].rearrange("q (c h) -> q c h", h=H)
                link(nc.vector.tensor_scalar(hw, k.head_sel[:, 0, :, :], k.rel[0:Q, 0:1], None, ALU.mult))
                for r in range(1, R):
                    link(nc.vector.scalar_tensor_tensor(hw, k.head_sel[:, r, :, :], k.rel[0:Q, r:r + 1], hw,
                                                        ALU.mult, ALU.add))
                dve.wait_ge(rooted, 3)
                link(nc.vector.tensor_scalar(k.eps1[:, :], k.eps1[:, :], 1.0, None, ALU.add))
                for cc, scale, bias in ((lambda n: colm[:, n, :], k.bn1_s[:, :], k.bn1_b[:, :]),
                                        (lambda n: row2[:, n, :], row2[:, 1, :], k.bn2_row[:, :])):
                    link(nc.vector.reciprocal(cc(5), cc(5)))
                    link(nc.vector.tensor_tensor(scale, cc(5), cc(1), ALU.mult))
                    link(nc.vector.tensor_tensor(cc(0), cc(0), cc(3), ALU.subtract))
                    link(nc.vector.tensor_tensor(cc(0), cc(0), scale, ALU.mult))
                    link(nc.vector.tensor_tensor(bias, cc(0), cc(2), ALU.add))
                for a in range(2):
                    link(nc.vector.tensor_tensor(k.wm2[:, a, :], k.wm2[:, a, :], row2[:, 1, :], ALU.mult))
                for rows in (k.w2[:, :], k.wm2[:, 0, :], k.wm2[:, 1, :], k.bn2_row[:, :]):
                    link(nc.vector.reduce_sum(sums[:, 0:1], rows, AX_X))
                    link(nc.vector.tensor_scalar(sums[:, 1:2], sums[:, 0:1], -1.0 / D, None, ALU.mult))
                    link(nc.vector.tensor_scalar(rows, rows, sums[:, 1:2], None, ALU.add))
                link(nc.vector.tensor_scalar(k.bn1_s_own[:, :], k.bn1_s[:, :], k.eps1[:, 0:1], None, ALU.mult))


class Scans:

    def __init__(self, kit, k, ctx, name, psum):
        self.kit, self.k, self.nc = kit, k, kit.nc
        self.row = kit.sb(f"{name}_row", [1, RH, CHUNKS], ctx=ctx)
        self.into = kit.sb(f"{name}_into", [1, CHUNKS, RH], ctx=ctx)
        self.carry = kit.sb(f"{name}_carry", [Q, 1], ctx=ctx)
        self.end = kit.sb(f"{name}_end", [Q, 1], ctx=ctx)
        self.turn, self.back = psum[0:1, 0:Q], psum[0:Q, 128:129]
        self.end_ready, self.turned, self.into_ready, self.returned = (
            kit.sem(f"{name}_{n}") for n in ("end_ready", "turned", "into_ready", "returned"))
        self.dve_n = self.pe_n = 0

    def pe_row(self, pe):
        self.pe_n += 1
        pe.wait_ge(self.end_ready, self.pe_n)
        self.nc.tensor.transpose(self.turn, self.end[:, :], self.k.ident[0:Q, 0:Q]).then_inc(self.turned, 1)

    def pe_scan(self, pe):
        self.pe_row(pe)
        pe.wait_ge(self.into_ready, self.pe_n)
        self.nc.tensor.matmul(self.back, self.into[:, :, :].rearrange("p c r -> p (c r)"), self.k.one[0:1, 0:1],
                              start=True, stop=True).then_inc(self.returned, 1)

    def gather_row(self, dve, link, src, forward):
        self.dve_n += 1
        self.nc.vector.tensor_copy(self.end[:, :], src).then_inc(self.end_ready, 1)
        dve.wait_ge(self.turned, self.dve_n)
        turned = self.turn.rearrange("p (c r) -> p r c", r=RH)
        for c in range(CHUNKS):
            s = c if forward else CHUNKS - 1 - c
            last = self.nc.vector.tensor_copy(self.row[:, :, c:c + 1], turned[:, :, s:s + 1])
        link(last)

    def flags_row(self, dve, link, product, out, forward):
        edge = product[:, -1:] if forward else product[:, 0:1]
        self.gather_row(dve, link, edge, forward)
        link(self.nc.vector.tensor_copy(out[:, :, :], self.row[:, :, :]))
        link(self.nc.vector.memset(out[:, :, 0:1], 0.0))
        self.nc.vector.memset(self.into[:, :, :], 0.0).then_inc(self.into_ready, 1)
        dve.wait_ge(self.returned, self.dve_n)

    def scan(self, dve, link, out, data, flags, product, flags_row, op, forward):
        vec = self.nc.vector
        n = out.shape[1]
        if forward:
            link(vec.tensor_tensor_scan(out[:, :], flags, data, 0.0, ALU.mult, op))
        else:
            link(vec.tensor_tensor_scan(out[:, ::-1], flags[:, ::-1], data[:, ::-1], 0.0, ALU.mult, op))
        self.gather_row(dve, link, out[:, n - 1:n] if forward else out[:, 0:1], forward)
        row = self.row[:, :, :].rearrange("p r c -> p (r c)")
        link(vec.tensor_tensor_scan(row, flags_row[:, :, :].rearrange("p r c -> p (r c)"), row, 0.0, ALU.mult, op))
        link(vec.memset(self.into[:, :, :], 0.0))
        for c in range(1, CHUNKS):
            d = c if forward else CHUNKS - 1 - c
            last = vec.tensor_copy(self.into[:, d:d + 1, :].rearrange("p c r -> p r c"), self.row[:, :, c - 1:c])
        last.then_inc(self.into_ready, 1)
        dve.wait_ge(self.returned, self.dve_n)
        link(vec.tensor_copy(self.carry[:, :], self.back))
        link(vec.scalar_tensor_tensor(out[:, :], product, self.carry[:, 0:1], out[:, :], ALU.mult, op))


class Chain:

    def __init__(self, kit, name):
        self.sem, self.count = kit.sem(name), 0

    def on(self, eng):
        def link(ins):
            self.count += 1
            ins.then_inc(self.sem, 1)
            eng.wait_ge(self.sem, self.count)
        return link


def turn_rows(kit, k, name, psum, src, parts, M, take):
    nc = kit.nc
    turned, took = kit.sem(f"{name}_turned"), kit.sem(f"{name}_took")
    with nc.Block() as block:
        @block.tensor
        def _(pe):
            for n in range(M // 4):
                need(pe, took, n - 1)
                for j in range(4):
                    t = 4 * n + j
                    last = nc.tensor.transpose(psum[n % 2][:, j * T:j * T + parts], src[:, t * T:(t + 1) * T],
                                               k.ident[0:parts, 0:parts])
                last.then_inc(turned, 1)

        @block.vector
        def _(dve):
            for n in range(M // 4):
                dve.wait_ge(turned, n + 1)
                take(n, psum[n % 2][:, :].rearrange("p (j q) -> p j q", j=4)).then_inc(took, 1)


def by_chunk(rows):
    return rows[:, :].rearrange("p (c j) -> p j c", c=CHUNKS)


def index_stage(kit, k, src, dst, etype, N, E, M):
    nc = kit.nc
    CH = M * T
    PIECES = CH // 512
    with ExitStack() as ctx:
        def sb(name, shape, dt=F32):
            return kit.sb(name, shape, dt, ctx)

        raw = sb("raw", [T, CH + 2], I32)
        val = sb("val", [T, CH + 2])
        same7 = sb("same7", [CHUNKS, CH])
        next7 = sb("next7", [CHUNKS, CH])
        far7 = sb("far7", [T, CH])
        wide = sb("wide", [Q, CH])
        wide2 = sb("wide2", [Q, CH])
        number7 = wide2[0:CHUNKS, :].bitcast(I32)
        psum = [ctx.enter_context(nc.psum_tensor(f"ix{i}", [T, 512], F32)) for i in range(8)]
        sc = Scans(kit, k, ctx, "ixs", psum[7])
        cleared, loaded, numbered, spread, copied, turned0, took0, copied_same = (kit.sem(f"ix_{n}") for n in (
            "cleared", "loaded", "numbered", "spread", "copied", "turned0", "took0", "copied_same"))
        chain = Chain(kit, "ix_chain")
        parts = max(p for p in range(1, T + 1) if N % p == 0)
        identity = sb("identity_place", [parts, N // parts], I32)
        loads = []
        for c in range(CHUNKS):
            lo, hi = max(c * CH - 1, 0), min(c * CH + CH + 1, E)
            at = lo - (c * CH - 1)
            for base, a in ((0, dst), (96, dst), (32, src), (64, etype)):
                loads.append((raw[base + c:base + c + 1, at:at + hi - lo], a[lo:hi].rearrange("(a n) -> a n", a=1)))

        with nc.Block() as block:
            @block.sync
            def _(sp):
                sp.wait_ge(cleared, 1)
                for o, i in loads:
                    sp.dma_start(o, i).then_inc(loaded, 16)
                sp.wait_ge(loaded, 16 * len(loads))
                sp.wait_ge(numbered, 3)
                sp.dma_start(k.place[:, :].rearrange("(p n) a -> p (n a)", p=parts), identity[:, :]
                             ).then_inc(kit.place_clear, 16)
                sp.wait_ge(kit.place_clear, 16)

            @block.gpsimd
            def _(pool):
                nc.gpsimd.iota(k.edge_row[:, :], pattern=[[T, k.NT]], base=N, channel_multiplier=1).then_inc(numbered, 1)
                nc.gpsimd.iota(number7[:, :], pattern=[[1, CH]], base=N, channel_multiplier=CH).then_inc(numbered, 1)
                nc.gpsimd.iota(identity[:, :], pattern=[[1, N // parts]], base=0,
                               channel_multiplier=N // parts).then_inc(numbered, 1)

            @block.vector
            def _(dve):
                v, link = nc.vector, chain.on(dve)
                link(v.memset(raw[:, :], 0))
                for base in (0, 96):
                    link(v.memset(raw[base:base + CHUNKS, 0:1], -1))
                    link(v.memset(raw[base:base + CHUNKS, 1:CH + 1], N))
                    link(v.memset(raw[base:base + CHUNKS, CH + 1:CH + 2], N + 1))
                link(v.memset(k.same[:, k.NT * T:], 0.0))
                v.memset(sc.into[:, :, :], 0.0).then_inc(cleared, 1)
                dve.wait_ge(loaded, 16 * len(loads))
                link(v.tensor_copy(val[:, :], raw[:, :]))
                link(v.tensor_tensor(same7[:, :], val[0:CHUNKS, 1:CH + 1], val[0:CHUNKS, 0:CH], ALU.is_equal))
                link(v.tensor_tensor(next7[:, :], val[0:CHUNKS, 1:CH + 1], val[0:CHUNKS, 2:CH + 2], ALU.is_equal))
                a96, f96 = val[96:96 + CHUNKS, :], far7[96:96 + CHUNKS, :]
                link(v.tensor_tensor(f96, a96[:, 1:CH + 1], a96[:, 2:CH + 2], ALU.is_equal))
                link(v.scalar_tensor_tensor(a96[:, 1:CH + 1], f96, FAR, a96[:, 1:CH + 1], ALU.mult, ALU.add))
                link(v.tensor_scalar(val[0:CHUNKS, 1:CH + 1], val[0:CHUNKS, 1:CH + 1], float(N - 1), None, ALU.min))
                dve.wait_ge(numbered, 2)
                link(v.tensor_copy(far7[0:CHUNKS, :], number7[:, :]))
                link(v.tensor_scalar(raw[0:CHUNKS, 0:CH].bitcast(F32), next7[:, :], -1.0, 1.0, ALU.mult, ALU.add))
                link(v.tensor_tensor(far7[0:CHUNKS, :], far7[0:CHUNKS, :], raw[0:CHUNKS, 0:CH].bitcast(F32), ALU.mult))

        def take(n, bank):
            for f, out in enumerate((k.dst_i, k.src_i, k.type_f, k.last_i)):
                ins = nc.vector.tensor_copy(by_chunk(out)[:, 4 * n:4 * n + 4, :], bank[:, :, 32 * f:32 * f + CHUNKS])
            return nc.vector.tensor_scalar(by_chunk(k.last_f)[:, 4 * n:4 * n + 4, :], bank[:, :, 96:96 + CHUNKS],
                                           float(N), None, ALU.is_lt)

        turn_rows(kit, k, "ix_all", psum, val[:, 1:CH + 1], T, M, take)

        jobs = [(same7, k.same84), (next7, k.next84), (far7, wide)]
        with nc.Block() as block:
            @block.tensor
            def _(pe):
                for n in range(3 * PIECES):
                    at = n % PIECES * 512
                    need(pe, copied, n - 1)
                    nc.tensor.matmul(psum[n % 2][0:Q, :], k.chunk_of[:, :], jobs[n // PIECES][0][0:CHUNKS, at:at + 512],
                                     start=True, stop=True).then_inc(spread, 1)
                for n in range(k.NG):
                    at = n % PIECES * 512
                    need(pe, copied_same, n - 1)
                    nc.tensor.matmul(psum[2 + n % 2][:, :], k.one_chunk[:, n // PIECES, :], same7[:, at:at + 512],
                                     start=True, stop=True).then_inc(turned0, 1)

            @block.vector
            def _(dve):
                for n in range(3 * PIECES):
                    at = n % PIECES * 512
                    dve.wait_ge(spread, n + 1)
                    nc.vector.tensor_copy(jobs[n // PIECES][1][:, at:at + 512], psum[n % 2][0:Q, :]).then_inc(copied, 1)

            @block.scalar
            def _(act):
                for n in range(k.NG):
                    act.wait_ge(turned0, n + 1)
                    nc.scalar.activation(k.same[:, n * 512:(n + 1) * 512], psum[2 + n % 2][:, :],
                                         ACT.Copy).then_inc(copied_same, 1)

        with nc.Block() as block:
            @block.vector
            def _(dve):
                v, link = nc.vector, chain.on(dve)
                for r in range(R):
                    link(v.tensor_scalar(k.is_type[:, :, r], k.type_f[:, :], float(r), None, ALU.is_equal))
                link(v.memset(wide2[:, :], 0.0))
                link(v.tensor_tensor_scan(k.prod_f[:, :], k.same84[:, :], wide2[:, :], 1.0, ALU.mult, ALU.add))
                link(v.tensor_tensor_scan(k.prod_b[:, ::-1], k.next84[:, ::-1], wide2[:, ::-1], 1.0, ALU.mult, ALU.add))
                sc.flags_row(dve, link, k.prod_f, k.flow_f, True)
                sc.flags_row(dve, link, k.prod_b, k.flow_b, False)
                sc.scan(dve, link, wide2, wide[:, :], k.next84[:, :], k.prod_b[:, :], k.flow_b, ALU.add, False)

            @block.tensor
            def _(pe):
                for _ in range(3):
                    sc.pe_scan(pe)

        turn_rows(kit, k, "ix_pos", psum, wide2, Q, M, lambda n, bank: nc.vector.tensor_copy(
            by_chunk(k.dstp_i)[:, 4 * n:4 * n + 4, :], bank[:, :, 0:Q:RH]))

        with nc.Block() as block:
            @block.vector
            def _(dve):
                v, link = nc.vector, chain.on(dve)
                link(v.memset(wide[:, :], 1.0))
                sc.scan(dve, link, wide2, wide[:, :], k.same84[:, :], k.prod_f[:, :], k.flow_f, ALU.add, True)

            @block.tensor
            def _(pe):
                sc.pe_scan(pe)

        turn_rows(kit, k, "ix_deg", psum, wide2, Q, M, lambda n, bank: nc.vector.tensor_copy(
            by_chunk(k.deg)[:, 4 * n:4 * n + 4, :], bank[:, :, 0:Q:RH]))
        with nc.Block() as block:
            @block.vector
            def _(dve):
                nc.vector.reciprocal(k.rdeg[:, :], k.deg[:, :]).then_inc(cleared, 1)

            @block.scalar
            def _(act):
                act.wait_ge(cleared, 2)
                nc.scalar.activation(k.norm[:, :], k.rdeg[:, :], ACT.Sqrt)


def over(row):
    return row[:, :].rearrange("p (a d) -> p a d", a=1).to_broadcast([T, G, D])


def turn(nc, k, bank, buf, done):
    for j in range(G):
        last = nc.tensor.transpose(bank[:, j * T:(j + 1) * T], buf[:, j * T:(j + 1) * T], k.ident[:, :])
    last.then_inc(done, 1)


def multiply_rows(nc, bank, turned, weights, done):
    for j in range(G):
        last = nc.tensor.matmul(bank[:, j * T:(j + 1) * T], turned[:, j * T:(j + 1) * T], weights, start=True, stop=True)
    last.then_inc(done, 1)


def edge_rows(dram, g, base):
    return dram[bass.ds(g * W + base, W), :].rearrange("(j p) d -> p j d", p=T)


class Gather:

    def __init__(self, kit, ctx, name, index, table, bufs, n=G, place=lambda g: g):
        self.kit, self.index, self.table, self.bufs, self.n, self.place = kit, index, table, bufs, n, place
        self.now = [kit.sb(f"{name}_now{b}", [T, n], I32, ctx) for b in range(2)]
        self.staged = kit.sem(f"{name}_staged")
        self.arrived = [kit.sem(f"{name}_arrived{b}", True) for b in range(2)]

    def stage(self, pool, free):
        def run(g, h, b):
            nc = self.kit.nc
            waits = list(free(g, h, b))
            if not (isinstance(h, int) and h <= 0):
                waits.append((self.arrived[b], h * 16 * self.n))
            self.kit.hold("pool", pool, *waits)
            nc.gpsimd.tensor_copy(self.now[b][:, :], self.index[:, bass.ds(self.place(g) * self.n, self.n)]).then_inc(self.staged, 1)
            self.kit.hold("pool", pool, (self.staged, g + 1))
            for j in range(self.n):
                pool.indirect_dma_start(self.bufs[b][:, j * T:(j + 1) * T], None, self.table,
                                        bass.IndirectOffsetOnAxis(ap=self.now[b][:, j:j + 1], axis=0)
                                        ).then_inc(self.arrived[b], 16)
        return run

    def wait(self, eng, h, b):
        eng.wait_ge(self.arrived[b], (h + 1) * 16 * self.n)


def segment_sum(kit, k, dve, out, messages, ready, summed, free):
    def stage(g, h, b):
        for sem, value in free(g):
            need(dve, sem, value)
        need(dve, summed, g)
        kit.hold("dve", dve, (ready, g + 1))
        first = isinstance(g, int) and g == 0
        kit.nc.vector.tensor_tensor_scan(out[b][:, :], k.same[:, bass.ds(g * W, W)], messages[b][:, :],
                                         0.0 if first else out[1 - b][:, W - 1:W], ALU.mult, ALU.add).then_inc(summed, 1)
    return stage


class Spread:

    def __init__(self, kit, ctx, name):
        self.kit = kit
        self.sums, self.std, self.rstd = ([kit.sb(f"{name}_{n}{b}", [T, G], F32, ctx) for b in range(2)]
                                          for n in ("sums", "std", "rstd"))
        self.square = kit.sb(f"{name}_square", [T, W], F32, ctx)
        self.summed, self.rooted, self.inverted = (kit.sem(f"{name}_{n}") for n in ("summed", "rooted", "inverted"))

    def on_act(self, act, eps, tile, g, b):
        nc = self.kit.nc
        need(act, self.inverted, g - 1)
        for j in range(G):
            last = nc.scalar.activation(self.square[:, j * D:(j + 1) * D], tile(j), ACT.Square, accum_out=self.sums[b][:, j:j + 1])
        last.then_inc(self.summed, 1)
        act.wait_ge(self.summed, g + 1)
        nc.scalar.activation(self.std[b][:, :], self.sums[b][:, :], ACT.Sqrt, bias=eps, scale=1.0 / D
                             ).then_inc(self.rooted, 1)

    def invert(self, dve, g, b):
        dve.wait_ge(self.rooted, g + 1)
        self.kit.nc.vector.reciprocal(self.rstd[b][:, :], self.std[b][:, :]).then_inc(self.inverted, 1)
        dve.wait_ge(self.inverted, g + 1)


def wide(col):
    return col[:, :].rearrange("p (j a) -> p j a", a=1).to_broadcast([T, G, D])


def first_pass(kit, k, x, out, x_own):
    nc = kit.nc
    N = k.N
    GD = -(-N // W)
    GE = k.NT // 2
    E2 = 2 * T
    LAG = 9
    both = max(GD, GE)
    with ExitStack() as ctx:
        def pair(name, shape=(T, W), dt=F32):
            return [kit.sb(f"dn_{name}{b}", list(shape), dt, ctx) for b in range(2)]

        X, XT, H1T, H1R, H2T, YT, X1R, Y2, X2R = (pair(n) for n in "X XT H1T H1R H2T YT X1R Y2 X2R".split())
        Y3, X3R, X3B, X3T, MA, MB, Y4, X4R = (pair(n) for n in "Y3 X3R X3B X3T MA MB Y4 X4R".split())
        XS, XD, XDT, AG, BASE, MIX, HR = (pair(n, (T, E2)) for n in "XS XD XDT AG BASE MIX HR".split())
        B = [ctx.enter_context(nc.psum_tensor(f"dn_bank{i}", [T, 512], F32)) for i in range(8)]
        sp1, sp2, sp3, sp4 = (Spread(kit, ctx, f"dn_sp{i}") for i in (1, 2, 3, 4))
        (xt_turned, xt, h1_mul, h1t, h1_turned, h1r, h2_mul, h2t, yt, mixed, x1, y2, x2, y3, x3, x3b, x3_turned, x3t,
         ma_mul, mb_mul, ma, mb, out_mul, y4, x4) = (kit.sem(f"dn_{n}") for n in (
             "xt_turned xt h1_mul h1t h1_turned h1r h2_mul h2t yt mixed x1 y2 x2 y3 x3 x3b x3_turned x3t "
             "ma_mul mb_mul ma mb out_mul y4 x4").split())
        s_turned, d_turned, summed, xdt, a_mul, b_mul, base, joined, hr = (kit.sem(f"se_{n}") for n in (
            "s_turned d_turned summed xdt a_mul b_mul base joined hr").split())
        x_in = [kit.sem(f"dn_x_in{b}") for b in range(2)]
        h1_out, x1_out, x2_out, x3_out, out_out, kept, stored = ([kit.sem(f"dn_{n}{b}") for b in range(2)] for n in (
            "h1_out", "x1_out", "x2_out", "x3_out", "out_out", "kept", "stored"))
        src_g = Gather(kit, ctx, "se_src", k.src_i, x, XS, 2)
        own_g = Gather(kit, ctx, "se_own", k.dst_i, x, XD, 2)
        now, vals = pair("pl_now", (T, G), I32), pair("pl_vals", (T, G), I32)
        got = pair("pl_got", (T, G), I32)
        pl_now, pl_kept = kit.sem("pl_staged"), kit.sem("pl_kept")
        pl_put, pl_got = ([kit.sem(f"pl_{n}{b}", True) for b in range(2)] for n in ("put", "got"))

        def rows(dram, g):
            base_row = g * W if not isinstance(g, int) else min(g * W, N - W)
            return dram[bass.ds(base_row, W), :].rearrange("(p j) d -> p (j d)", j=G)

        def pair_rows(dram, g, base_row):
            return dram[bass.ds(g * E2 + base_row, E2), :].rearrange("(j p) d -> p j d", p=T)

        def two(buf):
            return buf[:, :].rearrange("p (j d) -> p j d", j=2)

        def run(eng, *line):
            def body(at_n, at_e):
                for stream, lag, stage in line:
                    g = (at_n if stream == "n" else at_e)(lag)
                    if g is not None:
                        stage(*g)
            two_streams(eng, GD, GE, LAG, body)

        def gone(stored_sem, h, b):
            return (stored_sem[b], h * 16)

        with nc.Block() as block:
            @block.gpsimd
            def _(pool):
                pool.wait_ge(kit.place_clear, 16)

                def put_place(g, h, b):
                    kit.hold("pool", pool, (pl_put[b], h * 16 * G))
                    nc.gpsimd.tensor_copy(now[b][:, :], k.last_i[:, bass.ds(g * G, G)]).then_inc(pl_now, 1)
                    nc.gpsimd.tensor_copy(vals[b][:, :], k.edge_row[:, bass.ds(g * G, G)]).then_inc(pl_now, 1)
                    kit.hold("pool", pool, (pl_now, g * 2 + 2))
                    for j in range(G):
                        pool.indirect_dma_start(k.place, bass.IndirectOffsetOnAxis(ap=now[b][:, j:j + 1], axis=0),
                                                vals[b][:, j:j + 1], None, bounds_check=N - 1,
                                                oob_is_err=False).then_inc(pl_put[b], 16)

                def fetch(g, h, b):
                    kit.hold("pool", pool, (pl_got[b], h * 16 * G), (pl_kept, g - 1))
                    nc.gpsimd.tensor_copy(now[b][:, :], k.src_i[:, bass.ds(g * G, G)]).then_inc(pl_now, 1)
                    kit.hold("pool", pool, (pl_now, 2 * k.NG + g + 1))
                    for j in range(G):
                        pool.indirect_dma_start(got[b][:, j:j + 1], None, k.place,
                                                bass.IndirectOffsetOnAxis(ap=now[b][:, j:j + 1], axis=0)
                                                ).then_inc(pl_got[b], 16)

                def keep_place(g, h, b):
                    kit.hold("pool", pool, (pl_got[b], (h + 1) * 16 * G))
                    nc.gpsimd.tensor_copy(k.srcp_i[:, bass.ds(g * G, G)], got[b][:, :]).then_inc(pl_kept, 1)

                gather_src = src_g.stage(pool, lambda g, h, b: [(s_turned, g - 1)])
                gather_own = own_g.stage(pool, lambda g, h, b: [(d_turned, g - 1), (kept[b], h * 16)])
                half = k.NG // 2 * 2

                def with_puts(s, h, b):
                    gather_src(s, h, b)
                    gather_own(s, h, b)
                    put_place(s, h, b)

                def with_fetches(s, h, b, g):
                    gather_src(s, h, b)
                    gather_own(s, h, b)
                    fetch(*g)

                for s in range(2):
                    with_puts(s, 0, s)
                with pool.Fori(1, half // 2) as i:
                    for u in range(2):
                        with_puts(i * 2 + u, i, u)
                for g in range(half, k.NG):
                    put_place(g, g // 2, g % 2)
                for b in range(2):
                    pool.wait_ge(pl_put[b], 16 * G * ((k.NG - b + 1) // 2))
                off = half // 2
                for s in range(2):
                    with_fetches(half + s, off, s, (s, 0, s))
                with pool.Fori(1, half // 2) as i:
                    for u in range(2):
                        keep_place(i * 2 + (u - 2), i - 1, u)
                        with_fetches(i * 2 + (half + u), i + off, u, (i * 2 + u, i, u))
                for g in range(half - 2, half):
                    keep_place(g, g // 2, g % 2)
                for g in range(half, k.NG):
                    fetch(g, g // 2, g % 2)
                    keep_place(g, g // 2, g % 2)
                for s in range(2 * half, GE):
                    gather_src(s, s // 2, s % 2)
                    gather_own(s, s // 2, s % 2)

            @block.sync
            def _(sp):
                def load(g, h, b):
                    need(sp, xt_turned, g - 1)
                    sp.dma_start(X[b][:, :], rows(x, g)).then_inc(x_in[b], 16)

                def store(dram, buf, written, landed):
                    def stage(g, h, b):
                        sp.wait_ge(written, g + 1)
                        if isinstance(g, int) and g == GD - 1:
                            sp.wait_ge(landed[1 - b], 16 * ((g - 1) // 2 + 1))
                        sp.dma_start(rows(dram, g), buf[b][:, :]).then_inc(landed[b], 16)
                    return stage

                def keep(g, h, b):
                    own_g.wait(sp, h, b)
                    sp.dma_start(pair_rows(x_own, g, 0), two(XD[b])).then_inc(kept[b], 16)

                def store_h(g, h, b):
                    sp.wait_ge(hr, g + 1)
                    sp.dma_start(pair_rows(k.tab[0], g, N), two(HR[b])).then_inc(stored[b], 16)

                run(sp, ("n", 0, load), ("n", 3, store(k.tab[1], X1R, x1, x1_out)),
                    ("n", 4, store(k.tab[0], H1R, h1r, h1_out)), ("n", 4, store(k.tab[2], X2R, x2, x2_out)),
                    ("n", 5, store(k.tab[3], X3R, x3, x3_out)), ("n", LAG, store(out, X4R, x4, out_out)),
                    ("e", 5, store_h), ("e", 1, keep))
                for s in (h1_out, x1_out, x2_out, x3_out, out_out):
                    for b in range(2):
                        sp.wait_ge(s[b], 16 * ((GD - b + 1) // 2))
                for s in (kept, stored):
                    for b in range(2):
                        sp.wait_ge(s[b], 16 * ((GE - b + 1) // 2))

            @block.tensor
            def _(pe):
                def clear(g, lag, *users):
                    for read, stream, its_lag, before in users:
                        value = g + (lag - its_lag + before)
                        need(pe, read, min(value, GD if stream == "n" else GE) if isinstance(g, int) else value)

                def turn_x(g, h, b):
                    pe.wait_ge(x_in[b], (h + 1) * 16)
                    clear(g, 1, (ma, "n", 5, 0), (summed, "e", 1, 0))
                    turn(nc, k, B[4], X[b], xt_turned)

                def mul_mix(g, h, b):
                    pe.wait_ge(yt, g + 1)
                    clear(g, 2, (x1, "n", 2, 0), (y2, "n", 2, 0))
                    for j in range(G):
                        last = nc.tensor.matmul(B[2 + j // 2][:, (j % 2) * 2 * D:(j % 2 + 1) * 2 * D],
                                                YT[b][:, j * T:(j + 1) * T], k.pair_mix[:, :], start=True, stop=True)
                    last.then_inc(mixed, 1)

                def turn_h1(g, h, b):
                    pe.wait_ge(h1t, g + 1)
                    clear(g, 2, (h1r, "n", 2, 0))
                    turn(nc, k, B[7], H1T[b], h1_turned)

                def mul_h1(g, h, b):
                    pe.wait_ge(xt, g + 1)
                    clear(g, 1, (xdt, "e", 1, 1), (h2t, "n", 1, 0))
                    nc.tensor.matmul(B[6][:, :], k.wr1[:, :], XT[b][:, :], start=True, stop=True).then_inc(h1_mul, 1)

                def mul_out(g, h, b):
                    pe.wait_ge(ma, g + 1)
                    pe.wait_ge(mb, g + 1)
                    clear(g, 6, (joined, "e", 2, 0), (y4, "n", 6, 0))
                    for j in range(G):
                        at = slice(j * T, (j + 1) * T)
                        nc.tensor.matmul(B[5][:, at], MA[b][:, at], k.wm2[:, 0, :], start=True, stop=False)
                        last = nc.tensor.matmul(B[5][:, at], MB[b][:, at], k.wm2[:, 1, :], start=False, stop=True)
                    last.then_inc(out_mul, 1)

                def mul_h2(g, h, b):
                    pe.wait_ge(h1t, g + 1)
                    clear(g, 1, (xdt, "e", 1, 1), (h2t, "n", 1, 0))
                    nc.tensor.matmul(B[6][:, :], k.wr2[:, :], H1T[b][:, :], start=True, stop=True).then_inc(h2_mul, 1)

                def mul_ma(g, h, b):
                    pe.wait_ge(x3t, g + 1)
                    clear(g, 5, (summed, "e", 1, 1), (xt, "n", 1, 1), (ma, "n", 5, 0))
                    nc.tensor.matmul(B[4][:, :], k.wm1[:, 0:D], X3T[b][:, :], start=True, stop=True).then_inc(ma_mul, 1)

                def turn_x3(g, h, b):
                    pe.wait_ge(x3, g + 1)
                    clear(g, 4, (x3t, "n", 4, 0))
                    turn(nc, k, B[0], X3R[b], x3_turned)

                def mul_mb(g, h, b):
                    pe.wait_ge(x3t, g + 1)
                    clear(g, 5, (base, "e", 1, 1), (mb, "n", 5, 0))
                    nc.tensor.matmul(B[1][:, :], k.wm1[:, D:2 * D], X3T[b][:, :], start=True, stop=True).then_inc(mb_mul, 1)

                def turn_e(bank, buf, done):
                    for j in range(2):
                        last = nc.tensor.transpose(bank[:, j * T:(j + 1) * T], buf[:, j * T:(j + 1) * T], k.ident[:, :])
                    last.then_inc(done, 1)

                def mul_e(bank, buf, weights, done):
                    for j in range(2):
                        last = nc.tensor.matmul(bank[:, j * T:(j + 1) * T], buf[:, j * T:(j + 1) * T], weights,
                                                start=True, stop=True)
                    last.then_inc(done, 1)

                def turn_s(g, h, b):
                    src_g.wait(pe, h, b)
                    clear(g, 1, (xt, "n", 1, 1), (ma, "n", 5, 0), (summed, "e", 1, 0))
                    turn_e(B[4], XS[b], s_turned)

                def turn_d(g, h, b):
                    own_g.wait(pe, h, b)
                    clear(g, 1, (h2t, "n", 1, 0), (xdt, "e", 1, 0))
                    turn_e(B[6], XD[b], d_turned)

                def mul_a(g, h, b):
                    pe.wait_ge(summed, g + 1)
                    clear(g, 2, (y4, "n", 6, 1), (joined, "e", 2, 0))
                    mul_e(B[5], AG[b], k.wl1[:, :], a_mul)

                def mul_b(g, h, b):
                    pe.wait_ge(xdt, g + 1)
                    clear(g, 1, (mb, "n", 5, 0), (base, "e", 1, 0))
                    mul_e(B[1], XDT[b], k.wr1[:, :], b_mul)

                run(pe, ("e", 1, turn_d), ("n", 1, turn_x), ("n", 2, mul_mix), ("n", 2, turn_h1), ("e", 1, turn_s),
                    ("n", 1, mul_h1), ("n", 6, mul_out), ("n", 1, mul_h2), ("n", 5, mul_ma), ("e", 1, mul_b),
                    ("e", 2, mul_a), ("n", 4, turn_x3), ("n", 5, mul_mb))

            @block.scalar
            def _(act):
                def on(dst, bank, ready, done, func, free, **more):
                    def stage(g, h, b):
                        for sem in free:
                            need(act, sem, g - 1)
                        act.wait_ge(ready, g + 1)
                        nc.scalar.activation(dst[b][:, :], bank[:, 0:dst[b].shape[1]], func, **more).then_inc(done, 1)
                    return stage

                def spread(sp, rows_ready, tile):
                    def stage(g, h, b):
                        act.wait_ge(rows_ready, g + 1)
                        sp.on_act(act, k.eps[:, 0:1], lambda j: tile(b, j), g, b)
                    return stage

                def tile_of(buf):
                    return lambda b, j: buf[b][:, j * D:(j + 1) * D]

                def relu_h(g, h, b):
                    need(act, *gone(stored, h, b))
                    act.wait_ge(joined, g + 1)
                    nc.scalar.activation(HR[b][:, :], MIX[b][:, :], ACT.Relu).then_inc(hr, 1)

                copy_x = on(XT, B[4], xt_turned, xt, ACT.Copy, [yt])
                relu_h1 = on(H1T, B[6], h1_mul, h1t, ACT.Relu, [h1_turned, h2_mul], bias=k.bl1_col[:, 0:1])
                relu_h2 = on(H2T, B[6], h2_mul, h2t, ACT.Relu, [yt], bias=k.bl2_col[:, 0:1])
                copy_x3 = on(X3T, B[0], x3_turned, x3t, ACT.Copy, [ma_mul, mb_mul])
                relu_a, relu_b = (
                    on(m, bank, ready, done, ACT.Relu, [out_mul], bias=k.bn1_b[:, n:n + 1], scale=k.bn1_s_own[:, n:n + 1])
                    for n, (m, bank, ready, done) in enumerate(((MA, B[4], ma_mul, ma), (MB, B[1], mb_mul, mb))))
                copy_d = on(XDT, B[6], d_turned, xdt, ACT.Copy, [b_mul])
                run(act, ("e", 4, relu_h), ("n", 8, spread(sp4, y4, tile_of(Y4))), ("n", 4, spread(sp3, y3, tile_of(Y3))),
                    ("n", 2, relu_h2), ("n", 6, relu_a), ("n", 3, spread(sp2, y2, tile_of(Y2))), ("e", 1, copy_d),
                    ("n", 6, relu_b), ("n", 5, copy_x3), ("n", 1, copy_x),
                    ("n", 2, spread(sp1, mixed, lambda b, j: B[2 + j // 2][:, (j % 2) * 2 * D:(j % 2) * 2 * D + D])),
                    ("n", 1, relu_h1))

            @block.vector
            def _(dve):
                v = nc.vector

                def add_y(g, h, b):
                    need(dve, mixed, g - 1)
                    dve.wait_ge(h2t, g + 1)
                    v.tensor_tensor(YT[b][:, :], H2T[b][:, :], XT[b][:, :], ALU.add).then_inc(yt, 1)

                def take_h1(g, h, b):
                    need(dve, *gone(h1_out, h, b))
                    dve.wait_ge(h1_turned, g + 1)
                    v.tensor_copy(H1R[b][:, :], B[7][:, :]).then_inc(h1r, 1)

                def scale_x1(g, h, b):
                    sp1.invert(dve, g, b)
                    need(dve, *gone(x1_out, h, b))
                    for i in range(2):
                        last = v.tensor_tensor(
                            tiles(X1R[b])[:, 2 * i:2 * i + 2, :],
                            B[2 + i][:, :].rearrange("p (j n) -> p j n", j=2)[:, :, 0:D],
                            wide(sp1.rstd[b])[:, 2 * i:2 * i + 2, :], ALU.mult)
                    last.then_inc(x1, 1)

                def scale_y2(g, h, b):
                    need(dve, x2, g - 1)
                    for j in range(G):
                        last = v.scalar_tensor_tensor(
                            Y2[b][:, j * D:(j + 1) * D], B[2 + j // 2][:, (j % 2) * 2 * D + D:(j % 2 + 1) * 2 * D],
                            sp1.rstd[b][:, j:j + 1], k.bbar_row[:, :], ALU.mult, ALU.add)
                    last.then_inc(y2, 1)

                def scale_x2(g, h, b):
                    sp2.invert(dve, g, b)
                    need(dve, *gone(x2_out, h, b))
                    need(dve, y3, g - 1)
                    v.tensor_tensor(tiles(X2R[b]), tiles(Y2[b]), wide(sp2.rstd[b]), ALU.mult).then_inc(x2, 1)

                def add_y3(g, h, b):
                    need(dve, x3, g - 1)
                    dve.wait_ge(x2, g + 1)
                    v.tensor_tensor(tiles(Y3[b]), tiles(X2R[b]), over(k.b2_row), ALU.add).then_inc(y3, 1)

                def scale_x3(g, h, b):
                    sp3.invert(dve, g, b)
                    need(dve, *gone(x3_out, h, b))
                    need(dve, x3_turned, g - 1)
                    need(dve, x3b, g - 1)
                    v.tensor_tensor(tiles(X3R[b]), tiles(Y3[b]), wide(sp3.rstd[b]), ALU.mult).then_inc(x3, 1)

                def bias_x3(g, h, b):
                    dve.wait_ge(x3, g + 1)
                    need(dve, y4, g - 1)
                    v.tensor_tensor(tiles(X3B[b]), tiles(X3R[b]), over(k.bn2_row), ALU.add).then_inc(x3b, 1)

                def add_y4(g, h, b):
                    dve.wait_ge(x3b, g + 1)
                    need(dve, x4, g - 1)
                    dve.wait_ge(out_mul, g + 1)
                    v.tensor_tensor(Y4[b][:, :], B[5][:, :], X3B[b][:, :], ALU.add).then_inc(y4, 1)

                def scale_x4(g, h, b):
                    sp4.invert(dve, g, b)
                    need(dve, *gone(out_out, h, b))
                    v.tensor_tensor(tiles(X4R[b]), tiles(Y4[b]), wide(sp4.rstd[b]), ALU.mult).then_inc(x4, 1)

                def total(g, h, b):
                    need(dve, a_mul, g - 1)
                    need(dve, summed, g)
                    kit.hold("dve", dve, (s_turned, g + 1))
                    first = isinstance(g, int) and g == 0
                    v.tensor_tensor_scan(AG[b][:, :], k.same[:, bass.ds(g * E2, E2)], B[4][:, 0:E2],
                                         0.0 if first else AG[1 - b][:, E2 - 1:E2], ALU.mult, ALU.add
                                         ).then_inc(summed, 1)

                def add_bias(g, h, b):
                    dve.wait_ge(b_mul, g + 1)
                    need(dve, joined, g - 1)
                    v.tensor_tensor(two(BASE[b]), two(B[1][:, 0:E2]), k.bl1_row[:, :].rearrange(
                        "p (a d) -> p a d", a=1).to_broadcast([T, 2, D]), ALU.add).then_inc(base, 1)

                def join(g, h, b):
                    need(dve, hr, g - 1)
                    kit.hold("dve", dve, (base, g + 1), (a_mul, g + 1))
                    for j in range(2):
                        at = slice(j * T, (j + 1) * T)
                        last = v.scalar_tensor_tensor(MIX[b][:, at], B[5][:, at], k.rdeg[:, bass.ds(g * 2 + j, 1)],
                                                      BASE[b][:, at], ALU.mult, ALU.add)
                    last.then_inc(joined, 1)

                run(dve, ("e", 3, join), ("n", 2, add_y), ("n", 3, take_h1), ("n", 3, scale_x2), ("n", 6, bias_x3),
                    ("n", 4, scale_x3), ("n", 8, scale_x4), ("n", 3, add_y3), ("e", 1, total), ("n", 2, scale_x1),
                    ("n", 6, add_y4), ("n", 2, scale_y2), ("e", 1, add_bias))


def two_streams(eng, n1, n2, lag, body):
    def fixed(s, n):
        def at(k):
            g = s - k
            return (g, g // 2, g % 2) if 0 <= g < n else None
        return at

    first = lag + 2 + (lag % 2)
    pairs = (min(n1, n2) - 1 - first) // 2
    start = max(n1, n2) + lag if pairs < 2 else first
    for s in range(start):
        body(fixed(s, n1), fixed(s, n2))
    if pairs < 2:
        return
    with eng.Fori(0, pairs) as i:
        for u in range(2):
            def at(k, u=u):
                c = first + u - k
                return i * 2 + c, i + c // 2, c % 2
            body(at, at)
    for s in range(first + 2 * pairs, max(n1, n2) + lag):
        body(fixed(s, n1), fixed(s, n2))


def sage(kit, k):
    nc = kit.nc
    LAG = 5
    name = "s2"
    with ExitStack() as ctx:
        def pair(n):
            return [kit.sb(f"{name}_{n}{b}", [T, W], F32, ctx) for b in range(2)]

        XS, XD, XDT, AG, BASE, MIX, HR, XR, Y, OUT = (pair(n) for n in "XS XD XDT AG BASE MIX HR XR Y OUT".split())
        ln = Norm(kit, ctx, f"{name}_ln")
        B = [ctx.enter_context(nc.psum_tensor(f"{name}_bank{i}", [T, 512], F32)) for i in range(4)]
        src_g = Gather(kit, ctx, f"{name}_src", k.srcp_i, k.tab[0], XS)
        s_turned, d_turned, summed, xdt, a_mul, b_mul, base, mixed, hr, added = (kit.sem(f"{name}_{n}") for n in (
            "s_turned", "d_turned", "summed", "xdt", "a_mul", "b_mul", "base", "mixed", "hr", "added"))
        own_in, x_in, stored = ([kit.sem(f"{name}_{n}{b}") for b in range(2)] for n in ("own_in", "x_in", "stored"))

        with nc.Block() as block:
            @block.gpsimd
            def _(pool):
                steps(pool, k.NG, LAG, lambda at: rounds(
                    at, [(0, src_g.stage(pool, lambda g, h, b: [(s_turned, g - 1)]))]))

            @block.sync
            def _(sp):
                def load(g, h, b):
                    need(sp, d_turned, g - 1)
                    sp.dma_start(tiles(XD[b]), edge_rows(k.tab[0], g, k.N)).then_inc(own_in[b], 16)

                def load_x(g, h, b):
                    need(sp, added, g - 1)
                    sp.dma_start(tiles(XR[b]), edge_rows(k.x_own, g, 0)).then_inc(x_in[b], 16)

                def store(g, h, b):
                    sp.wait_ge(ln.done, g + 1)
                    sp.dma_start(edge_rows(k.tab[1], g, k.N), tiles(OUT[b])).then_inc(stored[b], 16)

                steps(sp, k.NG, LAG, lambda at: rounds(at, [(0, load), (2, load_x), (LAG, store)]))
                for b in range(2):
                    sp.wait_ge(stored[b], 16 * ((k.NG - b + 1) // 2))

            @block.tensor
            def _(pe):
                def turn_s(g, h, b):
                    src_g.wait(pe, h, b)
                    need(pe, summed, g)
                    turn(nc, k, B[0], XS[b], s_turned)

                def turn_d(g, h, b):
                    pe.wait_ge(own_in[b], (h + 1) * 16)
                    need(pe, xdt, g)
                    turn(nc, k, B[1], XD[b], d_turned)

                def mul_b(g, h, b):
                    need(pe, base, g)
                    pe.wait_ge(xdt, g + 1)
                    multiply_rows(nc, B[3], XDT[b], k.wr2[:, :], b_mul)

                def mul_a(g, h, b):
                    need(pe, mixed, g)
                    pe.wait_ge(summed, g + 1)
                    multiply_rows(nc, B[2], AG[b], k.wl2[:, :], a_mul)

                steps(pe, k.NG, LAG, lambda at: rounds(at, [(3, mul_a), (2, mul_b), (1, turn_d), (1, turn_s)]))

            @block.scalar
            def _(act):
                def copy_own(g, h, b):
                    need(act, b_mul, g - 1)
                    act.wait_ge(d_turned, g + 1)
                    nc.scalar.activation(XDT[b][:, :], B[1][:, :], ACT.Copy).then_inc(xdt, 1)

                def relu(g, h, b):
                    need(act, added, g - 1)
                    act.wait_ge(mixed, g + 1)
                    nc.scalar.activation(HR[b][:, :], MIX[b][:, :], ACT.Relu).then_inc(hr, 1)

                def scale(g, h, b):
                    if not (isinstance(h, int) and h <= 0):
                        act.wait_ge(stored[b], h * 16)
                    ln.scale(act, tiles(OUT[b]), tiles(Y[b]), g, b)

                steps(act, k.NG, LAG, lambda at: rounds(at, [
                    (3, relu), (1, copy_own), (4, lambda g, h, b: ln.root(act, k.eps[:, 0:1], g, b)), (4, scale)]))

            @block.vector
            def _(dve):
                v = nc.vector
                total = segment_sum(kit, k, dve, AG, [B[0]] * 2, s_turned, summed, lambda g: [(a_mul, g - 1)])

                def add_bias(g, h, b):
                    need(dve, mixed, g - 1)
                    dve.wait_ge(b_mul, g + 1)
                    v.tensor_tensor(tiles(BASE[b]), tiles(B[3]), over(k.bl2_row), ALU.add).then_inc(base, 1)

                def mix(g, h, b):
                    need(dve, hr, g - 1)
                    kit.hold("dve", dve, (base, g + 1), (a_mul, g + 1))
                    for j in range(G):
                        last = v.scalar_tensor_tensor(MIX[b][:, j * T:(j + 1) * T], B[2][:, j * T:(j + 1) * T],
                                                      k.rdeg[:, bass.ds(g * G + j, 1)], BASE[b][:, j * T:(j + 1) * T],
                                                      ALU.mult, ALU.add)
                    last.then_inc(mixed, 1)

                def add_x(g, h, b):
                    need(dve, ln.done, g - 1)
                    dve.wait_ge(x_in[b], (h + 1) * 16)
                    dve.wait_ge(hr, g + 1)
                    v.tensor_tensor(Y[b][:, :], HR[b][:, :], XR[b][:, :], ALU.add).then_inc(added, 1)

                def measure(g, h, b):
                    dve.wait_ge(added, g + 1)
                    ln.bn_moments(dve, tiles(Y[b]), g, b)

                steps(dve, k.NG, LAG, lambda at: rounds(at, [
                    (3, mix), (2, add_bias), (4, measure), (1, total), (3, add_x),
                    (4, lambda g, h, b: ln.invert(dve, g, b))]))


def gat_messages(kit, k):
    nc = kit.nc
    LAG = 3
    name = "ga"
    with ExitStack() as ctx:
        def pair(n):
            return [kit.sb(f"{name}_{n}{b}", [T, W], F32, ctx) for b in range(2)]

        XS, XD, XM, DFT, XDT, Z = (pair(n) for n in "XS XD XM DFT XDT Z".split())
        NEXT = [kit.sb(f"{name}_next{b}", [T, W], BF16, ctx) for b in range(2)]
        PART = [kit.sb(f"{name}_part{i}", [T, D], F32, ctx) for i in range(4)]
        B = [ctx.enter_context(nc.psum_tensor(f"{name}_bank{i}", [T, 512], F32)) for i in range(8)]
        src_g = Gather(kit, ctx, f"{name}_src", k.srcp_i, k.tab[1], XS, place=lambda g: (k.NG - 1) - g)
        flags, xm, d_turned, xdt, s_turned, dft, s_mul, taken, z_mul, z0, z1, zed, scored = (kit.sem(f"{name}_{n}") for n in (
            "flags", "xm", "d_turned", "xdt", "s_turned", "dft", "s_mul", "taken", "z_mul", "z0", "z1", "zed", "scored"))
        own_in, stored = ([kit.sem(f"{name}_{n}{b}") for b in range(2)] for n in ("own_in", "stored"))

        def back(g):
            return (k.NG - 1) - g

        with nc.Block() as block:
            @block.gpsimd
            def _(pool):
                steps(pool, k.NG, LAG, lambda at: rounds(
                    at, [(0, src_g.stage(pool, lambda g, h, b: [(s_turned, g - 1)]))]))

            @block.sync
            def _(sp):
                def load(g, h, b):
                    kit.hold("sp", sp, (xm, g - 1))
                    sp.dma_start(tiles(XD[b]), edge_rows(k.tab[1], back(g), k.N)).then_inc(own_in[b], 16)

                def store(g, h, b):
                    kit.hold("sp", sp, (zed, g * G + G))
                    sp.dma_start(edge_rows(k.messages, back(g), 0), tiles(Z[b])).then_inc(stored[b], 16)

                steps(sp, k.NG, LAG, lambda at: rounds(at, [(0, load), (LAG, store)]))
                for b in range(2):
                    sp.wait_ge(stored[b], 16 * ((k.NG - b + 1) // 2))

            @block.tensor
            def _(pe):
                def turn_d(g, h, b):
                    pe.wait_ge(xm, g + 1)
                    need(pe, xdt, g)
                    turn(nc, k, B[1], XM[b], d_turned)

                def turn_s(g, h, b):
                    src_g.wait(pe, h, b)
                    need(pe, dft, g)
                    turn(nc, k, B[0], XS[b], s_turned)

                def scores(g, h, b):
                    pe.wait_ge(xdt, g + 1)
                    need(pe, taken, g)
                    for j in range(G):
                        last = nc.tensor.matmul(B[2][:, j * RH:(j + 1) * RH], XDT[b][:, j * T:(j + 1) * T], k.self_w[:, :],
                                                start=True, stop=True)
                    last.then_inc(s_mul, 1)

                def messages(g, h, b):
                    pe.wait_ge(dft, g + 1)
                    for j in range(G):
                        need(pe, zed, g * G + j - 3)
                        nc.tensor.matmul(B[3 + j][:, 0:R * D + RH], DFT[b][:, j * T:(j + 1) * T], k.w_cat[:, :],
                                         start=True, stop=True).then_inc(z_mul, 1)

                steps(pe, k.NG, LAG, lambda at: rounds(at, [(2, scores), (2, messages), (1, turn_d), (1, turn_s)]))

            @block.scalar
            def _(act):
                def mask(g, h, b):
                    need(act, xdt, g - 1)
                    nc.scalar.activation(NEXT[b][:, :], k.same[:, bass.ds(back(g) * W + 1, W)], ACT.Copy).then_inc(flags, 1)
                    need(act, d_turned, g - 1)
                    kit.hold("act", act, (own_in[b], (h + 1) * 16))
                    for j in range(G):
                        last = nc.scalar.activation(XM[b][:, j * T:(j + 1) * T], XD[b][:, j * T:(j + 1) * T], ACT.Copy,
                                                    scale=k.last_f[:, bass.ds(back(g) * G + j, 1)])
                    last.then_inc(xm, 1)

                def first(g, h, b):
                    for j in range(G):
                        n = g * G + j
                        kit.hold("act", act, (zed, n - 3), (z_mul, n + 1))
                        nc.scalar.activation(PART[j][:, :], B[3 + j][:, 0:D], ACT.Copy,
                                             scale=k.is_type[:, bass.ds(back(g) * G + j, 1), 0]).then_inc(z0, 1)

                steps(act, k.NG, LAG, lambda at: rounds(at, [(1, mask), (2, first)]))

            @block.vector
            def _(dve):
                v = nc.vector

                def flow_back(g, h, b):
                    need(dve, s_mul, g - 1)
                    need(dve, dft, g - 1)
                    need(dve, xdt, g)
                    dve.wait_ge(flags, g + 1)
                    dve.wait_ge(d_turned, g + 1)
                    first = isinstance(g, int) and g == 0
                    v.tensor_tensor_scan(XDT[b][:, ::-1], NEXT[b][:, ::-1], B[1][:, ::-1],
                                         0.0 if first else XDT[1 - b][:, 0:1], ALU.mult, ALU.add).then_inc(xdt, 1)

                def subtract(g, h, b):
                    need(dve, z_mul, (g - 1) * G)
                    dve.wait_ge(s_turned, g + 1)
                    dve.wait_ge(xdt, g + 1)
                    v.tensor_tensor(DFT[b][:, :], B[0][:, :], XDT[b][:, :], ALU.subtract).then_inc(dft, 1)

                def take(g, h, b):
                    kit.hold("dve", dve, (s_mul, g + 1))
                    v.tensor_copy(k.scores[:, bass.ds(back(g) * G, G), RH:2 * RH],
                                  B[2][:, 0:G * RH].rearrange("p (j n) -> p j n", j=G)).then_inc(taken, 1)

                def select(g, h, b):
                    if not (isinstance(h, int) and h <= 0):
                        dve.wait_ge(stored[b], h * 16)
                    for j in range(G):
                        n, tile = g * G + j, back(g) * G + j
                        kit.hold("dve", dve, (z0, n + 1))
                        v.scalar_tensor_tensor(PART[j][:, :], B[3 + j][:, D:2 * D], k.is_type[:, bass.ds(tile, 1), 1],
                                               PART[j][:, :], ALU.mult, ALU.add).then_inc(z1, 1)
                        kit.hold("dve", dve, (taken, g + 1))
                        v.tensor_tensor(k.scores[:, bass.ds(tile, 1), 0:RH],
                                        B[3 + j][:, R * D:R * D + RH].rearrange("p (a n) -> p a n", a=1),
                                        k.scores[:, bass.ds(tile, 1), RH:2 * RH], ALU.add).then_inc(scored, 1)
                        kit.hold("dve", dve, (z1, n + 1), (scored, n + 1))
                        v.scalar_tensor_tensor(Z[b][:, j * T:(j + 1) * T], B[3 + j][:, 2 * D:3 * D],
                                               k.is_type[:, bass.ds(tile, 1), 2], PART[j][:, :],
                                               ALU.mult, ALU.add).then_inc(zed, 1)

                steps(dve, k.NG, LAG, lambda at: rounds(at, [(2, take), (1, flow_back), (1, subtract), (2, select)]))


def attention(kit, k, M):
    nc = kit.nc
    CH = M * T
    with ExitStack() as ctx:
        def sb(name, shape, dt=F32):
            return kit.sb(name, shape, dt, ctx)

        rel = sb("at_rel", [T, k.NT, RH])
        off = sb("at_off", [T, k.NT])
        by_tile = sb("at_by_tile", [T, M, CHUNKS, RH])
        score = sb("at_score", [Q, CH])
        work = sb("at_work", [Q, CH])
        peak = sb("at_peak", [Q, CH])
        last = sb("at_last", [Q, CH], BF16)
        psum = [ctx.enter_context(nc.psum_tensor(f"at{i}", [T, 512], F32)) for i in range(8)]
        sc = Scans(kit, k, ctx, "ats", psum[7])
        chain, turned, took, act_in, act_out, out_mul, out_took = Chain(kit, "at_chain"), *(
            kit.sem(f"at_{n}") for n in ("turned", "took", "act_in", "act_out", "out_mul", "out_took"))

        with nc.Block() as block:
            @block.vector
            def _(dve):
                v, link = nc.vector, chain.on(dve)
                s = k.scores[:, :, :].rearrange("p t n -> p (t n)")
                link(v.scalar_tensor_tensor(s, s, 0.2, s, ALU.mult, ALU.max))
                link(v.tensor_tensor(rel[:, :, :], k.scores[:, :, 0:RH], k.scores[:, :, RH:2 * RH], ALU.subtract))
                for r in range(R):
                    mask = k.is_type[:, :, r]
                    link(v.tensor_scalar(off[:, :], mask, MASKED, -MASKED, ALU.mult, ALU.add))
                    part = rel[:, :, r * H:(r + 1) * H]
                    link(v.tensor_tensor(part, part, across(mask), ALU.mult))
                    link(v.tensor_tensor(by_tile[:, :, :, r * H:(r + 1) * H].rearrange("p j c n -> p c j n"),
                                         part.rearrange("p (c j) n -> p c j n", c=CHUNKS),
                                         across(off[:, :]).rearrange("p (c j) n -> p c j n", c=CHUNKS), ALU.add))

        with nc.Block() as block:
            @block.tensor
            def _(pe):
                for n in range(M // 4):
                    need(pe, took, n - 1)
                    for j in range(4):
                        ins = nc.tensor.transpose(psum[n % 2][0:Q, j * T:(j + 1) * T], by_tile[:, 4 * n + j, :, :].rearrange("p c n -> p (c n)"),
                                                  k.ident[:, :])
                    ins.then_inc(turned, 1)

            @block.vector
            def _(dve):
                for n in range(M // 4):
                    dve.wait_ge(turned, n + 1)
                    nc.vector.tensor_copy(score[:, n * 512:(n + 1) * 512], psum[n % 2][0:Q, :]).then_inc(took, 1)

        with nc.Block() as block:
            @block.tensor
            def _(pe):
                for _ in range(4):
                    sc.pe_scan(pe)

            @block.scalar
            def _(act):
                act.wait_ge(act_in, 1)
                nc.scalar.activation(score[:, :], score[:, :], ACT.Exp).then_inc(act_out, 1)
                nc.scalar.activation(peak[:, :], peak[:, :], ACT.Exp, scale=-1.0).then_inc(act_out, 1)

            @block.vector
            def _(dve):
                v, link = nc.vector, chain.on(dve)
                link(v.tensor_scalar(last[:, :], k.next84[:, :], -1.0, 1.0, ALU.mult, ALU.add))
                sc.scan(dve, link, work, score[:, :], k.same84[:, :], k.prod_f[:, :], k.flow_f, ALU.max, True)
                link(v.tensor_scalar(work[:, :], work[:, :], 0.0, None, ALU.max))
                link(v.tensor_tensor(work[:, :], work[:, :], last[:, :], ALU.mult))
                sc.scan(dve, link, peak, work[:, :], k.next84[:, :], k.prod_b[:, :], k.flow_b, ALU.add, False)
                v.tensor_tensor(score[:, :], score[:, :], peak[:, :], ALU.subtract).then_inc(act_in, 1)
                dve.wait_ge(act_out, 2)
                sc.scan(dve, link, work, score[:, :], k.same84[:, :], k.prod_f[:, :], k.flow_f, ALU.add, True)
                link(v.tensor_tensor(work[:, :], work[:, :], peak[:, :], ALU.add))
                link(v.tensor_tensor(work[:, :], work[:, :], last[:, :], ALU.mult))
                sc.scan(dve, link, peak, work[:, :], k.next84[:, :], k.prod_b[:, :], k.flow_b, ALU.add, False)
                link(v.reciprocal(peak[:, :], peak[:, :]))
                link(v.tensor_tensor(score[:, :], score[:, :], peak[:, :], ALU.mult))

        with nc.Block() as block:
            @block.tensor
            def _(pe):
                for n in range(M // 4):
                    need(pe, out_took, n - 1)
                    for j in range(4):
                        t = 4 * n + j
                        ins = nc.tensor.matmul(psum[n % 2][:, j * CHUNKS * H:(j + 1) * CHUNKS * H],
                                               score[:, t * T:(t + 1) * T], k.head_w[:, :], start=True, stop=True)
                    ins.then_inc(out_mul, 1)

            @block.vector
            def _(dve):
                beta = k.beta[:, :, :].rearrange("p (c j) h -> p j c h", c=CHUNKS)
                for n in range(M // 4):
                    dve.wait_ge(out_mul, n + 1)
                    p = psum[n % 2][:, 0:4 * CHUNKS * H].rearrange("p (j c h) -> p j c h", j=4, h=H)
                    for j in range(4):
                        ins = nc.vector.tensor_copy(beta[:, 4 * n + j, :, :], p[:, j, :, :])
                    ins.then_inc(out_took, 1)


def across(ap):
    return ap.rearrange("p (t a) -> p t a", a=1).to_broadcast([ap.shape[0], ap.shape[1], H])


def gat_combine(kit, k):
    nc = kit.nc
    LAG = 5
    name = "gb"
    with ExitStack() as ctx:
        def pair(n):
            return [kit.sb(f"{name}_{n}{b}", [T, W], F32, ctx) for b in range(2)]

        Z, V, XD, XDT, AG, Y, OUT, OUTN = (pair(n) for n in "Z V XD XDT AG Y OUT OUTN".split())
        B = [ctx.enter_context(nc.psum_tensor(f"{name}_bank{i}", [T, 512], F32)) for i in range(4)]
        norm = Spread(kit, ctx, f"{name}_sp")
        weighted, v_turned, d_turned, summed, xdt, mul, y, x2, scaled = (kit.sem(f"{name}_{n}") for n in (
            "weighted", "v_turned", "d_turned", "summed", "xdt", "mul", "y", "x2", "scaled"))
        z_in, x_in, stored, stored_n = ([kit.sem(f"{name}_{n}{b}") for b in range(2)] for n in (
            "z_in", "x_in", "stored", "stored_n"))

        with nc.Block() as block:
            @block.sync
            def _(sp):
                def load(g, h, b):
                    need(sp, weighted, g - 1)
                    sp.dma_start(tiles(Z[b]), edge_rows(k.messages, g, 0)).then_inc(z_in[b], 16)
                    need(sp, d_turned, g - 1)
                    sp.dma_start(tiles(XD[b]), edge_rows(k.tab[1], g, k.N)).then_inc(x_in[b], 16)

                def store(g, h, b):
                    sp.wait_ge(x2, g + 1)
                    sp.dma_start(edge_rows(k.x_own, g, 0), tiles(OUT[b])).then_inc(stored[b], 16)
                    sp.wait_ge(scaled, g + 1)
                    sp.dma_start(edge_rows(k.tab[2], g, k.N), tiles(OUTN[b])).then_inc(stored_n[b], 16)

                steps(sp, k.NG, LAG, lambda at: rounds(at, [(0, load), (LAG, store)]))
                for b in range(2):
                    sp.wait_ge(stored[b], 16 * ((k.NG - b + 1) // 2))
                    sp.wait_ge(stored_n[b], 16 * ((k.NG - b + 1) // 2))

            @block.tensor
            def _(pe):
                def turn_d(g, h, b):
                    pe.wait_ge(x_in[b], (h + 1) * 16)
                    need(pe, xdt, g)
                    turn(nc, k, B[1], XD[b], d_turned)

                def turn_v(g, h, b):
                    pe.wait_ge(weighted, g + 1)
                    need(pe, summed, g)
                    turn(nc, k, B[0], V[b], v_turned)

                def product(g, h, b):
                    pe.wait_ge(xdt, g + 1)
                    pe.wait_ge(summed, g + 1)
                    need(pe, y, g)
                    for j in range(G):
                        at = slice(j * T, (j + 1) * T)
                        nc.tensor.matmul(B[2][:, at], XDT[b][:, at], k.own_mix[:, :], start=True, stop=False)
                        last = nc.tensor.matmul(B[2][:, at], AG[b][:, at], k.centre[:, :], start=False, stop=True)
                    last.then_inc(mul, 1)

                steps(pe, k.NG, LAG, lambda at: rounds(at, [(3, product), (1, turn_d), (1, turn_v)]))

            @block.scalar
            def _(act):
                def copy_own(g, h, b):
                    need(act, mul, g - 1)
                    act.wait_ge(d_turned, g + 1)
                    nc.scalar.activation(XDT[b][:, :], B[1][:, :], ACT.Copy).then_inc(xdt, 1)

                def spread(g, h, b):
                    act.wait_ge(y, g + 1)
                    norm.on_act(act, k.eps[:, 0:1], lambda j: Y[b][:, j * D:(j + 1) * D], g, b)

                def scale_out(g, h, b):
                    if not (isinstance(h, int) and h <= 0):
                        act.wait_ge(stored_n[b], h * 16)
                    kit.hold("act", act, (x2, g + 1))
                    for j in range(G):
                        last = nc.scalar.activation(OUTN[b][:, j * T:(j + 1) * T], OUT[b][:, j * T:(j + 1) * T], ACT.Copy,
                                                    scale=k.norm[:, bass.ds(g * G + j, 1)])
                    last.then_inc(scaled, 1)

                steps(act, k.NG, LAG, lambda at: rounds(at, [
                    (1, copy_own), (3, spread), (4, scale_out)]))

            @block.vector
            def _(dve):
                v = nc.vector
                total = segment_sum(kit, k, dve, AG, [B[0]] * 2, v_turned, summed, lambda g: [(mul, g - 1)])

                def weigh(g, h, b):
                    need(dve, v_turned, g - 1)
                    kit.hold("dve", dve, (z_in[b], (h + 1) * 16))
                    beta = k.beta[:, bass.ds(g * G, G), :].rearrange("p t h -> p (t h)")
                    v.tensor_tensor(V[b][:, :].rearrange("p (q c) -> p q c", c=HD),
                                    Z[b][:, :].rearrange("p (q c) -> p q c", c=HD),
                                    beta.rearrange("p (q a) -> p q a", a=1).to_broadcast([T, G * H, HD]),
                                    ALU.mult).then_inc(weighted, 1)

                def add_bias(g, h, b):
                    need(dve, x2, g - 1)
                    dve.wait_ge(mul, g + 1)
                    v.tensor_tensor(tiles(Y[b]), tiles(B[2]), over(k.bbar_row), ALU.add).then_inc(y, 1)

                def scale(g, h, b):
                    if not (isinstance(h, int) and h <= 0):
                        dve.wait_ge(stored[b], h * 16)
                    need(dve, scaled, g - 1)
                    norm.invert(dve, g, b)
                    v.tensor_tensor(tiles(OUT[b]), tiles(Y[b]), wide(norm.rstd[b]), ALU.mult).then_inc(x2, 1)

                steps(dve, k.NG, LAG, lambda at: rounds(at, [(1, weigh), (3, add_bias), (4, scale), (1, total)]))


def gcn(kit, k):
    nc = kit.nc
    LAG = 4
    name = "gc"
    with ExitStack() as ctx:
        def pair(n):
            return [kit.sb(f"{name}_{n}{b}", [T, W], F32, ctx) for b in range(2)]

        XS, AG, XR, BASE, MIX, OUT = (pair(n) for n in "XS AG XR BASE MIX OUT".split())
        B = [ctx.enter_context(nc.psum_tensor(f"{name}_bank{i}", [T, 512], F32)) for i in range(2)]
        norm = Spread(kit, ctx, f"{name}_sp")
        src_g = Gather(kit, ctx, f"{name}_src", k.srcp_i, k.tab[2], XS)
        turned, summed, mul, base, mixed, x3 = (kit.sem(f"{name}_{n}") for n in ("turned", "summed", "mul", "base", "mixed", "x3"))
        x_in, stored = ([kit.sem(f"{name}_{n}{b}") for b in range(2)] for n in ("x_in", "stored"))

        with nc.Block() as block:
            @block.gpsimd
            def _(pool):
                steps(pool, k.NG, LAG, lambda at: rounds(at, [(0, src_g.stage(pool, lambda g, h, b: [(turned, g - 1)]))]))

            @block.sync
            def _(sp):
                def load(g, h, b):
                    need(sp, base, g - 1)
                    sp.dma_start(tiles(XR[b]), edge_rows(k.x_own, g, 0)).then_inc(x_in[b], 16)

                def store(g, h, b):
                    sp.wait_ge(x3, g + 1)
                    sp.dma_start(edge_rows(k.tab[3], g, k.N), tiles(OUT[b])).then_inc(stored[b], 16)

                steps(sp, k.NG, LAG, lambda at: rounds(at, [(1, load), (LAG, store)]))
                for b in range(2):
                    sp.wait_ge(stored[b], 16 * ((k.NG - b + 1) // 2))

            @block.tensor
            def _(pe):
                def turn_s(g, h, b):
                    src_g.wait(pe, h, b)
                    need(pe, summed, g)
                    turn(nc, k, B[0], XS[b], turned)

                def product(g, h, b):
                    pe.wait_ge(summed, g + 1)
                    need(pe, mixed, g)
                    multiply_rows(nc, B[1], AG[b], k.w2[:, :], mul)

                steps(pe, k.NG, LAG, lambda at: rounds(at, [(1, turn_s), (2, product)]))

            @block.scalar
            def _(act):
                def spread(g, h, b):
                    act.wait_ge(mixed, g + 1)
                    norm.on_act(act, k.eps[:, 0:1], lambda j: MIX[b][:, j * D:(j + 1) * D], g, b)

                steps(act, k.NG, LAG, lambda at: rounds(at, [(3, spread)]))

            @block.vector
            def _(dve):
                v = nc.vector
                total = segment_sum(kit, k, dve, AG, [B[0]] * 2, turned, summed, lambda g: [(mul, g - 1)])

                def add_bias(g, h, b):
                    need(dve, mixed, g - 1)
                    dve.wait_ge(x_in[b], (h + 1) * 16)
                    v.tensor_tensor(tiles(BASE[b]), tiles(XR[b]), over(k.b2_row), ALU.add).then_inc(base, 1)

                def mix(g, h, b):
                    need(dve, x3, g - 1)
                    kit.hold("dve", dve, (base, g + 1), (mul, g + 1))
                    for j in range(G):
                        last = v.scalar_tensor_tensor(MIX[b][:, j * T:(j + 1) * T], B[1][:, j * T:(j + 1) * T],
                                                      k.norm[:, bass.ds(g * G + j, 1)], BASE[b][:, j * T:(j + 1) * T],
                                                      ALU.mult, ALU.add)
                    last.then_inc(mixed, 1)

                def scale(g, h, b):
                    if not (isinstance(h, int) and h <= 0):
                        dve.wait_ge(stored[b], h * 16)
                    norm.invert(dve, g, b)
                    v.tensor_tensor(tiles(OUT[b]), tiles(MIX[b]), wide(norm.rstd[b]), ALU.mult).then_inc(x3, 1)

                steps(dve, k.NG, LAG, lambda at: rounds(at, [(2, add_bias), (2, mix), (1, total), (3, scale)]))


def gin(kit, k, edge_attr, out, E):
    nc = kit.nc
    LAG = 5
    name = "gi"
    A = edge_attr.shape[1]
    with ExitStack() as ctx:
        def pair(n, shape=(T, W), dt=F32):
            return [kit.sb(f"{name}_{n}{b}", list(shape), dt, ctx) for b in range(2)]

        XS, MS, AG, XD, XB, XDT, HT, MA, MB, Y, OUT = (pair(n) for n in "XS MS AG XD XB XDT HT MA MB Y OUT".split())
        ea_last = kit.sb(f"{name}_ea_last", [T, G, A], F32, ctx)
        EA, EAT, now = pair("EA", (T, G, A)), pair("EAT", (A, W)), pair("now", (T, G), I32)
        B = [ctx.enter_context(nc.psum_tensor(f"{name}_bank{i}", [T, 512], F32)) for i in range(8)]
        norm = Spread(kit, ctx, f"{name}_sp")
        src_g = Gather(kit, ctx, f"{name}_src", k.srcp_i, k.tab[3], XS)
        (e_clear, e_turned, eat, m_sum, ms, summed, d_turned, xdt, ht, xb, ma_mul, mb_mul, ma, mb, out_mul, y, x4,
         staged) = (kit.sem(f"{name}_{n}") for n in (
             "e_clear e_turned eat m_sum ms summed d_turned xdt ht xb ma_mul mb_mul ma mb out_mul y x4 staged"
         ).split())
        e_last = kit.sem(f"{name}_e_last")
        put = [kit.sem(f"{name}_put{b}", True) for b in range(2)]
        e_in, x_in = ([kit.sem(f"{name}_{n}{b}") for b in range(2)] for n in ("e_in", "x_in"))
        rest = E - (k.NG - 1) * W

        with nc.Block() as block:
            @block.gpsimd
            def _(pool):
                def put_rows(g, h, b):
                    waits = [(put[b], h * 16 * G)] if not (isinstance(h, int) and h <= 0) else []
                    kit.hold("pool", pool, *waits)
                    nc.gpsimd.tensor_copy(now[b][:, :], k.last_i[:, bass.ds(g * G, G)]).then_inc(staged, 1)
                    kit.hold("pool", pool, (staged, g + 1), (x4, g + 1))
                    for j in range(G):
                        pool.indirect_dma_start(out, bass.IndirectOffsetOnAxis(ap=now[b][:, j:j + 1], axis=0),
                                                OUT[b][:, j * T:(j + 1) * T], None, bounds_check=k.N - 1,
                                                oob_is_err=False).then_inc(put[b], 16)

                steps(pool, k.NG, LAG, lambda at: rounds(
                    at, [(1, src_g.stage(pool, lambda g, h, b: [(m_sum, g - 1)])), (LAG, put_rows)]))
                for b in range(2):
                    pool.wait_ge(put[b], 16 * G * ((k.NG - b + 1) // 2))

            @block.sync
            def _(sp):
                def load_e(g, h, b):
                    need(sp, e_turned, g - 1)
                    if isinstance(g, int) and g == k.NG - 1:
                        sp.wait_ge(e_clear, 1)
                        for j in range(-(-rest // T)):
                            n = min(T, rest - j * T)
                            sp.dma_start(ea_last[0:n, j, :], edge_attr[g * W + j * T:g * W + j * T + n, :]
                                         ).then_inc(e_last, 16)
                    else:
                        sp.dma_start(EA[b][:, :, :], edge_attr[bass.ds(g * W, W), :].rearrange(
                            "(j p) a -> p j a", p=T)).then_inc(e_in[b], 16)

                def load_x(g, h, b):
                    need(sp, d_turned, g - 1)
                    need(sp, xb, g - 1)
                    sp.dma_start(tiles(XD[b]), edge_rows(k.tab[3], g, k.N)).then_inc(x_in[b], 16)

                steps(sp, k.NG, LAG, lambda at: rounds(at, [(0, load_e), (2, load_x)]))

            @block.tensor
            def _(pe):
                def turn_e(g, h, b):
                    last_one = isinstance(g, int) and g == k.NG - 1
                    if last_one:
                        pe.wait_ge(e_last, 16 * -(-rest // T))
                    else:
                        pe.wait_ge(e_in[b], (h + 1) * 16)
                    rows = ea_last if last_one else EA[b]
                    need(pe, eat, g)
                    for j in range(G):
                        last = nc.tensor.transpose(B[0][0:A, j * T:(j + 1) * T], rows[:, j, :], k.ident[:, :])
                    last.then_inc(e_turned, 1)

                def message(g, h, b):
                    src_g.wait(pe, h, b)
                    pe.wait_ge(eat, g + 1)
                    need(pe, ms, g)
                    for j in range(G):
                        at = slice(j * T, (j + 1) * T)
                        nc.tensor.matmul(B[1][:, at], k.we[:, :], EAT[b][:, at], start=True, stop=False)
                        last = nc.tensor.matmul(B[1][:, at], XS[b][:, at], k.ident[:, :], start=False, stop=True)
                    last.then_inc(m_sum, 1)

                def turn_x(g, h, b):
                    pe.wait_ge(x_in[b], (h + 1) * 16)
                    need(pe, xdt, g)
                    turn(nc, k, B[2], XD[b], d_turned)

                def hidden(g, h, b):
                    pe.wait_ge(ht, g + 1)
                    need(pe, ma, g)
                    nc.tensor.matmul(B[3][:, :], k.wm1[:, 0:D], HT[b][:, :], start=True, stop=True).then_inc(ma_mul, 1)
                    need(pe, mb, g)
                    nc.tensor.matmul(B[4][:, :], k.wm1[:, D:2 * D], HT[b][:, :], start=True, stop=True).then_inc(mb_mul, 1)

                def project(g, h, b):
                    pe.wait_ge(ma, g + 1)
                    pe.wait_ge(mb, g + 1)
                    need(pe, y, g)
                    for j in range(G):
                        at = slice(j * T, (j + 1) * T)
                        nc.tensor.matmul(B[5][:, at], MA[b][:, at], k.wm2[:, 0, :], start=True, stop=False)
                        last = nc.tensor.matmul(B[5][:, at], MB[b][:, at], k.wm2[:, 1, :], start=False, stop=True)
                    last.then_inc(out_mul, 1)

                steps(pe, k.NG, LAG, lambda at: rounds(at, [
                    (3, turn_x), (4, hidden), (3, message), (4, project), (1, turn_e)]))

            @block.scalar
            def _(act):
                def turned_e(g, h, b):
                    need(act, m_sum, g - 1)
                    act.wait_ge(e_turned, g + 1)
                    nc.scalar.activation(EAT[b][:, :], B[0][0:A, :], ACT.Copy).then_inc(eat, 1)

                def relu_message(g, h, b):
                    need(act, summed, g - 1)
                    act.wait_ge(m_sum, g + 1)
                    nc.scalar.activation(MS[b][:, :], B[1][:, :], ACT.Relu, bias=k.be_col[:, 0:1]).then_inc(ms, 1)

                def copy_x(g, h, b):
                    need(act, ht, g - 1)
                    act.wait_ge(d_turned, g + 1)
                    nc.scalar.activation(XDT[b][:, :], B[2][:, :], ACT.Copy).then_inc(xdt, 1)

                def relu_hidden(n, m, mul, done):
                    def stage(g, h, b):
                        need(act, out_mul, g - 1)
                        act.wait_ge(mul, g + 1)
                        nc.scalar.activation(m[b][:, :], B[3 + n][:, :], ACT.Relu, bias=k.bn1_b[:, n:n + 1],
                                             scale=k.bn1_s[:, n:n + 1]).then_inc(done, 1)
                    return stage

                def spread(g, h, b):
                    act.wait_ge(y, g + 1)
                    norm.on_act(act, k.eps[:, 0:1], lambda j: Y[b][:, j * D:(j + 1) * D], g, b)

                steps(act, k.NG, LAG, lambda at: rounds(at, [
                    (4, relu_hidden(0, MA, ma_mul, ma)), (3, copy_x), (2, turned_e), (4, relu_hidden(1, MB, mb_mul, mb)),
                    (3, relu_message), (4, spread)]))

            @block.vector
            def _(dve):
                v = nc.vector
                total = segment_sum(kit, k, dve, AG, MS, ms, summed, lambda g: [(ht, g - 1)])
                v.memset(ea_last[:, :, :], 0.0).then_inc(e_clear, 1)

                def own(g, h, b):
                    need(dve, mb_mul, g - 1)
                    dve.wait_ge(xdt, g + 1)
                    dve.wait_ge(summed, g + 1)
                    v.scalar_tensor_tensor(HT[b][:, :], XDT[b][:, :], k.eps1[:, 0:1], AG[b][:, :],
                                           ALU.mult, ALU.add).then_inc(ht, 1)

                def bias_x(g, h, b):
                    dve.wait_ge(x_in[b], (h + 1) * 16)
                    need(dve, y, g - 1)
                    v.tensor_tensor(tiles(XB[b]), tiles(XD[b]), over(k.bn2_row), ALU.add).then_inc(xb, 1)

                def add_x(g, h, b):
                    dve.wait_ge(xb, g + 1)
                    need(dve, x4, g - 1)
                    dve.wait_ge(out_mul, g + 1)
                    v.tensor_tensor(Y[b][:, :], B[5][:, :], XB[b][:, :], ALU.add).then_inc(y, 1)

                def scale(g, h, b):
                    if not (isinstance(h, int) and h <= 0):
                        dve.wait_ge(put[b], h * 16 * G)
                    norm.invert(dve, g, b)
                    v.tensor_tensor(tiles(OUT[b]), tiles(Y[b]), wide(norm.rstd[b]), ALU.mult).then_inc(x4, 1)

                steps(dve, k.NG, LAG, lambda at: rounds(
                    at, [(3, bias_x), (3, total), (3, own), (4, add_x), (4, scale)]))


class Tensors:
    pass


def gnn(nc, x, src, dst, edge_attr, edge_type, ins, out, place, tabs, x_own, messages):
    N, E = x.shape[0], src.shape[0]
    M = 4 * -(-E // (CHUNKS * G * T))
    with ExitStack() as ctx:
        kit = Kit(nc, ctx)
        k = Tensors()
        k.N, k.NT = N, CHUNKS * M
        k.NG = k.NT // G
        k.place, k.tab, k.x_own, k.messages = place, tabs, x_own, messages
        CH = M * T
        sb = kit.sb
        k.eps, k.one, k.eps1 = sb("eps", [T, 1]), sb("one", [T, 1]), sb("eps1", [T, 1])
        k.ident = sb("ident", [T, T])
        k.chunk_of = sb("chunk_of", [CHUNKS, Q])
        k.one_chunk = sb("one_chunk", [CHUNKS, CHUNKS, T])
        k.head_sel = sb("head_sel", [Q, R, CHUNKS, H])
        k.head_w = sb("head_w", [Q, CHUNKS * H])
        k.rel = sb("rel", [T, R])
        k.wl1, k.wr1, k.wl2, k.wr2, k.w2, k.w_bar = (sb(n, [D, D]) for n in "wl1 wr1 wl2 wr2 w2 w_bar".split())
        k.centre, k.own_mix, k.pair_mix = sb("centre", [D, D]), sb("own_mix", [D, D]), sb("pair_mix", [D, 2 * D])
        k.w_cat, k.wm1, k.wm2 = sb("w_cat", [D, R * D + RH]), sb("wm1", [D, 2 * D]), sb("wm2", [D, 2, D])
        k.we = sb("we", [16, D])
        k.self_w = sb("self_w", [D, RH])
        k.bl1_row, k.bl2_row, k.b2_row, k.bbar_row, k.bn2_row = (
            sb(n, [T, D]) for n in "bl1_row bl2_row b2_row bbar_row bn2_row".split())
        k.bl1_col, k.bl2_col, k.be_col = (sb(n, [D, 1]) for n in "bl1_col bl2_col be_col".split())
        k.bn1_s, k.bn1_b, k.bn1_s_own = (sb(n, [D, 2]) for n in "bn1_s bn1_b bn1_s_own".split())
        k.src_i, k.dst_i, k.last_i, k.srcp_i, k.dstp_i, k.edge_row = (
            sb(n, [T, k.NT], I32) for n in "src_i dst_i last_i srcp_i dstp_i edge_row".split())
        k.type_f, k.last_f, k.deg, k.rdeg, k.norm = (sb(n, [T, k.NT]) for n in "type_f last_f deg rdeg norm".split())
        k.is_type = sb("is_type", [T, k.NT, R])
        k.same = sb("same", [T, k.NT * T + 1], BF16)
        k.same84, k.next84, k.prod_f, k.prod_b = (sb(n, [Q, CH], BF16) for n in "same84 next84 prod_f prod_b".split())
        k.flow_f, k.flow_b = (sb(n, [1, RH, CHUNKS]) for n in "flow_f flow_b".split())
        kit.place_clear = kit.sem("place_clear", True)

        prepare(kit, k, ins)
        kit.end_phase()
        index_stage(kit, k, src, dst, edge_type, N, E, M)
        kit.end_phase()
        first_pass(kit, k, x, out, x_own)
        kit.end_phase()
        sage(kit, k)
        kit.end_phase()
        with ExitStack() as gat:
            k.scores = sb("scores", [T, k.NT, 2 * RH], F32, gat)
            k.beta = sb("beta", [T, k.NT, H], F32, gat)
            gat_messages(kit, k)
            kit.end_phase()
            attention(kit, k, M)
            kit.end_phase()
            gat_combine(kit, k)
            kit.end_phase()
        gcn(kit, k)
        kit.end_phase()
        gin(kit, k, edge_attr, out, E)


_DATA = ("x", "src", "dst", "edge_attr_16", "edge_type_3")


def kernel(**inputs):
    import numpy as np
    import concourse.bacc as bacc
    from concourse.bass_utils import run_bass_kernel_spmd as run

    nc = bacc.Bacc("TRN2", target_bir_lowering=False, num_devices=1)
    arrays = {name: np.ascontiguousarray(a) for name, a in inputs.items()}
    args = {name: nc.dram_tensor(name, a.shape, mybir.dt.from_np(a.dtype), kind="ExternalInput").ap()
            for name, a in arrays.items()}
    N, E = arrays["x"].shape[0], arrays["src"].shape[0]
    EP = CHUNKS * G * T * -(-E // (CHUNKS * G * T))
    out = nc.dram_tensor("out", (N, D), F32, kind="ExternalOutput").ap()
    place = nc.dram_tensor("place", (N, 1), I32).ap()
    tabs = [nc.dram_tensor(f"tab{i}", (N + EP, D), F32).ap() for i in range(4)]
    x_own = nc.dram_tensor("x_own", (EP, D), F32).ap()
    messages = nc.dram_tensor("messages", (EP, D), F32).ap()
    gnn(nc, *(args[n] for n in _DATA), {n: a for n, a in args.items() if n not in _DATA}, out, place, tabs,
        x_own, messages)
    return run(nc, [arrays], core_ids=[0]).results[0]["out"]
```

```python
from contextlib import ExitStack

import concourse.bass as bass
from concourse import mybir

F32 = mybir.dt.float32
I32 = mybir.dt.int32
BF16 = mybir.dt.bfloat16
ALU = mybir.AluOpType
ACT = mybir.ActivationFunctionType
AX_X = mybir.AxisListType.X

D = 128
T = 128
G = 4
W = G * T
CHUNKS = 7
R, H = 3, 4
RH = R * H
HD = D // H
Q = CHUNKS * RH
FAR = float(1 << 20)
MASKED = 1.0e9
LN_EPS = 1e-5
BN_EPS = 1e-3


def steps(eng, groups, lag, body):
    def fixed(s):
        def at(k):
            g = s - k
            return (g, g // 2, g % 2) if 0 <= g < groups else None
        return at

    first = lag + 2 + (lag % 2)
    pairs = (groups - 1 - first) // 2
    if pairs < 2:
        for s in range(groups + lag):
            body(fixed(s))
        return
    for s in range(first):
        body(fixed(s))
    with eng.Fori(0, pairs) as i:
        for u in range(2):
            def at(k, u=u):
                c = first + u - k
                return i * 2 + c, i + c // 2, c % 2
            body(at)
    for s in range(first + 2 * pairs, groups + lag):
        body(fixed(s))


def rounds(at, *table):
    for line in table:
        for lag, stage in line:
            g = at(lag)
            if g is not None:
                stage(*g)


class Kit:

    def __init__(self, nc, ctx):
        self.nc, self.ctx = nc, ctx
        self.passing = []
        self.held = {n: ctx.enter_context(nc.semaphore(f"held_{n}")) for n in ("pe", "act", "dve", "pool", "sp")}

    def sb(self, name, shape, dt=F32, ctx=None):
        return (ctx or self.ctx).enter_context(self.nc.sbuf_tensor(name, shape, dt))

    def sem(self, name, lasting=False):
        if lasting:
            return self.ctx.enter_context(self.nc.semaphore(name))
        self.passing.append(self.nc.alloc_semaphore(name=name))
        return self.passing[-1]

    def end_phase(self):
        sems, self.passing = self.passing, []
        with self.nc.Block() as block:
            @block.gpsimd
            def _(pool):
                self.nc.clear_and_free_semaphores(sems)

    def hold(self, name, eng, *waits):
        for sem, value in waits:
            if isinstance(value, int) and value <= 0:
                continue
            eng.wait_ge(sem, value)
            if not isinstance(value, int):
                eng.sem_inc(self.held[name], 1)


def need(eng, sem, value):
    if not (isinstance(value, int) and value <= 0):
        eng.wait_ge(sem, value)


class Norm:

    def __init__(self, kit, ctx, name):
        self.kit, self.name = kit, name
        self.stats = kit.sb(f"{name}_stats", [T, G, 6], ctx=ctx)
        self.mv = [kit.sb(f"{name}_mv{b}", [T, G, 2], ctx=ctx) for b in range(2)]
        self.std = [kit.sb(f"{name}_std{b}", [T, G], ctx=ctx) for b in range(2)]
        self.rstd, self.shift = ([kit.sb(f"{name}_{n}{b}", [T, G], ctx=ctx) for b in range(2)] for n in ("rstd", "shift"))
        self.counted = kit.sem(f"{name}_counted")
        self.moments = kit.sem(f"{name}_moments")
        self.rooted = kit.sem(f"{name}_rooted")
        self.inverted = kit.sem(f"{name}_inverted")
        self.done = kit.sem(f"{name}_done")

    def bn_moments(self, dve, x, g, b):
        nc = self.kit.nc
        need(dve, self.moments, g)
        need(dve, self.inverted, 2 * g - 2)
        for j in range(G):
            last = nc.vector.bn_stats(self.stats[:, j, :], x[:, j, :])
        last.then_inc(self.counted, 1)
        self.kit.hold("dve", dve, (self.counted, g + 1))
        for j in range(G):
            last = nc.vector.bn_aggr(self.mv[b][:, j, :], self.stats[:, j, :])
        last.then_inc(self.moments, 1)

    def root(self, act, eps, g, b):
        act.wait_ge(self.moments, g + 1)
        self.kit.nc.scalar.activation(self.std[b][:, :], self.mv[b][:, :, 1], ACT.Sqrt,
                                      bias=eps).then_inc(self.rooted, 1)

    def invert(self, dve, g, b):
        nc = self.kit.nc
        need(dve, self.done, g - 1)
        dve.wait_ge(self.rooted, g + 1)
        nc.vector.reciprocal(self.rstd[b][:, :], self.std[b][:, :]).then_inc(self.inverted, 1)
        dve.wait_ge(self.inverted, 2 * g + 1)
        nc.vector.scalar_tensor_tensor(self.shift[b][:, :], self.mv[b][:, :, 0], -1.0, self.rstd[b][:, :],
                                       ALU.mult, ALU.mult).then_inc(self.inverted, 1)

    def scale(self, act, out, x, g, b):
        act.wait_ge(self.inverted, 2 * g + 2)
        for j in range(G):
            last = self.kit.nc.scalar.activation(out[:, j, :], x[:, j, :], ACT.Identity, bias=self.shift[b][:, j:j + 1],
                                                 scale=self.rstd[b][:, j:j + 1])
        last.then_inc(self.done, 1)


def tiles(buf):
    return buf[:, :].rearrange("p (j d) -> p j d", j=G)


def prepare(kit, k, ins, raw, index_loads, compare):
    nc = kit.nc
    with ExitStack() as ctx:
        def sb(name, shape, dt=F32):
            return kit.sb(name, shape, dt, ctx)

        W = sb("w_cat_loose", [D, R, D])
        att = sb("att", [T, 2, R * D])
        prod = sb("att_prod", [T, R, D])
        a_dst = sb("a_dst", [D, RH])
        bias_r = sb("bias_r", [R, D])
        we1 = sb("we1", [16, 2 * D])
        we1t = sb("we1t", [D, 2, 16])
        we2 = sb("we2", [D, 2, D])
        be1 = sb("be1", [D, 2])
        be2 = sb("be2", [D, 1])
        relw = sb("relw", [T, R])
        relw3 = sb("relw3", [R, D])
        mix = sb("mix", [D, 3, D])
        sums = sb("sums", [T, 2])
        tmp = sb("tmp", [T, 16])
        part = sb("bias_part", [T, D], BF16)
        left = sb("bias_left", [T, D])
        chunk_of = sb("chunk_of_f", [CHUNKS, Q])
        one_chunk = sb("one_chunk_f", [CHUNKS, CHUNKS, T])
        colm = sb("colm", [D, 6, 2])
        row2 = sb("row2", [T, 6, D])
        P0 = ctx.enter_context(nc.psum_tensor("prep0", [T, 512], F32))
        P1 = ctx.enter_context(nc.psum_tensor("prep1", [T, 512], F32))
        P2 = ctx.enter_context(nc.psum_tensor("prep2", [T, 512], F32))
        loaded, made, chain, turned, folded, rooted, masks, raw_cleared, indices_in = (kit.sem(f"prep_{n}") for n in (
            "loaded", "made", "chain", "turned", "folded", "rooted", "masks", "raw_cleared", "indices_in"))
        loads = []

        def col(ap):
            return ap.rearrange("(p a) -> p a", a=1)

        def bcast(ap, n):
            return ap.rearrange("(a n) -> a n", a=1).to_broadcast([T, n])

        loads += [(k.wl1, ins["L0_gnn_Wl1"]), (k.wr1, ins["L0_gnn_Wr1"]), (k.wl2, ins["L0_gnn_Wl2"]),
                  (k.wr2, ins["L0_gnn_Wr2"]), (k.w2, ins["L2_gnn_weight"]), (k.wm1, ins["L3_gnn_Wm1"]),
                  (we1, ins["L3_gnn_We1"])]
        loads = [(a[:, :], b) for a, b in loads]
        loads += [(W[:, :, :], ins["L1_gnn_W"].rearrange("r k n -> k r n")),
                  (k.wm2[:, :, :], ins["L3_gnn_Wm2"].rearrange("(a k) n -> k a n", a=2)),
                  (we2[:, :, :], ins["L3_gnn_We2"].rearrange("(a k) n -> k a n", a=2)),
                  (bias_r[:, :], ins["L1_gnn_bias"]),
                  (relw[:, :], bcast(ins["L1_gnn_rel_w"], R)),
                  (k.eps1[:, :], bcast(ins["L3_gnn_eps"], 1)),
                  (k.bl1_col[:, :], col(ins["L0_gnn_bl1"])), (k.bl2_col[:, :], col(ins["L0_gnn_bl2"])),
                  (be2[:, :], col(ins["L3_gnn_be2"])),
                  (be1[:, :], ins["L3_gnn_be1"].rearrange("(a p) -> p a", a=2)),
                  (k.bl1_row[:, :], bcast(ins["L0_gnn_bl1"], D)), (k.bl2_row[:, :], bcast(ins["L0_gnn_bl2"], D)),
                  (k.b2_row[:, :], bcast(ins["L2_gnn_bias"], D)),
                  (att[:, 0, :], bcast(ins["L1_gnn_att_src"].rearrange("r h c -> (r h c)"), R * D)),
                  (att[:, 1, :], bcast(ins["L1_gnn_att_dst"].rearrange("r h c -> (r h c)"), R * D))]
        for n, name in enumerate(("bm1", "g1", "b1", "m1", "v1")):
            loads.append((colm[:, n, :], ins[f"L3_gnn_{name}"].rearrange("(a p) -> p a", a=2)))
        for n, name in enumerate(("bm2", "g2", "b2", "m2", "v2")):
            loads.append((row2[:, n, :], bcast(ins[f"L3_gnn_{name}"], D)))

        with nc.Block() as block:
            @block.sync
            def _(sp):
                with nc.allow_non_contiguous_dma(reason="per-feature vectors, one value to a partition"):
                    for dst, src in loads:
                        sp.dma_start(dst, src).then_inc(loaded, 16)

            @block.gpsimd
            def _(pool):
                nc.gpsimd.memset(k.ident[:, :], 0.0).then_inc(masks, 1)
                nc.gpsimd.memset(chunk_of[:, :], 1.0).then_inc(masks, 1)
                nc.gpsimd.memset(one_chunk[:, :, :], 0.0).then_inc(masks, 1)
                nc.gpsimd.memset(k.head_sel[:, :, :, :], 0.0).then_inc(masks, 1)
                pool.wait_ge(masks, 4)
                nc.gpsimd.affine_select(out=k.ident[:, :], in_=k.ident[:, :], compare_op=ALU.not_equal, fill=1.0,
                                        base=0, pattern=[[-1, T]], channel_multiplier=1).then_inc(made, 1)
                nc.gpsimd.affine_select(out=chunk_of[:, :], in_=chunk_of[:, :], compare_op=ALU.is_ge, fill=0.0,
                                        base=0, pattern=[[1, Q]], channel_multiplier=-RH).then_inc(masks, 1)
                pool.wait_ge(masks, 5)
                nc.gpsimd.affine_select(out=chunk_of[:, :], in_=chunk_of[:, :], compare_op=ALU.is_ge, fill=0.0,
                                        base=RH - 1, pattern=[[-1, Q]], channel_multiplier=RH).then_inc(made, 1)
                nc.gpsimd.affine_select(out=one_chunk[:, :, :], in_=one_chunk[:, :, :],
                                        compare_op=ALU.not_equal, fill=1.0, base=0,
                                        pattern=[[-1, CHUNKS], [0, T]], channel_multiplier=1).then_inc(made, 1)
                for r in range(R):
                    nc.gpsimd.affine_select(out=k.head_sel[:, r, :, :], in_=k.head_sel[:, r, :, :],
                                            compare_op=ALU.not_equal, fill=1.0, base=-H * r,
                                            pattern=[[-RH, CHUNKS], [-1, H]], channel_multiplier=1).then_inc(made, 1)

            @block.scalar
            def _(act):
                act.wait_ge(raw_cleared, 1)
                with nc.allow_non_contiguous_dma(reason="the neighbours of chunks, one value to a partition"):
                    for dst, src in index_loads:
                        act.dma_start(dst, src).then_inc(indices_in, 16)
                act.wait_ge(folded, 1)
                nc.scalar.activation(tmp[:, 0:R], tmp[:, 4:4 + R], ACT.Exp).then_inc(rooted, 1)
                act.wait_ge(folded, 2)
                nc.scalar.activation(colm[:, 5, :], colm[:, 4, :], ACT.Sqrt).then_inc(rooted, 1)
                nc.scalar.activation(row2[:, 5, :], row2[:, 4, :], ACT.Sqrt).then_inc(rooted, 1)

            @block.tensor
            def _(pe):
                pe.wait_ge(loaded, 16 * len(loads))
                pe.wait_ge(made, 3 + R)
                for a in range(2):
                    last = nc.tensor.transpose(P0[:, 16 * a:16 * a + 16], we1[:, a * D:(a + 1) * D],
                                               k.ident[0:16, 0:16])
                last.then_inc(turned, 1)
                pe.wait_ge(folded, 3)
                for a in range(2):
                    nc.tensor.matmul(P1[0:16, 0:D], we1t[:, a, :], we2[:, a, :], start=a == 0, stop=a == 1)
                for a in range(2):
                    last = nc.tensor.matmul(P2[:, 0:1], we2[:, a, :], be1[:, a:a + 1], start=a == 0, stop=a == 1)
                last.then_inc(turned, 1)
                pe.wait_ge(folded, 4)
                nc.tensor.matmul(P0[:, 64:64 + D], relw3[:, :], bias_r[:, :], start=True, stop=True)
                nc.tensor.matmul(P0[:, 256:256 + D], k.centre[:, :], mix[:, 0, :], start=True, stop=True)
                nc.tensor.transpose(P0[:, 384:384 + D], mix[:, 0, :], k.ident[:, :]).then_inc(turned, 1)
                pe.wait_ge(folded, 5)
                nc.tensor.transpose(P1[:, 0:D], mix[:, 1, :], k.ident[:, :])
                nc.tensor.matmul(P1[:, D:2 * D], mix[:, 2, :], k.centre[:, :], start=True, stop=True).then_inc(turned, 1)
                pe.wait_ge(folded, 6)
                nc.tensor.matmul(P1[:, 2 * D:3 * D], mix[:, 0, :], k.centre[:, :], start=True, stop=True).then_inc(turned, 1)

            @block.vector
            def _(dve):
                count = [0]

                def link(ins):
                    count[0] += 1
                    ins.then_inc(chain, 1)
                    dve.wait_ge(chain, count[0])

                pad = k.E - (CHUNKS - 1) * (raw.shape[1] - 2) + 1
                link(nc.vector.memset(raw[:, :], 0))
                for base in (0, 96):
                    link(nc.vector.memset(raw[base:base + CHUNKS, 0:1], -1))
                    link(nc.vector.memset(raw[base:base + CHUNKS, pad:-1], k.N))
                    ins = nc.vector.memset(raw[base:base + CHUNKS, -1:], k.N + 1)
                    if base == 0:
                        link(ins)
                ins.then_inc(raw_cleared, 1)
                link(nc.vector.memset(k.eps[:, :], LN_EPS))
                link(nc.vector.memset(k.one[:, :], 1.0))
                dve.wait_ge(indices_in, 16 * len(index_loads))
                compare(nc.vector, link)
                dve.wait_ge(loaded, 16 * len(loads))
                link(nc.vector.reduce_max(tmp[:, 3:4], relw[:, :], AX_X))
                nc.vector.tensor_scalar(tmp[:, 4:4 + R], relw[:, :], tmp[:, 3:4], None,
                                        ALU.subtract).then_inc(folded, 1)
                dve.wait_ge(rooted, 1)
                link(nc.vector.reduce_sum(tmp[:, 8:9], tmp[:, 0:R], AX_X))
                link(nc.vector.reciprocal(tmp[:, 9:10], tmp[:, 8:9]))
                link(nc.vector.tensor_scalar(k.rel[:, :], tmp[:, 0:R], tmp[:, 9:10], None, ALU.mult))
                link(nc.vector.tensor_scalar(colm[:, 4, :], colm[:, 4, :], BN_EPS, None, ALU.add))
                nc.vector.tensor_scalar(row2[:, 4, :], row2[:, 4, :], BN_EPS, None, ALU.add).then_inc(folded, 1)
                link(nc.vector.tensor_copy(k.w_cat[:, 0:R * D].rearrange("k (r n) -> k r n", r=R), W[:, :, :]))
                link(nc.vector.tensor_scalar(k.w_bar[:, :], W[:, 0, :], k.rel[:, 0:1], None, ALU.mult))
                for r in range(1, R):
                    link(nc.vector.scalar_tensor_tensor(k.w_bar[:, :], W[:, r, :], k.rel[:, r:r + 1],
                                                        k.w_bar[:, :], ALU.mult, ALU.add))
                a_src = k.w_cat[:, R * D:R * D + RH]
                for s, out in ((0, a_src), (1, a_dst[:, :])):
                    link(nc.vector.tensor_tensor(prod[:, :, :], W[:, :, :],
                                                 att[:, s, :].rearrange("p (r d) -> p r d", r=R), ALU.mult))
                    link(nc.vector.reduce_sum(out, prod[:, :, :].rearrange("p r (h c) -> p (r h) c", h=H), AX_X))
                link(nc.vector.tensor_tensor(k.self_w[:, :], a_src, a_dst[:, :], ALU.add))
                dve.wait_ge(turned, 1)
                nc.vector.tensor_copy(we1t[:, :, :], P0[:, 0:32].rearrange("p (a n) -> p a n", a=2)).then_inc(folded, 1)
                dve.wait_ge(turned, 2)
                link(nc.vector.tensor_copy(k.we[:, :], P1[0:16, 0:D]))
                link(nc.vector.tensor_tensor(k.be_col[:, :], P2[:, 0:1], be2[:, :], ALU.add))
                dve.wait_ge(made, 3 + R)
                link(nc.vector.tensor_copy(k.chunk_of[:, :], chunk_of[:, :]))
                link(nc.vector.tensor_copy(k.one_chunk[:, :, :], one_chunk[:, :, :]))
                link(nc.vector.tensor_tensor(tmp[0:R, 12:12 + R], k.rel[0:R, :], k.ident[0:R, 0:R], ALU.mult))
                link(nc.vector.reduce_sum(tmp[0:R, 15:16], tmp[0:R, 12:12 + R], AX_X))
                link(nc.vector.memset(relw3[:, :], 1.0))
                link(nc.vector.tensor_scalar(relw3[:, :], relw3[:, :], tmp[0:R, 15:16], None, ALU.mult))
                link(nc.vector.tensor_scalar(k.centre[:, :], k.ident[:, :], -1.0 / D, None, ALU.add))
                link(nc.vector.tensor_tensor(mix[:, 0, :], k.ident[:, :], k.w_bar[:, :], ALU.add))
                for rows, n in ((k.b2_row, T), (bias_r, R)):
                    link(nc.vector.reduce_sum(sums[0:n, 0:1], rows[:, :], AX_X))
                    link(nc.vector.tensor_scalar(sums[0:n, 1:2], sums[0:n, 0:1], -1.0 / D, None, ALU.mult))
                    ins = nc.vector.tensor_scalar(rows[:, :], rows[:, :], sums[0:n, 1:2], None, ALU.add)
                    if rows is k.b2_row:
                        link(ins)
                ins.then_inc(folded, 1)
                dve.wait_ge(turned, 3)
                link(nc.vector.tensor_copy(k.bbar_row[:, :], P0[:, 64:64 + D]))
                link(nc.vector.tensor_copy(mix[:, 1, :], P0[:, 256:256 + D]))
                nc.vector.tensor_copy(mix[:, 2, :], P0[:, 384:384 + D]).then_inc(folded, 1)
                dve.wait_ge(turned, 4)
                link(nc.vector.tensor_copy(k.own_mix[:, :], P1[:, D:2 * D]))
                nc.vector.tensor_copy(mix[:, 0, :], P1[:, 0:D]).then_inc(folded, 1)
                dve.wait_ge(turned, 5)
                link(nc.vector.tensor_copy(k.pair_mix[:, D:2 * D], P1[:, 2 * D:3 * D]))
                link(nc.vector.tensor_copy(k.pair_mix[:, 0:D], k.centre[:, :]))
                link(nc.vector.memset(k.ones[:, :], 1.0))
                for row, parts in ((k.bl2_row, k.bl2_parts), (k.bbar_row, k.bbar_parts)):
                    link(nc.vector.tensor_copy(left[:, :], row[:, :]))
                    for i in range(3):
                        link(nc.vector.tensor_copy(part[:, :], left[:, :]))
                        if i == 0:
                            link(nc.vector.tensor_scalar(parts[:, 0, :], part[:, :], k.ident[:, 0:1], None, ALU.mult))
                        else:
                            link(nc.vector.scalar_tensor_tensor(parts[:, 0, :], part[:, :], k.ident[:, i:i + 1],
                                                                parts[:, 0, :], ALU.mult, ALU.add))
                        if i < 2:
                            link(nc.vector.tensor_tensor(left[:, :], left[:, :], part[:, :], ALU.subtract))
                    for j in range(1, G):
                        nc.vector.tensor_copy(parts[:, j, :], parts[:, 0, :])
                hw = k.head_w[:, :].rearrange("q (c h) -> q c h", h=H)
                link(nc.vector.tensor_scalar(hw, k.head_sel[:, 0, :, :], k.rel[0:Q, 0:1], None, ALU.mult))
                for r in range(1, R):
                    link(nc.vector.scalar_tensor_tensor(hw, k.head_sel[:, r, :, :], k.rel[0:Q, r:r + 1], hw,
                                                        ALU.mult, ALU.add))
                dve.wait_ge(rooted, 3)
                link(nc.vector.tensor_scalar(k.eps1[:, :], k.eps1[:, :], 1.0, None, ALU.add))
                for cc, scale, bias in ((lambda n: colm[:, n, :], k.bn1_s[:, :], k.bn1_b[:, :]),
                                        (lambda n: row2[:, n, :], row2[:, 1, :], k.bn2_row[:, :])):
                    link(nc.vector.reciprocal(cc(5), cc(5)))
                    link(nc.vector.tensor_tensor(scale, cc(5), cc(1), ALU.mult))
                    link(nc.vector.tensor_tensor(cc(0), cc(0), cc(3), ALU.subtract))
                    link(nc.vector.tensor_tensor(cc(0), cc(0), scale, ALU.mult))
                    link(nc.vector.tensor_tensor(bias, cc(0), cc(2), ALU.add))
                for a in range(2):
                    link(nc.vector.tensor_tensor(k.wm2[:, a, :], k.wm2[:, a, :], row2[:, 1, :], ALU.mult))
                for rows in (k.w2[:, :], k.wm2[:, 0, :], k.wm2[:, 1, :], k.bn2_row[:, :]):
                    link(nc.vector.reduce_sum(sums[:, 0:1], rows, AX_X))
                    link(nc.vector.tensor_scalar(sums[:, 1:2], sums[:, 0:1], -1.0 / D, None, ALU.mult))
                    link(nc.vector.tensor_scalar(rows, rows, sums[:, 1:2], None, ALU.add))
                link(nc.vector.tensor_scalar(k.bn1_s_own[:, :], k.bn1_s[:, :], k.eps1[:, 0:1], None, ALU.mult))


class Scans:

    def __init__(self, kit, k, ctx, name, psum):
        self.kit, self.k, self.nc = kit, k, kit.nc
        self.row = kit.sb(f"{name}_row", [1, RH, CHUNKS], ctx=ctx)
        self.into = kit.sb(f"{name}_into", [1, CHUNKS, RH], ctx=ctx)
        self.carry = kit.sb(f"{name}_carry", [Q, 1], ctx=ctx)
        self.end = kit.sb(f"{name}_end", [Q, 1], ctx=ctx)
        self.turn, self.back = psum[0:1, 0:Q], psum[0:Q, 128:129]
        self.end_ready, self.turned, self.into_ready, self.returned = (
            kit.sem(f"{name}_{n}") for n in ("end_ready", "turned", "into_ready", "returned"))
        self.dve_n = self.pe_n = 0

    def pe_row(self, pe):
        self.pe_n += 1
        pe.wait_ge(self.end_ready, self.pe_n)
        self.nc.tensor.transpose(self.turn, self.end[:, :], self.k.ident[0:Q, 0:Q]).then_inc(self.turned, 1)

    def pe_scan(self, pe):
        self.pe_row(pe)
        pe.wait_ge(self.into_ready, self.pe_n)
        self.nc.tensor.matmul(self.back, self.into[:, :, :].rearrange("p c r -> p (c r)"), self.k.one[0:1, 0:1],
                              start=True, stop=True).then_inc(self.returned, 1)

    def gather_row(self, dve, link, src, forward):
        self.dve_n += 1
        self.nc.vector.tensor_copy(self.end[:, :], src).then_inc(self.end_ready, 1)
        dve.wait_ge(self.turned, self.dve_n)
        turned = self.turn.rearrange("p (c r) -> p r c", r=RH)
        for c in range(CHUNKS):
            s = c if forward else CHUNKS - 1 - c
            last = self.nc.vector.tensor_copy(self.row[:, :, c:c + 1], turned[:, :, s:s + 1])
        link(last)

    def flags_row(self, dve, link, product, out, forward):
        edge = product[:, -1:] if forward else product[:, 0:1]
        self.gather_row(dve, link, edge, forward)
        link(self.nc.vector.tensor_copy(out[:, :, :], self.row[:, :, :]))
        link(self.nc.vector.memset(out[:, :, 0:1], 0.0))
        self.nc.vector.memset(self.into[:, :, :], 0.0).then_inc(self.into_ready, 1)
        dve.wait_ge(self.returned, self.dve_n)

    def scan(self, dve, link, out, data, flags, product, flags_row, op, forward):
        vec = self.nc.vector
        n = out.shape[1]
        if forward:
            link(vec.tensor_tensor_scan(out[:, :], flags, data, 0.0, ALU.mult, op))
        else:
            link(vec.tensor_tensor_scan(out[:, ::-1], flags[:, ::-1], data[:, ::-1], 0.0, ALU.mult, op))
        self.gather_row(dve, link, out[:, n - 1:n] if forward else out[:, 0:1], forward)
        row = self.row[:, :, :].rearrange("p r c -> p (r c)")
        link(vec.tensor_tensor_scan(row, flags_row[:, :, :].rearrange("p r c -> p (r c)"), row, 0.0, ALU.mult, op))
        link(vec.memset(self.into[:, :, :], 0.0))
        for c in range(1, CHUNKS):
            d = c if forward else CHUNKS - 1 - c
            last = vec.tensor_copy(self.into[:, d:d + 1, :].rearrange("p c r -> p r c"), self.row[:, :, c - 1:c])
        last.then_inc(self.into_ready, 1)
        dve.wait_ge(self.returned, self.dve_n)
        link(vec.tensor_copy(self.carry[:, :], self.back))
        link(vec.scalar_tensor_tensor(out[:, :], product, self.carry[:, 0:1], out[:, :], ALU.mult, op))


class Chain:

    def __init__(self, kit, name):
        self.sem, self.count = kit.sem(name), 0

    def on(self, eng):
        def link(ins):
            self.count += 1
            ins.then_inc(self.sem, 1)
            eng.wait_ge(self.sem, self.count)
        return link


def turn_rows(kit, k, name, psum, src, parts, M, take):
    nc = kit.nc
    turned, took = kit.sem(f"{name}_turned"), kit.sem(f"{name}_took")
    with nc.Block() as block:
        @block.tensor
        def _(pe):
            for n in range(M // 4):
                need(pe, took, n - 1)
                for j in range(4):
                    t = 4 * n + j
                    last = nc.tensor.transpose(psum[n % 2][:, j * T:j * T + parts], src[:, t * T:(t + 1) * T],
                                               k.ident[0:parts, 0:parts])
                last.then_inc(turned, 1)

        @block.vector
        def _(dve):
            for n in range(M // 4):
                dve.wait_ge(turned, n + 1)
                take(n, psum[n % 2][:, :].rearrange("p (j q) -> p j q", j=4)).then_inc(took, 1)


def by_chunk(rows):
    return rows[:, :].rearrange("p (c j) -> p j c", c=CHUNKS)


def index_loads(raw, src, dst, etype, E, CH):
    full, rest = E // CH, E % CH
    loads = []
    for base, a in ((0, dst), (96, dst), (32, src), (64, etype)):
        whole = a[0:full * CH].rearrange("(c n) -> c n", n=CH)
        tail = a[full * CH:E].rearrange("(a n) -> a n", a=1)
        loads.append((raw[base:base + full, 1:CH + 1], whole))
        if rest:
            loads.append((raw[base + full:base + full + 1, 1:rest + 1], tail))
        if a is dst:
            followed = full if rest else full - 1
            loads.append((raw[base + 1:base + 1 + followed, 0:1], whole[0:followed, CH - 1:CH]))
            loads.append((raw[base:base + full - 1, CH + 1:CH + 2], whole[1:full, 0:1]))
            if rest:
                loads.append((raw[base + full - 1:base + full, CH + 1:CH + 2], tail[:, 0:1]))
    return loads


def compare_neighbours(k, raw, val, equal, link, vec):
    n = raw.shape[1] - 1
    link(vec.tensor_copy(val[:, :], raw[:, :]))
    link(vec.tensor_tensor(equal[:, :], val[:, 0:n], val[:, 1:n + 1], ALU.is_equal))
    last = val[96:96 + CHUNKS, 1:n]
    link(vec.scalar_tensor_tensor(last, equal[96:96 + CHUNKS, 1:n], FAR, last, ALU.mult, ALU.add))


def index_stage(kit, k, val, equal, N, M):
    nc = kit.nc
    CH = M * T
    PIECES = CH // 512
    with ExitStack() as ctx:
        def sb(name, shape, dt=F32):
            return kit.sb(name, shape, dt, ctx)

        same7, next7 = equal[0:CHUNKS, 0:CH], equal[0:CHUNKS, 1:CH + 1]
        wide = sb("wide", [Q, CH])
        wide2 = sb("wide2", [Q, CH])
        psum = [ctx.enter_context(nc.psum_tensor(f"ix{i}", [T, 512], F32)) for i in range(8)]
        sc = Scans(kit, k, ctx, "ixs", psum[7])
        constants, numbered, spread, copied, spread_all, copied_all, inverted = (kit.sem(f"ix_{n}") for n in (
            "constants", "numbered", "spread", "copied", "spread_all", "copied_all", "inverted"))
        chain = Chain(kit, "ix_chain")
        parts = max(p for p in range(1, T + 1) if N % p == 0)
        identity = sb("identity_place", [parts, N // parts], I32)

        with nc.Block() as block:
            @block.sync
            def _(sp):
                sp.wait_ge(numbered, 2)
                sp.dma_start(k.place[:, :].rearrange("(p n) a -> p (n a)", p=parts), identity[:, :]
                             ).then_inc(kit.place_clear, 16)
                sp.wait_ge(kit.place_clear, 16)

            @block.gpsimd
            def _(pool):
                nc.gpsimd.iota(k.edge_row[:, :], pattern=[[T, k.NT]], base=N, channel_multiplier=1).then_inc(numbered, 1)
                nc.gpsimd.iota(identity[:, :], pattern=[[1, N // parts]], base=0,
                               channel_multiplier=N // parts).then_inc(numbered, 1)

            @block.vector
            def _(dve):
                v, link = nc.vector, chain.on(dve)
                link(v.memset(k.same[:, k.NT * T:], 0.0))
                link(v.memset(sc.into[:, :, :], 0.0))

        def take(n, bank):
            for f, out in ((1, k.src_i), (2, k.type_f), (3, k.last_i)):
                nc.vector.tensor_copy(by_chunk(out)[:, 4 * n:4 * n + 4, :], bank[:, :, 32 * f:32 * f + CHUNKS])
            nc.vector.tensor_scalar(by_chunk(k.dst_i)[:, 4 * n:4 * n + 4, :], bank[:, :, 0:CHUNKS], float(N - 1), None, ALU.min)
            return nc.vector.tensor_scalar(by_chunk(k.last_f)[:, 4 * n:4 * n + 4, :], bank[:, :, 96:96 + CHUNKS],
                                           float(N), None, ALU.is_lt)

        turn_rows(kit, k, "ix_all", psum, val[:, 1:CH + 1], T, M, take)

        jobs = [(same7, k.same84), (next7, k.next84)]
        with nc.Block() as block:
            @block.gpsimd
            def _(pool):
                nc.gpsimd.memset(wide2[:, :], 0.0).then_inc(constants, 1)
                nc.gpsimd.memset(wide[:, :], 1.0).then_inc(constants, 1)

            @block.tensor
            def _(pe):
                for n in range(k.NG):
                    at = n % PIECES * 512
                    need(pe, copied_all, n - 3)
                    nc.tensor.matmul(psum[2 + n % 4][:, :], k.one_chunk[:, n // PIECES, :], same7[:, at:at + 512],
                                     start=True, stop=True).then_inc(spread_all, 1)
                    if n < 2 * PIECES:
                        need(pe, copied, n - 1)
                        nc.tensor.matmul(psum[n % 2][0:Q, :], k.chunk_of[:, :], jobs[n // PIECES][0][:, at:at + 512],
                                         start=True, stop=True).then_inc(spread, 1)

            @block.scalar
            def _(act):
                for n in range(k.NG):
                    act.wait_ge(spread_all, n + 1)
                    nc.scalar.activation(k.same[:, n * 512:(n + 1) * 512], psum[2 + n % 4][:, :],
                                         ACT.Copy).then_inc(copied_all, 1)

            @block.vector
            def _(dve):
                for n in range(2 * PIECES):
                    at = n % PIECES * 512
                    dve.wait_ge(spread, n + 1)
                    nc.vector.tensor_copy(jobs[n // PIECES][1][:, at:at + 512], psum[n % 2][0:Q, :]).then_inc(copied, 1)
                v, link = nc.vector, chain.on(dve)
                dve.wait_ge(copied, 2 * PIECES)
                dve.wait_ge(constants, 2)
                for r in range(R):
                    link(v.tensor_scalar(k.is_type[:, :, r], k.type_f[:, :], float(r), None, ALU.is_equal))
                link(v.tensor_tensor_scan(k.prod_f[:, :], k.same84[:, :], wide2[:, :], 1.0, ALU.mult, ALU.add))
                link(v.tensor_tensor_scan(k.prod_b[:, ::-1], k.next84[:, ::-1], wide2[:, ::-1], 1.0, ALU.mult, ALU.add))

        with nc.Block() as block:
            @block.vector
            def _(dve):
                v, link = nc.vector, chain.on(dve)
                sc.flags_row(dve, link, k.prod_f, k.flow_f, True)
                sc.flags_row(dve, link, k.prod_b, k.flow_b, False)
                sc.scan(dve, link, wide2, wide[:, :], k.same84[:, :], k.prod_f[:, :], k.flow_f, ALU.add, True)

            @block.tensor
            def _(pe):
                for _ in range(3):
                    sc.pe_scan(pe)

        turn_rows(kit, k, "ix_deg", psum, wide2, Q, M, lambda n, bank: nc.vector.tensor_copy(
            by_chunk(k.deg)[:, 4 * n:4 * n + 4, :], bank[:, :, 0:Q:RH]))
        with nc.Block() as block:
            @block.vector
            def _(dve):
                nc.vector.reciprocal(k.rdeg[:, :], k.deg[:, :]).then_inc(inverted, 1)

            @block.scalar
            def _(act):
                act.wait_ge(inverted, 1)
                nc.scalar.activation(k.norm[:, :], k.rdeg[:, :], ACT.Sqrt)


def over(row):
    return row[:, :].rearrange("p (a d) -> p a d", a=1).to_broadcast([T, G, D])


def turn(nc, k, bank, buf, done):
    for j in range(G):
        last = nc.tensor.transpose(bank[:, j * T:(j + 1) * T], buf[:, j * T:(j + 1) * T], k.ident[:, :])
    last.then_inc(done, 1)


def multiply_rows(nc, bank, turned, weights, done):
    for j in range(G):
        last = nc.tensor.matmul(bank[:, j * T:(j + 1) * T], turned[:, j * T:(j + 1) * T], weights, start=True, stop=True)
    last.then_inc(done, 1)


def begin_with_row(nc, k, bank, parts):
    nc.tensor.matmul(bank[:, :], k.ones[:, :], parts[:, :, :].rearrange("p j d -> p (j d)"), start=True, stop=False)


def edge_rows(dram, g, base):
    return dram[bass.ds(g * W + base, W), :].rearrange("(j p) d -> p j d", p=T)


class Gather:

    def __init__(self, kit, ctx, name, index, table, bufs, n=G, place=lambda g: g):
        self.kit, self.index, self.table, self.bufs, self.n, self.place = kit, index, table, bufs, n, place
        self.now = [kit.sb(f"{name}_now{b}", [T, n], I32, ctx) for b in range(2)]
        self.staged = kit.sem(f"{name}_staged")
        self.arrived = [kit.sem(f"{name}_arrived{b}", True) for b in range(2)]
        self.fed = [kit.sem(f"{name}_fed{b}") for b in range(2)]

    def stage(self, pool, free):
        def run(g, h, b):
            nc = self.kit.nc
            waits = list(free(g, h, b))
            if not (isinstance(h, int) and h <= 0):
                waits.append((self.arrived[b], h * 16 * self.n))
            self.kit.hold("pool", pool, *waits)
            nc.gpsimd.tensor_copy(self.now[b][:, :], self.index[:, bass.ds(self.place(g) * self.n, self.n)]).then_inc(self.staged, 1)
            self.kit.hold("pool", pool, (self.staged, g + 1))
            for j in range(self.n):
                pool.indirect_dma_start(self.bufs[b][:, j * T:(j + 1) * T], None, self.table,
                                        bass.IndirectOffsetOnAxis(ap=self.now[b][:, j:j + 1], axis=0)
                                        ).then_inc(self.arrived[b], 16)
        return run

    def stage_ahead(self, pool, free, groups):
        nc = self.kit.nc

        def copy(g, h, b):
            waits = [] if isinstance(h, int) and h <= 0 else [(self.arrived[b], h * 16 * self.n)]
            self.kit.hold("pool", pool, *waits)
            nc.gpsimd.tensor_copy(self.now[b][:, :], self.index[:, bass.ds(self.place(g) * self.n, self.n)]).then_inc(self.staged, 1)

        def run(g, h, b):
            if isinstance(g, int) and g == 0:
                copy(g, h, b)
            self.kit.hold("pool", pool, *free(g, h, b), (self.staged, g + 1))
            for j in range(self.n):
                if j == self.n - 1 and not (isinstance(g, int) and g == groups - 1):
                    copy(g + 1, h + b, 1 - b)
                pool.indirect_dma_start(self.bufs[b][:, j * T:(j + 1) * T], None, self.table,
                                        bass.IndirectOffsetOnAxis(ap=self.now[b][:, j:j + 1], axis=0)
                                        ).then_inc(self.arrived[b], 16)
        return run

    def feed(self, sp):
        def run(g, h, b):
            waits = [] if isinstance(h, int) and h <= 0 else [(self.arrived[b], h * 16 * self.n)]
            self.kit.hold("sp", sp, *waits)
            sp.dma_start(self.now[b][:, :], self.index[:, bass.ds(self.place(g) * self.n, self.n)]
                         ).then_inc(self.fed[b], 16)
        return run

    def fed_stage(self, pool, free):
        def run(g, h, b):
            self.kit.hold("pool", pool, *free(g, h, b), (self.fed[b], (h + 1) * 16))
            for j in range(self.n):
                pool.indirect_dma_start(self.bufs[b][:, j * T:(j + 1) * T], None, self.table,
                                        bass.IndirectOffsetOnAxis(ap=self.now[b][:, j:j + 1], axis=0)
                                        ).then_inc(self.arrived[b], 16)
        return run

    def wait(self, eng, h, b):
        eng.wait_ge(self.arrived[b], (h + 1) * 16 * self.n)


def segment_sum(kit, k, dve, out, messages, ready, summed, free):
    def stage(g, h, b):
        for sem, value in free(g):
            need(dve, sem, value)
        need(dve, summed, g)
        kit.hold("dve", dve, (ready, g + 1))
        first = isinstance(g, int) and g == 0
        kit.nc.vector.tensor_tensor_scan(out[b][:, :], k.same[:, bass.ds(g * W, W)], messages[b][:, :],
                                         0.0 if first else out[1 - b][:, W - 1:W], ALU.mult, ALU.add).then_inc(summed, 1)
    return stage


class Spread:

    def __init__(self, kit, ctx, name):
        self.kit = kit
        self.sums, self.std, self.rstd = ([kit.sb(f"{name}_{n}{b}", [T, G], F32, ctx) for b in range(2)]
                                          for n in ("sums", "std", "rstd"))
        self.square = kit.sb(f"{name}_square", [T, W], F32, ctx)
        self.summed, self.rooted, self.inverted = (kit.sem(f"{name}_{n}") for n in ("summed", "rooted", "inverted"))

    def on_act(self, act, eps, tile, g, b):
        nc = self.kit.nc
        need(act, self.inverted, g - 1)
        for j in range(G):
            last = nc.scalar.activation(self.square[:, j * D:(j + 1) * D], tile(j), ACT.Square, accum_out=self.sums[b][:, j:j + 1])
        last.then_inc(self.summed, 1)
        act.wait_ge(self.summed, g + 1)
        nc.scalar.activation(self.std[b][:, :], self.sums[b][:, :], ACT.Sqrt, bias=eps, scale=1.0 / D
                             ).then_inc(self.rooted, 1)

    def invert(self, dve, g, b):
        dve.wait_ge(self.rooted, g + 1)
        self.kit.nc.vector.reciprocal(self.rstd[b][:, :], self.std[b][:, :]).then_inc(self.inverted, 1)
        dve.wait_ge(self.inverted, g + 1)


def wide(col):
    return col[:, :].rearrange("p (j a) -> p j a", a=1).to_broadcast([T, G, D])


def first_pass(kit, k, x, out, x_own):
    nc = kit.nc
    N = k.N
    GD = -(-N // W)
    GE = k.NT // 2
    E2 = 2 * T
    LAG = 9
    with ExitStack() as ctx:
        def pair(name, shape=(T, W), dt=F32):
            return [kit.sb(f"dn_{name}{b}", list(shape), dt, ctx) for b in range(2)]

        X, XT, H1T, H1R, H2T, YT, X1R, Y2, X2R = (pair(n) for n in "X XT H1T H1R H2T YT X1R Y2 X2R".split())
        Y3, X3R, X3B, X3T, MA, MB, Y4, X4R = (pair(n) for n in "Y3 X3R X3B X3T MA MB Y4 X4R".split())
        XS, XD, XDT, AG, BASE, MIX, HR = (pair(n, (T, E2)) for n in "XS XD XDT AG BASE MIX HR".split())
        B = [ctx.enter_context(nc.psum_tensor(f"dn_bank{i}", [T, 512], F32)) for i in range(8)]
        sp1, sp2, sp3, sp4 = (Spread(kit, ctx, f"dn_sp{i}") for i in (1, 2, 3, 4))
        (xt_turned, xt, h1_mul, h1t, h1_turned, h1r, h2_mul, h2t, yt, mixed, x1, y2, x2, y3, x3, x3b, x3_turned, x3t,
         ma_mul, mb_mul, ma, mb, out_mul, y4, x4) = (kit.sem(f"dn_{n}") for n in (
             "xt_turned xt h1_mul h1t h1_turned h1r h2_mul h2t yt mixed x1 y2 x2 y3 x3 x3b x3_turned x3t "
             "ma_mul mb_mul ma mb out_mul y4 x4").split())
        s_turned, d_turned, summed, xdt, a_mul, b_mul, base, joined, hr = (kit.sem(f"se_{n}") for n in (
            "s_turned d_turned summed xdt a_mul b_mul base joined hr").split())
        x_in = [kit.sem(f"dn_x_in{b}") for b in range(2)]
        h1_out, x1_out, x2_out, x3_out, out_out, kept, stored = ([kit.sem(f"dn_{n}{b}") for b in range(2)] for n in (
            "h1_out", "x1_out", "x2_out", "x3_out", "out_out", "kept", "stored"))
        src_g = Gather(kit, ctx, "se_src", k.src_i, x, XS, 2)
        own_g = Gather(kit, ctx, "se_own", k.dst_i, x, XD, 2)
        now, vals = pair("pl_now", (T, G), I32), pair("pl_vals", (T, G), I32)
        got = pair("pl_got", (T, G), I32)
        pl_now, pl_kept = kit.sem("pl_staged"), kit.sem("pl_kept")
        pl_put, pl_got = ([kit.sem(f"pl_{n}{b}", True) for b in range(2)] for n in ("put", "got"))

        def rows(dram, g):
            base_row = g * W if not isinstance(g, int) else min(g * W, N - W)
            return dram[bass.ds(base_row, W), :].rearrange("(p j) d -> p (j d)", j=G)

        def pair_rows(dram, g, base_row):
            return dram[bass.ds(g * E2 + base_row, E2), :].rearrange("(j p) d -> p j d", p=T)

        def two(buf):
            return buf[:, :].rearrange("p (j d) -> p j d", j=2)

        def run(eng, *line):
            def body(at_n, at_e):
                for stream, lag, stage in line:
                    g = (at_n if stream == "n" else at_e)(lag)
                    if g is not None:
                        stage(*g)
            two_streams(eng, GD, GE, LAG, body)

        def gone(stored_sem, h, b):
            return (stored_sem[b], h * 16)

        with nc.Block() as block:
            @block.gpsimd
            def _(pool):
                pool.wait_ge(kit.place_clear, 16)

                def put_place(g, h, b):
                    kit.hold("pool", pool, (pl_put[b], h * 16 * G))
                    nc.gpsimd.tensor_copy(now[b][:, :], k.last_i[:, bass.ds(g * G, G)]).then_inc(pl_now, 1)
                    nc.gpsimd.tensor_copy(vals[b][:, :], k.edge_row[:, bass.ds(g * G, G)]).then_inc(pl_now, 1)
                    kit.hold("pool", pool, (pl_now, g * 2 + 2))
                    for j in range(G):
                        pool.indirect_dma_start(k.place, bass.IndirectOffsetOnAxis(ap=now[b][:, j:j + 1], axis=0),
                                                vals[b][:, j:j + 1], None, bounds_check=N - 1,
                                                oob_is_err=False).then_inc(pl_put[b], 16)

                def fetch(g, h, b):
                    kit.hold("pool", pool, (pl_got[b], h * 16 * G), (pl_kept, g - 1))
                    nc.gpsimd.tensor_copy(now[b][:, :], k.src_i[:, bass.ds(g * G, G)]).then_inc(pl_now, 1)
                    kit.hold("pool", pool, (pl_now, 2 * k.NG + g + 1))
                    for j in range(G):
                        pool.indirect_dma_start(got[b][:, j:j + 1], None, k.place,
                                                bass.IndirectOffsetOnAxis(ap=now[b][:, j:j + 1], axis=0)
                                                ).then_inc(pl_got[b], 16)

                def keep_place(g, h, b):
                    kit.hold("pool", pool, (pl_got[b], (h + 1) * 16 * G))
                    nc.gpsimd.tensor_copy(k.srcp_i[:, bass.ds(g * G, G)], got[b][:, :]).then_inc(pl_kept, 1)

                gather_src = src_g.stage(pool, lambda g, h, b: [(s_turned, g - 1)])
                gather_own = own_g.stage(pool, lambda g, h, b: [(d_turned, g - 1), (kept[b], h * 16)])
                half = k.NG // 2 * 2

                def with_puts(s, h, b):
                    gather_src(s, h, b)
                    gather_own(s, h, b)
                    put_place(s, h, b)

                def with_fetches(s, h, b, g):
                    gather_src(s, h, b)
                    gather_own(s, h, b)
                    fetch(*g)

                for s in range(2):
                    with_puts(s, 0, s)
                with pool.Fori(1, half // 2) as i:
                    for u in range(2):
                        with_puts(i * 2 + u, i, u)
                for g in range(half, k.NG):
                    put_place(g, g // 2, g % 2)
                for b in range(2):
                    pool.wait_ge(pl_put[b], 16 * G * ((k.NG - b + 1) // 2))
                off = half // 2
                for s in range(2):
                    with_fetches(half + s, off, s, (s, 0, s))
                with pool.Fori(1, half // 2) as i:
                    for u in range(2):
                        keep_place(i * 2 + (u - 2), i - 1, u)
                        with_fetches(i * 2 + (half + u), i + off, u, (i * 2 + u, i, u))
                for g in range(half - 2, half):
                    keep_place(g, g // 2, g % 2)
                for g in range(half, k.NG):
                    fetch(g, g // 2, g % 2)
                    keep_place(g, g // 2, g % 2)
                for s in range(2 * half, GE):
                    gather_src(s, s // 2, s % 2)
                    gather_own(s, s // 2, s % 2)

            @block.sync
            def _(sp):
                def load(g, h, b):
                    need(sp, xt_turned, g - 1)
                    sp.dma_start(X[b][:, :], rows(x, g)).then_inc(x_in[b], 16)

                def store(dram, buf, written, landed):
                    def stage(g, h, b):
                        sp.wait_ge(written, g + 1)
                        if isinstance(g, int) and g == GD - 1:
                            sp.wait_ge(landed[1 - b], 16 * ((g - 1) // 2 + 1))
                        sp.dma_start(rows(dram, g), buf[b][:, :]).then_inc(landed[b], 16)
                    return stage

                def keep(g, h, b):
                    own_g.wait(sp, h, b)
                    sp.dma_start(pair_rows(x_own, g, 0), two(XD[b])).then_inc(kept[b], 16)

                def store_h(g, h, b):
                    sp.wait_ge(hr, g + 1)
                    sp.dma_start(pair_rows(k.tab[0], g, N), two(HR[b])).then_inc(stored[b], 16)

                run(sp, ("n", 0, load), ("n", 3, store(k.tab[1], X1R, x1, x1_out)),
                    ("n", 4, store(k.tab[0], H1R, h1r, h1_out)), ("n", 4, store(k.tab[2], X2R, x2, x2_out)),
                    ("n", 5, store(k.tab[3], X3R, x3, x3_out)), ("n", LAG, store(out, X4R, x4, out_out)),
                    ("e", 5, store_h), ("e", 1, keep))
                for s in (h1_out, x1_out, x2_out, x3_out, out_out):
                    for b in range(2):
                        sp.wait_ge(s[b], 16 * ((GD - b + 1) // 2))
                for s in (kept, stored):
                    for b in range(2):
                        sp.wait_ge(s[b], 16 * ((GE - b + 1) // 2))

            @block.tensor
            def _(pe):
                def clear(g, lag, *users):
                    for read, stream, its_lag, before in users:
                        value = g + (lag - its_lag + before)
                        need(pe, read, min(value, GD if stream == "n" else GE) if isinstance(g, int) else value)

                def turn_x(g, h, b):
                    pe.wait_ge(x_in[b], (h + 1) * 16)
                    clear(g, 1, (ma, "n", 5, 0), (summed, "e", 1, 0))
                    turn(nc, k, B[4], X[b], xt_turned)

                def mul_mix(g, h, b):
                    pe.wait_ge(yt, g + 1)
                    clear(g, 2, (x1, "n", 2, 0), (y2, "n", 2, 0))
                    for j in range(G):
                        last = nc.tensor.matmul(B[2 + j // 2][:, (j % 2) * 2 * D:(j % 2 + 1) * 2 * D],
                                                YT[b][:, j * T:(j + 1) * T], k.pair_mix[:, :], start=True, stop=True)
                    last.then_inc(mixed, 1)

                def turn_h1(g, h, b):
                    pe.wait_ge(h1t, g + 1)
                    clear(g, 2, (h1r, "n", 2, 0))
                    turn(nc, k, B[7], H1T[b], h1_turned)

                def mul_h1(g, h, b):
                    pe.wait_ge(xt, g + 1)
                    clear(g, 1, (xdt, "e", 1, 1), (h2t, "n", 1, 0))
                    nc.tensor.matmul(B[6][:, :], k.wr1[:, :], XT[b][:, :], start=True, stop=True).then_inc(h1_mul, 1)

                def mul_out(g, h, b):
                    pe.wait_ge(ma, g + 1)
                    pe.wait_ge(mb, g + 1)
                    clear(g, 6, (joined, "e", 2, 0), (y4, "n", 6, 0))
                    for j in range(G):
                        at = slice(j * T, (j + 1) * T)
                        nc.tensor.matmul(B[5][:, at], MA[b][:, at], k.wm2[:, 0, :], start=True, stop=False)
                        last = nc.tensor.matmul(B[5][:, at], MB[b][:, at], k.wm2[:, 1, :], start=False, stop=True)
                    last.then_inc(out_mul, 1)

                def mul_h2(g, h, b):
                    pe.wait_ge(h1t, g + 1)
                    clear(g, 1, (xdt, "e", 1, 1), (h2t, "n", 1, 0))
                    nc.tensor.matmul(B[6][:, :], k.wr2[:, :], H1T[b][:, :], start=True, stop=True).then_inc(h2_mul, 1)

                def mul_ma(g, h, b):
                    pe.wait_ge(x3t, g + 1)
                    clear(g, 5, (summed, "e", 1, 1), (xt, "n", 1, 1), (ma, "n", 5, 0))
                    nc.tensor.matmul(B[4][:, :], k.wm1[:, 0:D], X3T[b][:, :], start=True, stop=True).then_inc(ma_mul, 1)

                def turn_x3(g, h, b):
                    pe.wait_ge(x3, g + 1)
                    clear(g, 4, (x3t, "n", 4, 0))
                    turn(nc, k, B[0], X3R[b], x3_turned)

                def mul_mb(g, h, b):
                    pe.wait_ge(x3t, g + 1)
                    clear(g, 5, (base, "e", 1, 1), (mb, "n", 5, 0))
                    nc.tensor.matmul(B[1][:, :], k.wm1[:, D:2 * D], X3T[b][:, :], start=True, stop=True).then_inc(mb_mul, 1)

                def turn_e(bank, buf, done):
                    for j in range(2):
                        last = nc.tensor.transpose(bank[:, j * T:(j + 1) * T], buf[:, j * T:(j + 1) * T], k.ident[:, :])
                    last.then_inc(done, 1)

                def mul_e(bank, buf, weights, done):
                    for j in range(2):
                        last = nc.tensor.matmul(bank[:, j * T:(j + 1) * T], buf[:, j * T:(j + 1) * T], weights,
                                                start=True, stop=True)
                    last.then_inc(done, 1)

                def turn_s(g, h, b):
                    src_g.wait(pe, h, b)
                    clear(g, 1, (xt, "n", 1, 1), (ma, "n", 5, 0), (summed, "e", 1, 0))
                    turn_e(B[4], XS[b], s_turned)

                def turn_d(g, h, b):
                    own_g.wait(pe, h, b)
                    clear(g, 1, (h2t, "n", 1, 0), (xdt, "e", 1, 0))
                    turn_e(B[6], XD[b], d_turned)

                def mul_a(g, h, b):
                    pe.wait_ge(summed, g + 1)
                    clear(g, 2, (y4, "n", 6, 1), (joined, "e", 2, 0))
                    mul_e(B[5], AG[b], k.wl1[:, :], a_mul)

                def mul_b(g, h, b):
                    pe.wait_ge(xdt, g + 1)
                    clear(g, 1, (mb, "n", 5, 0), (base, "e", 1, 0))
                    mul_e(B[1], XDT[b], k.wr1[:, :], b_mul)

                run(pe, ("e", 1, turn_d), ("n", 1, turn_x), ("n", 2, mul_mix), ("n", 2, turn_h1), ("e", 1, turn_s),
                    ("n", 1, mul_h1), ("n", 6, mul_out), ("n", 1, mul_h2), ("n", 5, mul_ma), ("e", 1, mul_b),
                    ("e", 2, mul_a), ("n", 4, turn_x3), ("n", 5, mul_mb))

            @block.scalar
            def _(act):
                def on(dst, bank, ready, done, func, free, **more):
                    def stage(g, h, b):
                        for sem in free:
                            need(act, sem, g - 1)
                        act.wait_ge(ready, g + 1)
                        nc.scalar.activation(dst[b][:, :], bank[:, 0:dst[b].shape[1]], func, **more).then_inc(done, 1)
                    return stage

                def spread(sp, rows_ready, tile):
                    def stage(g, h, b):
                        act.wait_ge(rows_ready, g + 1)
                        sp.on_act(act, k.eps[:, 0:1], lambda j: tile(b, j), g, b)
                    return stage

                def tile_of(buf):
                    return lambda b, j: buf[b][:, j * D:(j + 1) * D]

                def relu_h(g, h, b):
                    need(act, *gone(stored, h, b))
                    act.wait_ge(joined, g + 1)
                    nc.scalar.activation(HR[b][:, :], MIX[b][:, :], ACT.Relu).then_inc(hr, 1)

                copy_x = on(XT, B[4], xt_turned, xt, ACT.Copy, [yt])
                relu_h1 = on(H1T, B[6], h1_mul, h1t, ACT.Relu, [h1_turned, h2_mul], bias=k.bl1_col[:, 0:1])
                relu_h2 = on(H2T, B[6], h2_mul, h2t, ACT.Relu, [yt], bias=k.bl2_col[:, 0:1])
                copy_x3 = on(X3T, B[0], x3_turned, x3t, ACT.Copy, [ma_mul, mb_mul])
                relu_a, relu_b = (
                    on(m, bank, ready, done, ACT.Relu, [out_mul], bias=k.bn1_b[:, n:n + 1], scale=k.bn1_s_own[:, n:n + 1])
                    for n, (m, bank, ready, done) in enumerate(((MA, B[4], ma_mul, ma), (MB, B[1], mb_mul, mb))))
                copy_d = on(XDT, B[6], d_turned, xdt, ACT.Copy, [b_mul])
                run(act, ("e", 4, relu_h), ("n", 8, spread(sp4, y4, tile_of(Y4))), ("n", 4, spread(sp3, y3, tile_of(Y3))),
                    ("n", 2, relu_h2), ("n", 6, relu_a), ("n", 3, spread(sp2, y2, tile_of(Y2))), ("e", 1, copy_d),
                    ("n", 6, relu_b), ("n", 5, copy_x3), ("n", 1, copy_x),
                    ("n", 2, spread(sp1, mixed, lambda b, j: B[2 + j // 2][:, (j % 2) * 2 * D:(j % 2) * 2 * D + D])),
                    ("n", 1, relu_h1))

            @block.vector
            def _(dve):
                v = nc.vector

                def add_y(g, h, b):
                    need(dve, mixed, g - 1)
                    dve.wait_ge(h2t, g + 1)
                    v.tensor_tensor(YT[b][:, :], H2T[b][:, :], XT[b][:, :], ALU.add).then_inc(yt, 1)

                def take_h1(g, h, b):
                    need(dve, *gone(h1_out, h, b))
                    dve.wait_ge(h1_turned, g + 1)
                    v.tensor_copy(H1R[b][:, :], B[7][:, :]).then_inc(h1r, 1)

                def scale_x1(g, h, b):
                    sp1.invert(dve, g, b)
                    need(dve, *gone(x1_out, h, b))
                    for i in range(2):
                        last = v.tensor_tensor(
                            tiles(X1R[b])[:, 2 * i:2 * i + 2, :],
                            B[2 + i][:, :].rearrange("p (j n) -> p j n", j=2)[:, :, 0:D],
                            wide(sp1.rstd[b])[:, 2 * i:2 * i + 2, :], ALU.mult)
                    last.then_inc(x1, 1)

                def scale_y2(g, h, b):
                    need(dve, x2, g - 1)
                    for j in range(G):
                        last = v.scalar_tensor_tensor(
                            Y2[b][:, j * D:(j + 1) * D], B[2 + j // 2][:, (j % 2) * 2 * D + D:(j % 2 + 1) * 2 * D],
                            sp1.rstd[b][:, j:j + 1], k.bbar_row[:, :], ALU.mult, ALU.add)
                    last.then_inc(y2, 1)

                def scale_x2(g, h, b):
                    sp2.invert(dve, g, b)
                    need(dve, *gone(x2_out, h, b))
                    need(dve, y3, g - 1)
                    v.tensor_tensor(tiles(X2R[b]), tiles(Y2[b]), wide(sp2.rstd[b]), ALU.mult).then_inc(x2, 1)

                def add_y3(g, h, b):
                    need(dve, x3, g - 1)
                    dve.wait_ge(x2, g + 1)
                    v.tensor_tensor(tiles(Y3[b]), tiles(X2R[b]), over(k.b2_row), ALU.add).then_inc(y3, 1)

                def scale_x3(g, h, b):
                    sp3.invert(dve, g, b)
                    need(dve, *gone(x3_out, h, b))
                    need(dve, x3_turned, g - 1)
                    need(dve, x3b, g - 1)
                    v.tensor_tensor(tiles(X3R[b]), tiles(Y3[b]), wide(sp3.rstd[b]), ALU.mult).then_inc(x3, 1)

                def bias_x3(g, h, b):
                    dve.wait_ge(x3, g + 1)
                    need(dve, y4, g - 1)
                    v.tensor_tensor(tiles(X3B[b]), tiles(X3R[b]), over(k.bn2_row), ALU.add).then_inc(x3b, 1)

                def add_y4(g, h, b):
                    dve.wait_ge(x3b, g + 1)
                    need(dve, x4, g - 1)
                    dve.wait_ge(out_mul, g + 1)
                    v.tensor_tensor(Y4[b][:, :], B[5][:, :], X3B[b][:, :], ALU.add).then_inc(y4, 1)

                def scale_x4(g, h, b):
                    sp4.invert(dve, g, b)
                    need(dve, *gone(out_out, h, b))
                    v.tensor_tensor(tiles(X4R[b]), tiles(Y4[b]), wide(sp4.rstd[b]), ALU.mult).then_inc(x4, 1)

                def total(g, h, b):
                    need(dve, a_mul, g - 1)
                    need(dve, summed, g)
                    kit.hold("dve", dve, (s_turned, g + 1))
                    first = isinstance(g, int) and g == 0
                    v.tensor_tensor_scan(AG[b][:, :], k.same[:, bass.ds(g * E2, E2)], B[4][:, 0:E2],
                                         0.0 if first else AG[1 - b][:, E2 - 1:E2], ALU.mult, ALU.add
                                         ).then_inc(summed, 1)

                def add_bias(g, h, b):
                    dve.wait_ge(b_mul, g + 1)
                    need(dve, joined, g - 1)
                    v.tensor_tensor(two(BASE[b]), two(B[1][:, 0:E2]), k.bl1_row[:, :].rearrange(
                        "p (a d) -> p a d", a=1).to_broadcast([T, 2, D]), ALU.add).then_inc(base, 1)

                def join(g, h, b):
                    need(dve, hr, g - 1)
                    kit.hold("dve", dve, (base, g + 1), (a_mul, g + 1))
                    for j in range(2):
                        at = slice(j * T, (j + 1) * T)
                        last = v.scalar_tensor_tensor(MIX[b][:, at], B[5][:, at], k.rdeg[:, bass.ds(g * 2 + j, 1)],
                                                      BASE[b][:, at], ALU.mult, ALU.add)
                    last.then_inc(joined, 1)

                run(dve, ("e", 3, join), ("n", 2, add_y), ("n", 3, take_h1), ("n", 3, scale_x2), ("n", 6, bias_x3),
                    ("n", 4, scale_x3), ("n", 8, scale_x4), ("n", 3, add_y3), ("e", 1, total), ("n", 2, scale_x1),
                    ("n", 6, add_y4), ("n", 2, scale_y2), ("e", 1, add_bias))


def two_streams(eng, n1, n2, lag, body):
    def fixed(s, n):
        def at(k):
            g = s - k
            return (g, g // 2, g % 2) if 0 <= g < n else None
        return at

    first = lag + 2 + (lag % 2)
    pairs = (min(n1, n2) - 1 - first) // 2
    start = max(n1, n2) + lag if pairs < 2 else first
    for s in range(start):
        body(fixed(s, n1), fixed(s, n2))
    if pairs < 2:
        return
    with eng.Fori(0, pairs) as i:
        for u in range(2):
            def at(k, u=u):
                c = first + u - k
                return i * 2 + c, i + c // 2, c % 2
            body(at, at)
    for s in range(first + 2 * pairs, max(n1, n2) + lag):
        body(fixed(s, n1), fixed(s, n2))


def sage(kit, k):
    nc = kit.nc
    LAG = 6
    name = "s2"
    with ExitStack() as ctx:
        def pair(n):
            return [kit.sb(f"{name}_{n}{b}", [T, W], F32, ctx) for b in range(2)]

        XS, XD, XDT, AG, BASE, MIX, HR, XR, Y, OUT = (pair(n) for n in "XS XD XDT AG BASE MIX HR XR Y OUT".split())
        ln = Norm(kit, ctx, f"{name}_ln")
        B = [ctx.enter_context(nc.psum_tensor(f"{name}_bank{i}", [T, 512], F32)) for i in range(4)]
        src_g = Gather(kit, ctx, f"{name}_src", k.srcp_i, k.tab[0], XS)
        s_turned, d_turned, summed, xdt, a_mul, b_mul, base, mixed, hr, added = (kit.sem(f"{name}_{n}") for n in (
            "s_turned", "d_turned", "summed", "xdt", "a_mul", "b_mul", "base", "mixed", "hr", "added"))
        own_in, x_in, stored = ([kit.sem(f"{name}_{n}{b}") for b in range(2)] for n in ("own_in", "x_in", "stored"))

        with nc.Block() as block:
            @block.gpsimd
            def _(pool):
                steps(pool, k.NG, LAG, lambda at: rounds(
                    at, [(0, src_g.stage_ahead(pool, lambda g, h, b: [(s_turned, g - 1)], k.NG))]))

            @block.sync
            def _(sp):
                def load(g, h, b):
                    need(sp, d_turned, g - 1)
                    sp.dma_start(tiles(XD[b]), edge_rows(k.tab[0], g, k.N)).then_inc(own_in[b], 16)

                def load_x(g, h, b):
                    need(sp, added, g - 1)
                    sp.dma_start(tiles(XR[b]), edge_rows(k.x_own, g, 0)).then_inc(x_in[b], 16)

                def store(g, h, b):
                    sp.wait_ge(ln.done, g + 1)
                    sp.dma_start(edge_rows(k.tab[1], g, k.N), tiles(OUT[b])).then_inc(stored[b], 16)

                steps(sp, k.NG, LAG, lambda at: rounds(at, [(0, load), (3, load_x), (LAG, store)]))
                for b in range(2):
                    sp.wait_ge(stored[b], 16 * ((k.NG - b + 1) // 2))

            @block.tensor
            def _(pe):
                def turn_s(g, h, b):
                    src_g.wait(pe, h, b)
                    need(pe, summed, g)
                    turn(nc, k, B[0], XS[b], s_turned)

                def turn_d(g, h, b):
                    pe.wait_ge(own_in[b], (h + 1) * 16)
                    need(pe, xdt, g)
                    turn(nc, k, B[1], XD[b], d_turned)

                def mul_b(g, h, b):
                    need(pe, base, g)
                    pe.wait_ge(xdt, g + 1)
                    begin_with_row(nc, k, B[3], k.bl2_parts)
                    for j in range(G):
                        last = nc.tensor.matmul(B[3][:, j * T:(j + 1) * T], XDT[b][:, j * T:(j + 1) * T], k.wr2[:, :],
                                                start=False, stop=j == G - 1)
                    last.then_inc(b_mul, 1)

                def mul_a(g, h, b):
                    need(pe, mixed, g)
                    pe.wait_ge(summed, g + 1)
                    multiply_rows(nc, B[2], AG[b], k.wl2[:, :], a_mul)

                steps(pe, k.NG, LAG, lambda at: rounds(at, [(2, turn_s), (1, turn_d), (3, mul_a), (2, mul_b)]))

            @block.scalar
            def _(act):
                def copy_own(g, h, b):
                    need(act, b_mul, g - 1)
                    act.wait_ge(d_turned, g + 1)
                    nc.scalar.activation(XDT[b][:, :], B[1][:, :], ACT.Copy).then_inc(xdt, 1)

                def copy_base(g, h, b):
                    need(act, mixed, g - 1)
                    act.wait_ge(b_mul, g + 1)
                    nc.scalar.activation(BASE[b][:, :], B[3][:, :], ACT.Copy).then_inc(base, 1)

                def relu(g, h, b):
                    need(act, added, g - 1)
                    act.wait_ge(mixed, g + 1)
                    nc.scalar.activation(HR[b][:, :], MIX[b][:, :], ACT.Relu).then_inc(hr, 1)

                def scale(g, h, b):
                    if not (isinstance(h, int) and h <= 0):
                        act.wait_ge(stored[b], h * 16)
                    ln.scale(act, tiles(OUT[b]), tiles(Y[b]), g, b)

                steps(act, k.NG, LAG, lambda at: rounds(at, [
                    (5, lambda g, h, b: ln.root(act, k.eps[:, 0:1], g, b)), (2, copy_base), (1, copy_own), (3, relu),
                    (5, scale)]))

            @block.vector
            def _(dve):
                v = nc.vector
                total = segment_sum(kit, k, dve, AG, [B[0]] * 2, s_turned, summed, lambda g: [(a_mul, g - 1)])

                def mix(g, h, b):
                    need(dve, hr, g - 1)
                    kit.hold("dve", dve, (base, g + 1), (a_mul, g + 1))
                    for j in range(G):
                        last = v.scalar_tensor_tensor(MIX[b][:, j * T:(j + 1) * T], B[2][:, j * T:(j + 1) * T],
                                                      k.rdeg[:, bass.ds(g * G + j, 1)], BASE[b][:, j * T:(j + 1) * T],
                                                      ALU.mult, ALU.add)
                    last.then_inc(mixed, 1)

                def add_x(g, h, b):
                    need(dve, ln.done, g - 1)
                    dve.wait_ge(x_in[b], (h + 1) * 16)
                    dve.wait_ge(hr, g + 1)
                    v.tensor_tensor(Y[b][:, :], HR[b][:, :], XR[b][:, :], ALU.add).then_inc(added, 1)

                def measure(g, h, b):
                    dve.wait_ge(added, g + 1)
                    ln.bn_moments(dve, tiles(Y[b]), g, b)

                steps(dve, k.NG, LAG, lambda at: rounds(at, [
                    (2, total), (3, mix), (4, add_x), (5, lambda g, h, b: ln.invert(dve, g, b)), (4, measure)]))


def gat_messages(kit, k):
    nc = kit.nc
    LAG = 4
    name = "ga"
    with ExitStack() as ctx:
        def pair(n):
            return [kit.sb(f"{name}_{n}{b}", [T, W], F32, ctx) for b in range(2)]

        XS, XD, XM, DFT, XDT, Z = (pair(n) for n in "XS XD XM DFT XDT Z".split())
        NEXT = [kit.sb(f"{name}_next{b}", [T, W], BF16, ctx) for b in range(2)]
        PART = [kit.sb(f"{name}_part{i}", [T, D], F32, ctx) for i in range(4)]
        B = [ctx.enter_context(nc.psum_tensor(f"{name}_bank{i}", [T, 512], F32)) for i in range(8)]
        src_g = Gather(kit, ctx, f"{name}_src", k.srcp_i, k.tab[1], XS, place=lambda g: (k.NG - 1) - g)
        flags, xm, d_turned, xdt, s_turned, dft, s_mul, taken, z_mul, z0, z1, zed, scored = (kit.sem(f"{name}_{n}") for n in (
            "flags", "xm", "d_turned", "xdt", "s_turned", "dft", "s_mul", "taken", "z_mul", "z0", "z1", "zed", "scored"))
        own_in, stored = ([kit.sem(f"{name}_{n}{b}") for b in range(2)] for n in ("own_in", "stored"))

        def back(g):
            return (k.NG - 1) - g

        with nc.Block() as block:
            @block.gpsimd
            def _(pool):
                steps(pool, k.NG, LAG, lambda at: rounds(
                    at, [(1, src_g.stage_ahead(pool, lambda g, h, b: [(s_turned, g - 1)], k.NG))]))

            @block.sync
            def _(sp):
                def load(g, h, b):
                    kit.hold("sp", sp, (xm, g - 1))
                    sp.dma_start(tiles(XD[b]), edge_rows(k.tab[1], back(g), k.N)).then_inc(own_in[b], 16)

                def store(g, h, b):
                    kit.hold("sp", sp, (zed, g * G + G))
                    sp.dma_start(edge_rows(k.messages, back(g), 0), tiles(Z[b])).then_inc(stored[b], 16)

                steps(sp, k.NG, LAG, lambda at: rounds(at, [(0, load), (LAG, store)]))
                for b in range(2):
                    sp.wait_ge(stored[b], 16 * ((k.NG - b + 1) // 2))

            @block.tensor
            def _(pe):
                def turn_d(g, h, b):
                    pe.wait_ge(xm, g + 1)
                    need(pe, xdt, g)
                    turn(nc, k, B[1], XM[b], d_turned)

                def turn_s(g, h, b):
                    src_g.wait(pe, h, b)
                    need(pe, dft, g)
                    turn(nc, k, B[0], XS[b], s_turned)

                def scores(g, h, b):
                    pe.wait_ge(xdt, g + 1)
                    need(pe, taken, g)
                    for j in range(G):
                        last = nc.tensor.matmul(B[2][:, j * RH:(j + 1) * RH], XDT[b][:, j * T:(j + 1) * T], k.self_w[:, :],
                                                start=True, stop=True)
                    last.then_inc(s_mul, 1)

                def messages(some):
                    def stage(g, h, b):
                        pe.wait_ge(dft, g + 1)
                        for j in some:
                            need(pe, zed, g * G + j - 3)
                            nc.tensor.matmul(B[3 + j][:, 0:R * D + RH], DFT[b][:, j * T:(j + 1) * T], k.w_cat[:, :],
                                             start=True, stop=True).then_inc(z_mul, 1)
                    return stage

                steps(pe, k.NG, LAG, lambda at: rounds(at, [
                    (2, turn_s), (3, scores), (3, messages([0, 1])), (1, turn_d), (3, messages([2, 3]))]))

            @block.scalar
            def _(act):
                def mask(g, h, b):
                    need(act, xdt, g - 1)
                    nc.scalar.activation(NEXT[b][:, :], k.same[:, bass.ds(back(g) * W + 1, W)], ACT.Copy).then_inc(flags, 1)
                    need(act, d_turned, g - 1)
                    kit.hold("act", act, (own_in[b], (h + 1) * 16))
                    for j in range(G):
                        last = nc.scalar.activation(XM[b][:, j * T:(j + 1) * T], XD[b][:, j * T:(j + 1) * T], ACT.Copy,
                                                    scale=k.last_f[:, bass.ds(back(g) * G + j, 1)])
                    last.then_inc(xm, 1)

                def first(g, h, b):
                    for j in range(G):
                        n = g * G + j
                        kit.hold("act", act, (zed, n - 3), (z_mul, n + 1))
                        nc.scalar.activation(PART[j][:, :], B[3 + j][:, 0:D], ACT.Copy,
                                             scale=k.is_type[:, bass.ds(back(g) * G + j, 1), 0]).then_inc(z0, 1)

                steps(act, k.NG, LAG, lambda at: rounds(at, [(1, mask), (3, first)]))

            @block.vector
            def _(dve):
                v = nc.vector

                def flow_back(g, h, b):
                    need(dve, s_mul, g - 1)
                    need(dve, dft, g - 1)
                    need(dve, xdt, g)
                    dve.wait_ge(flags, g + 1)
                    dve.wait_ge(d_turned, g + 1)
                    first = isinstance(g, int) and g == 0
                    v.tensor_tensor_scan(XDT[b][:, ::-1], NEXT[b][:, ::-1], B[1][:, ::-1],
                                         0.0 if first else XDT[1 - b][:, 0:1], ALU.mult, ALU.add).then_inc(xdt, 1)

                def subtract(g, h, b):
                    need(dve, z_mul, (g - 1) * G)
                    dve.wait_ge(s_turned, g + 1)
                    dve.wait_ge(xdt, g + 1)
                    v.tensor_tensor(DFT[b][:, :], B[0][:, :], XDT[b][:, :], ALU.subtract).then_inc(dft, 1)

                def take(g, h, b):
                    kit.hold("dve", dve, (s_mul, g + 1))
                    v.tensor_copy(k.scores[:, bass.ds(back(g) * G, G), RH:2 * RH],
                                  B[2][:, 0:G * RH].rearrange("p (j n) -> p j n", j=G)).then_inc(taken, 1)

                def select(some):
                    def stage(g, h, b):
                        if not (isinstance(h, int) and h <= 0):
                            dve.wait_ge(stored[b], h * 16)
                        kit.hold("dve", dve, (taken, g + 1))
                        for i, j in enumerate(some):
                            n, tile = g * G + j, back(g) * G + j
                            kit.hold("dve", dve, (z0, n + 1))
                            v.scalar_tensor_tensor(PART[j][:, :], B[3 + j][:, D:2 * D], k.is_type[:, bass.ds(tile, 1), 1],
                                                   PART[j][:, :], ALU.mult, ALU.add).then_inc(z1, 1)
                            both = k.scores[:, bass.ds(tile, 1), :]
                            v.tensor_tensor(both[:, :, 0:RH], B[3 + j][:, R * D:R * D + RH].rearrange("p (a n) -> p a n", a=1),
                                            both[:, :, RH:2 * RH], ALU.add).then_inc(scored, 1)
                            if i > 0:
                                join(g, b, j - 1)
                        join(g, b, some[-1])
                    return stage

                def join(g, b, j):
                    n = g * G + j
                    kit.hold("dve", dve, (z1, n + 1), (scored, n + 1))
                    v.scalar_tensor_tensor(Z[b][:, j * T:(j + 1) * T], B[3 + j][:, 2 * D:3 * D],
                                           k.is_type[:, bass.ds(back(g) * G + j, 1), 2], PART[j][:, :],
                                           ALU.mult, ALU.add).then_inc(zed, 1)

                steps(dve, k.NG, LAG, lambda at: rounds(at, [
                    (3, take), (2, subtract), (3, select([0, 1])), (1, flow_back), (3, select([2, 3]))]))


def attention(kit, k, M):
    nc = kit.nc
    CH = M * T
    with ExitStack() as ctx:
        def sb(name, shape, dt=F32):
            return kit.sb(name, shape, dt, ctx)

        rel = k.scores[:, :, 0:RH]
        off = sb("at_off", [T, k.NT])
        by_tile = sb("at_by_tile", [T, M, CHUNKS, RH])
        score = sb("at_score", [Q, CH])
        work = sb("at_work", [Q, CH])
        own = sb("at_own", [Q, CH])
        peak = sb("at_peak", [Q, CH])
        last = sb("at_last", [Q, CH], BF16)
        psum = [ctx.enter_context(nc.psum_tensor(f"at{i}", [T, 512], F32)) for i in range(8)]
        sc = Scans(kit, k, ctx, "ats", psum[7])
        chain, turned, took, act_in, act_out, factors, out_mul, out_took = Chain(kit, "at_chain"), *(
            kit.sem(f"at_{n}") for n in ("turned", "took", "act_in", "act_out", "factors", "out_mul", "out_took"))

        with nc.Block() as block:
            @block.vector
            def _(dve):
                v, link = nc.vector, chain.on(dve)
                s = k.scores[:, :, :].rearrange("p t n -> p (t n)")
                link(v.scalar_tensor_tensor(s, s, 0.2, s, ALU.mult, ALU.max))
                link(v.tensor_tensor(rel, rel, k.scores[:, :, RH:2 * RH], ALU.subtract))
                for r in range(R):
                    mask = k.is_type[:, :, r]
                    link(v.tensor_scalar(off[:, :], mask, MASKED, -MASKED, ALU.mult, ALU.add))
                    part = rel[:, :, r * H:(r + 1) * H]
                    link(v.tensor_tensor(part, part, across(mask), ALU.mult))
                    link(v.tensor_tensor(by_tile[:, :, :, r * H:(r + 1) * H].rearrange("p j c n -> p c j n"),
                                         part.rearrange("p (c j) n -> p c j n", c=CHUNKS),
                                         across(off[:, :]).rearrange("p (c j) n -> p c j n", c=CHUNKS), ALU.add))

        with nc.Block() as block:
            @block.tensor
            def _(pe):
                for n in range(M // 4):
                    need(pe, took, n - 1)
                    for j in range(4):
                        ins = nc.tensor.transpose(psum[n % 2][0:Q, j * T:(j + 1) * T], by_tile[:, 4 * n + j, :, :].rearrange("p c n -> p (c n)"),
                                                  k.ident[:, :])
                    ins.then_inc(turned, 1)

            @block.vector
            def _(dve):
                for n in range(M // 4):
                    dve.wait_ge(turned, n + 1)
                    nc.vector.tensor_copy(score[:, n * 512:(n + 1) * 512], psum[n % 2][0:Q, :]).then_inc(took, 1)

        with nc.Block() as block:
            @block.scalar
            def _(act):
                act.wait_ge(act_in, 1)
                nc.scalar.activation(own[:, :], peak[:, :], ACT.Exp, scale=-1.0).then_inc(act_out, 1)
                act.wait_ge(act_in, 2)
                nc.scalar.activation(score[:, :], score[:, :], ACT.Exp).then_inc(act_out, 1)
                beta = k.beta[:, :, :].rearrange("p (c j) h -> p j c h", c=CHUNKS)
                for n in range(M // 4):
                    act.wait_ge(out_mul, n + 1)
                    p = psum[n % 2][:, 0:4 * CHUNKS * H].rearrange("p (j c h) -> p j c h", j=4, h=H)
                    for j in range(4):
                        ins = nc.scalar.activation(beta[:, 4 * n + j, :, :], p[:, j, :, :], ACT.Copy)
                    ins.then_inc(out_took, 1)

            @block.vector
            def _(dve):
                v, link = nc.vector, chain.on(dve)
                link(v.tensor_scalar(last[:, :], k.next84[:, :], -1.0, 1.0, ALU.mult, ALU.add))
                sc.scan(dve, link, work, score[:, :], k.same84[:, :], k.prod_f[:, :], k.flow_f, ALU.max, True)
                link(v.scalar_tensor_tensor(work[:, :], work[:, :], 0.0, last[:, :], ALU.max, ALU.mult))
                sc.scan(dve, link, peak, work[:, :], k.next84[:, :], k.prod_b[:, :], k.flow_b, ALU.add, False)
                v.sem_inc(act_in, 1)
                v.tensor_tensor(score[:, :], score[:, :], peak[:, :], ALU.subtract).then_inc(act_in, 1)
                dve.wait_ge(act_out, 2)
                sc.scan(dve, link, work, score[:, :], k.same84[:, :], k.prod_f[:, :], k.flow_f, ALU.add, True)
                link(v.tensor_tensor(work[:, :], work[:, :], own[:, :], ALU.add))
                link(v.tensor_tensor(work[:, :], work[:, :], last[:, :], ALU.mult))
                sc.scan(dve, link, peak, work[:, :], k.next84[:, :], k.prod_b[:, :], k.flow_b, ALU.add, False)
                for n in range(M // 4):
                    at = slice(n * W, (n + 1) * W)
                    link(v.reciprocal(peak[:, at], peak[:, at]))
                    v.tensor_tensor(score[:, at], score[:, at], peak[:, at], ALU.mult).then_inc(factors, 1)

            @block.tensor
            def _(pe):
                for _ in range(4):
                    sc.pe_scan(pe)
                for n in range(M // 4):
                    pe.wait_ge(factors, n + 1)
                    need(pe, out_took, n - 1)
                    for j in range(4):
                        t = 4 * n + j
                        ins = nc.tensor.matmul(psum[n % 2][:, j * CHUNKS * H:(j + 1) * CHUNKS * H],
                                               score[:, t * T:(t + 1) * T], k.head_w[:, :], start=True, stop=True)
                    ins.then_inc(out_mul, 1)


def across(ap):
    return ap.rearrange("p (t a) -> p t a", a=1).to_broadcast([ap.shape[0], ap.shape[1], H])


def gat_combine(kit, k):
    nc = kit.nc
    LAG = 5
    name = "gb"
    with ExitStack() as ctx:
        def pair(n):
            return [kit.sb(f"{name}_{n}{b}", [T, W], F32, ctx) for b in range(2)]

        Z, V, XD, XDT, AG, OUT, OUTN = (pair(n) for n in "Z V XD XDT AG OUT OUTN".split())
        B = [ctx.enter_context(nc.psum_tensor(f"{name}_bank{i}", [T, 512], F32)) for i in range(4)]
        norm = Spread(kit, ctx, f"{name}_sp")
        weighted, v_turned, d_turned, summed, xdt, mul, x2, scaled = (kit.sem(f"{name}_{n}") for n in (
            "weighted", "v_turned", "d_turned", "summed", "xdt", "mul", "x2", "scaled"))
        z_in, x_in, stored, stored_n = ([kit.sem(f"{name}_{n}{b}") for b in range(2)] for n in (
            "z_in", "x_in", "stored", "stored_n"))

        with nc.Block() as block:
            @block.gpsimd
            def _(pool):
                def scale_out(g, h, b):
                    waits = [(stored_n[b], h * 16)] if not (isinstance(h, int) and h <= 0) else []
                    kit.hold("pool", pool, *waits, (x2, g + 1))
                    nc.gpsimd.tensor_tensor(tiles(OUTN[b]), tiles(OUT[b]), k.norm[:, bass.ds(g * G, G)].rearrange(
                        "p (j a) -> p j a", a=1).to_broadcast([T, G, D]), ALU.mult).then_inc(scaled, 1)

                steps(pool, k.NG, LAG, lambda at: rounds(at, [(4, scale_out)]))

            @block.sync
            def _(sp):
                def load(g, h, b):
                    need(sp, weighted, g - 1)
                    sp.dma_start(tiles(Z[b]), edge_rows(k.messages, g, 0)).then_inc(z_in[b], 16)
                    need(sp, d_turned, g - 1)
                    sp.dma_start(tiles(XD[b]), edge_rows(k.tab[1], g, k.N)).then_inc(x_in[b], 16)

                def store(g, h, b):
                    sp.wait_ge(x2, g + 1)
                    sp.dma_start(edge_rows(k.x_own, g, 0), tiles(OUT[b])).then_inc(stored[b], 16)
                    sp.wait_ge(scaled, g + 1)
                    sp.dma_start(edge_rows(k.tab[2], g, k.N), tiles(OUTN[b])).then_inc(stored_n[b], 16)

                steps(sp, k.NG, LAG, lambda at: rounds(at, [(0, load), (LAG, store)]))
                for b in range(2):
                    sp.wait_ge(stored[b], 16 * ((k.NG - b + 1) // 2))
                    sp.wait_ge(stored_n[b], 16 * ((k.NG - b + 1) // 2))

            @block.tensor
            def _(pe):
                def turn_d(g, h, b):
                    pe.wait_ge(x_in[b], (h + 1) * 16)
                    need(pe, xdt, g)
                    turn(nc, k, B[1], XD[b], d_turned)

                def turn_v(g, h, b):
                    pe.wait_ge(weighted, g + 1)
                    need(pe, summed, g)
                    turn(nc, k, B[0], V[b], v_turned)

                def product(g, h, b):
                    pe.wait_ge(xdt, g + 1)
                    pe.wait_ge(summed, g + 1)
                    need(pe, x2, g - 1)
                    begin_with_row(nc, k, B[2 + b], k.bbar_parts)
                    for j in range(G):
                        at = slice(j * T, (j + 1) * T)
                        nc.tensor.matmul(B[2 + b][:, at], XDT[b][:, at], k.own_mix[:, :], start=False, stop=False)
                        last = nc.tensor.matmul(B[2 + b][:, at], AG[b][:, at], k.centre[:, :], start=False, stop=j == G - 1)
                    last.then_inc(mul, 1)

                steps(pe, k.NG, LAG, lambda at: rounds(at, [(3, product), (1, turn_d), (1, turn_v)]))

            @block.scalar
            def _(act):
                def copy_own(g, h, b):
                    need(act, mul, g - 1)
                    act.wait_ge(d_turned, g + 1)
                    nc.scalar.activation(XDT[b][:, :], B[1][:, :], ACT.Copy).then_inc(xdt, 1)

                def spread(g, h, b):
                    act.wait_ge(mul, g + 1)
                    norm.on_act(act, k.eps[:, 0:1], lambda j: B[2 + b][:, j * D:(j + 1) * D], g, b)

                steps(act, k.NG, LAG, lambda at: rounds(at, [
                    (1, copy_own), (3, spread)]))

            @block.vector
            def _(dve):
                v = nc.vector
                total = segment_sum(kit, k, dve, AG, [B[0]] * 2, v_turned, summed, lambda g: [(mul, g - 1)])

                def weigh(g, h, b):
                    need(dve, v_turned, g - 1)
                    kit.hold("dve", dve, (z_in[b], (h + 1) * 16))
                    beta = k.beta[:, bass.ds(g * G, G), :].rearrange("p t h -> p (t h)")
                    v.tensor_tensor(V[b][:, :].rearrange("p (q c) -> p q c", c=HD),
                                    Z[b][:, :].rearrange("p (q c) -> p q c", c=HD),
                                    beta.rearrange("p (q a) -> p q a", a=1).to_broadcast([T, G * H, HD]),
                                    ALU.mult).then_inc(weighted, 1)

                def scale(g, h, b):
                    if not (isinstance(h, int) and h <= 0):
                        dve.wait_ge(stored[b], h * 16)
                    need(dve, scaled, g - 1)
                    norm.invert(dve, g, b)
                    v.tensor_tensor(tiles(OUT[b]), tiles(B[2 + b]), wide(norm.rstd[b]), ALU.mult).then_inc(x2, 1)

                steps(dve, k.NG, LAG, lambda at: rounds(at, [(1, weigh), (4, scale), (1, total)]))


def gcn(kit, k):
    nc = kit.nc
    LAG = 6
    name = "gc"
    with ExitStack() as ctx:
        def pair(n):
            return [kit.sb(f"{name}_{n}{b}", [T, W], F32, ctx) for b in range(2)]

        XS, AG, XR, BASE, MIX, OUT = (pair(n) for n in "XS AG XR BASE MIX OUT".split())
        B = [ctx.enter_context(nc.psum_tensor(f"{name}_bank{i}", [T, 512], F32)) for i in range(2)]
        norm = Spread(kit, ctx, f"{name}_sp")
        src_g = Gather(kit, ctx, f"{name}_src", k.srcp_i, k.tab[2], XS)
        turned, summed, mul, base, mixed, x3 = (kit.sem(f"{name}_{n}") for n in ("turned", "summed", "mul", "base", "mixed", "x3"))
        x_in, stored = ([kit.sem(f"{name}_{n}{b}") for b in range(2)] for n in ("x_in", "stored"))

        with nc.Block() as block:
            @block.gpsimd
            def _(pool):
                steps(pool, k.NG, LAG, lambda at: rounds(at, [(0, src_g.stage_ahead(pool, lambda g, h, b: [(turned, g - 1)], k.NG))]))

            @block.sync
            def _(sp):
                def load(g, h, b):
                    need(sp, base, g - 1)
                    sp.dma_start(tiles(XR[b]), edge_rows(k.x_own, g, 0)).then_inc(x_in[b], 16)

                def store(g, h, b):
                    sp.wait_ge(x3, g + 1)
                    sp.dma_start(edge_rows(k.tab[3], g, k.N), tiles(OUT[b])).then_inc(stored[b], 16)

                steps(sp, k.NG, LAG, lambda at: rounds(at, [(3, load), (LAG, store)]))
                for b in range(2):
                    sp.wait_ge(stored[b], 16 * ((k.NG - b + 1) // 2))

            @block.tensor
            def _(pe):
                def turn_s(g, h, b):
                    src_g.wait(pe, h, b)
                    need(pe, summed, g)
                    turn(nc, k, B[0], XS[b], turned)

                def product(g, h, b):
                    pe.wait_ge(summed, g + 1)
                    need(pe, mixed, g)
                    multiply_rows(nc, B[1], AG[b], k.w2[:, :], mul)

                steps(pe, k.NG, LAG, lambda at: rounds(at, [(2, turn_s), (3, product)]))

            @block.scalar
            def _(act):
                def spread(g, h, b):
                    act.wait_ge(mixed, g + 1)
                    norm.on_act(act, k.eps[:, 0:1], lambda j: MIX[b][:, j * D:(j + 1) * D], g, b)

                steps(act, k.NG, LAG, lambda at: rounds(at, [(5, spread)]))

            @block.vector
            def _(dve):
                v = nc.vector
                total = segment_sum(kit, k, dve, AG, [B[0]] * 2, turned, summed, lambda g: [(mul, g - 1)])

                def add_bias(g, h, b):
                    need(dve, mixed, g - 1)
                    dve.wait_ge(x_in[b], (h + 1) * 16)
                    v.tensor_tensor(tiles(BASE[b]), tiles(XR[b]), over(k.b2_row), ALU.add).then_inc(base, 1)

                def mix(g, h, b):
                    need(dve, x3, g - 1)
                    kit.hold("dve", dve, (base, g + 1), (mul, g + 1))
                    for j in range(G):
                        last = v.scalar_tensor_tensor(MIX[b][:, j * T:(j + 1) * T], B[1][:, j * T:(j + 1) * T],
                                                      k.norm[:, bass.ds(g * G + j, 1)], BASE[b][:, j * T:(j + 1) * T],
                                                      ALU.mult, ALU.add)
                    last.then_inc(mixed, 1)

                def scale(g, h, b):
                    if not (isinstance(h, int) and h <= 0):
                        dve.wait_ge(stored[b], h * 16)
                    norm.invert(dve, g, b)
                    v.tensor_tensor(tiles(OUT[b]), tiles(MIX[b]), wide(norm.rstd[b]), ALU.mult).then_inc(x3, 1)

                steps(dve, k.NG, LAG, lambda at: rounds(at, [(4, add_bias), (4, mix), (2, total), (5, scale)]))


def gin(kit, k, edge_attr, out, E):
    nc = kit.nc
    LAG = 5
    name = "gi"
    A = edge_attr.shape[1]
    with ExitStack() as ctx:
        def pair(n, shape=(T, W), dt=F32):
            return [kit.sb(f"{name}_{n}{b}", list(shape), dt, ctx) for b in range(2)]

        XS, MS, AG, XD, XB, XDT, HT, MA, MB, Y, OUT = (pair(n) for n in "XS MS AG XD XB XDT HT MA MB Y OUT".split())
        ea_last = kit.sb(f"{name}_ea_last", [T, G, A], F32, ctx)
        EA, EAT, now = pair("EA", (T, G, A)), pair("EAT", (A, W)), pair("now", (T, G), I32)
        B = [ctx.enter_context(nc.psum_tensor(f"{name}_bank{i}", [T, 512], F32)) for i in range(8)]
        norm = Spread(kit, ctx, f"{name}_sp")
        src_g = Gather(kit, ctx, f"{name}_src", k.srcp_i, k.tab[3], XS)
        (e_clear, e_turned, eat, m_sum, ms, summed, d_turned, xdt, ht, xb, ma_mul, mb_mul, ma, mb, out_mul, y, x4) = (kit.sem(f"{name}_{n}") for n in (
             "e_clear e_turned eat m_sum ms summed d_turned xdt ht xb ma_mul mb_mul ma mb out_mul y x4"
         ).split())
        e_last = kit.sem(f"{name}_e_last")
        put = [kit.sem(f"{name}_put{b}", True) for b in range(2)]
        e_in, x_in, now_in = ([kit.sem(f"{name}_{n}{b}") for b in range(2)] for n in ("e_in", "x_in", "now_in"))
        rest = E - (k.NG - 1) * W

        with nc.Block() as block:
            @block.gpsimd
            def _(pool):
                def put_rows(g, h, b):
                    kit.hold("pool", pool, (now_in[b], (h + 1) * 16), (x4, g + 1))
                    for j in range(G):
                        pool.indirect_dma_start(out, bass.IndirectOffsetOnAxis(ap=now[b][:, j:j + 1], axis=0),
                                                OUT[b][:, j * T:(j + 1) * T], None, bounds_check=k.N - 1,
                                                oob_is_err=False).then_inc(put[b], 16)

                steps(pool, k.NG, LAG, lambda at: rounds(
                    at, [(1, src_g.fed_stage(pool, lambda g, h, b: [(m_sum, g - 1)])), (LAG, put_rows)]))
                for b in range(2):
                    pool.wait_ge(put[b], 16 * G * ((k.NG - b + 1) // 2))

            @block.sync
            def _(sp):
                def load_e(g, h, b):
                    need(sp, e_turned, g - 1)
                    if isinstance(g, int) and g == k.NG - 1:
                        sp.wait_ge(e_clear, 1)
                        for j in range(-(-rest // T)):
                            n = min(T, rest - j * T)
                            sp.dma_start(ea_last[0:n, j, :], edge_attr[g * W + j * T:g * W + j * T + n, :]
                                         ).then_inc(e_last, 16)
                    else:
                        sp.dma_start(EA[b][:, :, :], edge_attr[bass.ds(g * W, W), :].rearrange(
                            "(j p) a -> p j a", p=T)).then_inc(e_in[b], 16)

                def load_x(g, h, b):
                    need(sp, d_turned, g - 1)
                    need(sp, xb, g - 1)
                    sp.dma_start(tiles(XD[b]), edge_rows(k.tab[3], g, k.N)).then_inc(x_in[b], 16)

                def load_places(g, h, b):
                    waits = [(put[b], h * 16 * G)] if not (isinstance(h, int) and h <= 0) else []
                    kit.hold("sp", sp, *waits)
                    sp.dma_start(now[b][:, :], k.last_i[:, bass.ds(g * G, G)]).then_inc(now_in[b], 16)

                steps(sp, k.NG, LAG, lambda at: rounds(at, [
                    (0, load_e), (0, src_g.feed(sp)), (2, load_x), (4, load_places)]))

            @block.tensor
            def _(pe):
                def turn_e(g, h, b):
                    last_one = isinstance(g, int) and g == k.NG - 1
                    if last_one:
                        pe.wait_ge(e_last, 16 * -(-rest // T))
                    else:
                        pe.wait_ge(e_in[b], (h + 1) * 16)
                    rows = ea_last if last_one else EA[b]
                    need(pe, eat, g)
                    for j in range(G):
                        last = nc.tensor.transpose(B[0][0:A, j * T:(j + 1) * T], rows[:, j, :], k.ident[:, :])
                    last.then_inc(e_turned, 1)

                def message(g, h, b):
                    src_g.wait(pe, h, b)
                    pe.wait_ge(eat, g + 1)
                    need(pe, ms, g)
                    for j in range(G):
                        at = slice(j * T, (j + 1) * T)
                        nc.tensor.matmul(B[1][:, at], k.we[:, :], EAT[b][:, at], start=True, stop=False)
                        last = nc.tensor.matmul(B[1][:, at], XS[b][:, at], k.ident[:, :], start=False, stop=True)
                    last.then_inc(m_sum, 1)

                def turn_x(g, h, b):
                    pe.wait_ge(x_in[b], (h + 1) * 16)
                    need(pe, xdt, g)
                    turn(nc, k, B[2], XD[b], d_turned)

                def hidden(g, h, b):
                    pe.wait_ge(ht, g + 1)
                    need(pe, ma, g)
                    nc.tensor.matmul(B[3][:, :], k.wm1[:, 0:D], HT[b][:, :], start=True, stop=True).then_inc(ma_mul, 1)
                    need(pe, mb, g)
                    nc.tensor.matmul(B[4][:, :], k.wm1[:, D:2 * D], HT[b][:, :], start=True, stop=True).then_inc(mb_mul, 1)

                def project(g, h, b):
                    pe.wait_ge(ma, g + 1)
                    pe.wait_ge(mb, g + 1)
                    need(pe, y, g)
                    for j in range(G):
                        at = slice(j * T, (j + 1) * T)
                        nc.tensor.matmul(B[5][:, at], MA[b][:, at], k.wm2[:, 0, :], start=True, stop=False)
                        last = nc.tensor.matmul(B[5][:, at], MB[b][:, at], k.wm2[:, 1, :], start=False, stop=True)
                    last.then_inc(out_mul, 1)

                steps(pe, k.NG, LAG, lambda at: rounds(at, [
                    (3, turn_x), (4, hidden), (3, message), (4, project), (1, turn_e)]))

            @block.scalar
            def _(act):
                def turned_e(g, h, b):
                    need(act, m_sum, g - 1)
                    act.wait_ge(e_turned, g + 1)
                    nc.scalar.activation(EAT[b][:, :], B[0][0:A, :], ACT.Copy).then_inc(eat, 1)

                def relu_message(g, h, b):
                    need(act, summed, g - 1)
                    act.wait_ge(m_sum, g + 1)
                    nc.scalar.activation(MS[b][:, :], B[1][:, :], ACT.Relu, bias=k.be_col[:, 0:1]).then_inc(ms, 1)

                def copy_x(g, h, b):
                    need(act, ht, g - 1)
                    act.wait_ge(d_turned, g + 1)
                    nc.scalar.activation(XDT[b][:, :], B[2][:, :], ACT.Copy).then_inc(xdt, 1)

                def relu_hidden(n, m, mul, done):
                    def stage(g, h, b):
                        need(act, out_mul, g - 1)
                        act.wait_ge(mul, g + 1)
                        nc.scalar.activation(m[b][:, :], B[3 + n][:, :], ACT.Relu, bias=k.bn1_b[:, n:n + 1],
                                             scale=k.bn1_s[:, n:n + 1]).then_inc(done, 1)
                    return stage

                def spread(g, h, b):
                    act.wait_ge(y, g + 1)
                    norm.on_act(act, k.eps[:, 0:1], lambda j: Y[b][:, j * D:(j + 1) * D], g, b)

                steps(act, k.NG, LAG, lambda at: rounds(at, [
                    (4, relu_hidden(0, MA, ma_mul, ma)), (3, copy_x), (2, turned_e), (4, relu_hidden(1, MB, mb_mul, mb)),
                    (3, relu_message), (4, spread)]))

            @block.vector
            def _(dve):
                v = nc.vector
                total = segment_sum(kit, k, dve, AG, MS, ms, summed, lambda g: [(ht, g - 1)])
                v.memset(ea_last[:, :, :], 0.0).then_inc(e_clear, 1)

                def own(g, h, b):
                    need(dve, mb_mul, g - 1)
                    dve.wait_ge(xdt, g + 1)
                    dve.wait_ge(summed, g + 1)
                    v.scalar_tensor_tensor(HT[b][:, :], XDT[b][:, :], k.eps1[:, 0:1], AG[b][:, :],
                                           ALU.mult, ALU.add).then_inc(ht, 1)

                def bias_x(g, h, b):
                    dve.wait_ge(x_in[b], (h + 1) * 16)
                    need(dve, y, g - 1)
                    v.tensor_tensor(tiles(XB[b]), tiles(XD[b]), over(k.bn2_row), ALU.add).then_inc(xb, 1)

                def add_x(g, h, b):
                    dve.wait_ge(xb, g + 1)
                    need(dve, x4, g - 1)
                    dve.wait_ge(out_mul, g + 1)
                    v.tensor_tensor(Y[b][:, :], B[5][:, :], XB[b][:, :], ALU.add).then_inc(y, 1)

                def scale(g, h, b):
                    if not (isinstance(h, int) and h <= 0):
                        dve.wait_ge(put[b], h * 16 * G)
                    norm.invert(dve, g, b)
                    v.tensor_tensor(tiles(OUT[b]), tiles(Y[b]), wide(norm.rstd[b]), ALU.mult).then_inc(x4, 1)

                steps(dve, k.NG, LAG, lambda at: rounds(
                    at, [(3, bias_x), (3, total), (3, own), (4, add_x), (4, scale)]))


class Tensors:
    pass


def gnn(nc, x, src, dst, edge_attr, edge_type, ins, out, place, tabs, x_own, messages):
    N, E = x.shape[0], src.shape[0]
    M = 4 * -(-E // (CHUNKS * G * T))
    with ExitStack() as ctx:
        kit = Kit(nc, ctx)
        k = Tensors()
        k.N, k.E, k.NT = N, E, CHUNKS * M
        k.NG = k.NT // G
        k.place, k.tab, k.x_own, k.messages = place, tabs, x_own, messages
        CH = M * T
        sb = kit.sb
        k.eps, k.one, k.eps1 = sb("eps", [T, 1]), sb("one", [T, 1]), sb("eps1", [T, 1])
        k.ident = sb("ident", [T, T])
        k.chunk_of = sb("chunk_of", [CHUNKS, Q], BF16)
        k.one_chunk = sb("one_chunk", [CHUNKS, CHUNKS, T], BF16)
        k.head_sel = sb("head_sel", [Q, R, CHUNKS, H])
        k.head_w = sb("head_w", [Q, CHUNKS * H])
        k.rel = sb("rel", [T, R])
        k.wl1, k.wr1, k.wl2, k.wr2, k.w2, k.w_bar = (sb(n, [D, D]) for n in "wl1 wr1 wl2 wr2 w2 w_bar".split())
        k.centre, k.own_mix, k.pair_mix = sb("centre", [D, D]), sb("own_mix", [D, D]), sb("pair_mix", [D, 2 * D])
        k.w_cat, k.wm1, k.wm2 = sb("w_cat", [D, R * D + RH]), sb("wm1", [D, 2 * D]), sb("wm2", [D, 2, D])
        k.we = sb("we", [16, D])
        k.bl2_parts, k.bbar_parts = (sb(n, [T, G, D], BF16) for n in ("bl2_parts", "bbar_parts"))
        k.ones = sb("ones", [T, T], BF16)
        k.self_w = sb("self_w", [D, RH])
        k.bl1_row, k.bl2_row, k.b2_row, k.bbar_row, k.bn2_row = (
            sb(n, [T, D]) for n in "bl1_row bl2_row b2_row bbar_row bn2_row".split())
        k.bl1_col, k.bl2_col, k.be_col = (sb(n, [D, 1]) for n in "bl1_col bl2_col be_col".split())
        k.bn1_s, k.bn1_b, k.bn1_s_own = (sb(n, [D, 2]) for n in "bn1_s bn1_b bn1_s_own".split())
        k.src_i, k.dst_i, k.last_i, k.srcp_i, k.edge_row = (
            sb(n, [T, k.NT], I32) for n in "src_i dst_i last_i srcp_i edge_row".split())
        k.type_f, k.last_f, k.deg, k.rdeg, k.norm = (sb(n, [T, k.NT]) for n in "type_f last_f deg rdeg norm".split())
        k.is_type = sb("is_type", [T, k.NT, R])
        k.same = sb("same", [T, k.NT * T + 1], BF16)
        k.same84, k.next84, k.prod_f, k.prod_b = (sb(n, [Q, CH], BF16) for n in "same84 next84 prod_f prod_b".split())
        k.flow_f, k.flow_b = (sb(n, [1, RH, CHUNKS]) for n in "flow_f flow_b".split())
        kit.place_clear = kit.sem("place_clear", True)

        with ExitStack() as early:
            raw, val = sb("raw", [T, CH + 2], I32, early), sb("val", [T, CH + 2], F32, early)
            equal = sb("equal", [T, CH + 1], BF16, early)
            prepare(kit, k, ins, raw, index_loads(raw, src, dst, edge_type, E, CH),
                    lambda vec, link: compare_neighbours(k, raw, val, equal, link, vec))
            kit.end_phase()
            index_stage(kit, k, val, equal, N, M)
            kit.end_phase()
        first_pass(kit, k, x, out, x_own)
        kit.end_phase()
        sage(kit, k)
        kit.end_phase()
        with ExitStack() as gat:
            k.scores = sb("scores", [T, k.NT, 2 * RH], F32, gat)
            k.beta = sb("beta", [T, k.NT, H], F32, gat)
            gat_messages(kit, k)
            kit.end_phase()
            attention(kit, k, M)
            kit.end_phase()
            gat_combine(kit, k)
            kit.end_phase()
        gcn(kit, k)
        kit.end_phase()
        gin(kit, k, edge_attr, out, E)


_DATA = ("x", "src", "dst", "edge_attr_16", "edge_type_3")


def kernel(**inputs):
    import numpy as np
    import concourse.bacc as bacc
    from concourse.bass_utils import run_bass_kernel_spmd as run

    nc = bacc.Bacc("TRN2", target_bir_lowering=False, num_devices=1)
    arrays = {name: np.ascontiguousarray(a) for name, a in inputs.items()}
    args = {name: nc.dram_tensor(name, a.shape, mybir.dt.from_np(a.dtype), kind="ExternalInput").ap()
            for name, a in arrays.items()}
    N, E = arrays["x"].shape[0], arrays["src"].shape[0]
    EP = CHUNKS * G * T * -(-E // (CHUNKS * G * T))
    out = nc.dram_tensor("out", (N, D), F32, kind="ExternalOutput").ap()
    place = nc.dram_tensor("place", (N, 1), I32).ap()
    tabs = [nc.dram_tensor(f"tab{i}", (N + EP, D), F32).ap() for i in range(4)]
    x_own = nc.dram_tensor("x_own", (EP, D), F32).ap()
    messages = nc.dram_tensor("messages", (EP, D), F32).ap()
    gnn(nc, *(args[n] for n in _DATA), {n: a for n, a in args.items() if n not in _DATA}, out, place, tabs,
        x_own, messages)
    return run(nc, [arrays], core_ids=[0]).results[0]["out"]
```
